# Optimizing a Trainium2 kernel written in Bass

```python
import numpy as np
import jax
import jax.numpy as jnp

def _softmax(x, axis=-1):
    return jax.nn.softmax(x, axis=axis)

def _gelu(x):
    return jax.nn.gelu(x, approximate=True)

def _silu(x):
    return jax.nn.silu(x)

def _sigmoid(x):
    return jax.nn.sigmoid(x)

def _layernorm(x, axis=-1, eps=1e-05):
    m = jnp.mean(x, axis=axis, keepdims=True)
    v = jnp.var(x, axis=axis, keepdims=True)
    return (x - m) / jnp.sqrt(v + eps)

def _scatter_add(tgt, idx, src, axis=0):
    return tgt.at[idx].add(src)

def _segment_sum(src, seg, n):
    return jax.ops.segment_sum(src, seg, n)
kernel_name = 'mk_seq_preln_d2_jaxref_r4_6d495f'

def setup_inputs(seed: int=0):
    np.random.seed(seed)
    _w = jnp.asarray

    def _L0_attn_setup():
        import jax, jax.numpy as jnp
        import numpy as np
        B, S, D, H = (2, 512, 256, 16)
        HD = D // H
        key = jax.random.key(seed)
        ks = jax.random.split(key, 16)
        sc = 0.02
        return {'hidden_states': jax.random.normal(ks[0], (B, S, D), jnp.float32), 'Wq': jax.random.normal(ks[1], (D, D), jnp.float32) * sc, 'bq': jnp.zeros((D,), jnp.float32), 'Wk': jax.random.normal(ks[2], (D, D), jnp.float32) * sc, 'bk': jnp.zeros((D,), jnp.float32), 'Wv': jax.random.normal(ks[3], (D, D), jnp.float32) * sc, 'bv': jnp.zeros((D,), jnp.float32), 'Wo': jax.random.normal(ks[4], (D, D), jnp.float32) * sc, 'bo': jnp.zeros((D,), jnp.float32), 'rel_W': jax.random.normal(ks[5], (3, 2 * D), jnp.float32) * sc, 'rel_b': jnp.zeros((3,), jnp.float32), 'logical_bias': jax.random.normal(ks[6], (H, 3), jnp.float32) * sc, 'gate_W': jax.random.normal(ks[7], (H, D), jnp.float32) * sc, 'gate_b': jnp.zeros((H,), jnp.float32)}
    _L0_attn_in = _L0_attn_setup()

    def _L0_ffn_setup():
        import jax, jax.numpy as jnp
        import numpy as np
        FP8_MAX = 448.0
        key = jax.random.key(seed)
        k_x, k_w, k_b = jax.random.split(key, 3)
        B, S, IN, OUT = (4, 2048, 256, 256)
        x = jax.random.normal(k_x, (B, S, IN), dtype=jnp.float32)
        w_fp32 = jax.random.normal(k_w, (OUT, IN), dtype=jnp.float32)
        weight_fp8 = w_fp32.astype(jnp.float8_e4m3fn).astype(jnp.float32)
        bias = jax.random.normal(k_b, (OUT,), dtype=jnp.float32)
        input_scale = jnp.ones((1,), dtype=jnp.float32)
        weight_scale = jnp.ones((1,), dtype=jnp.float32)
        return {'x': x, 'weight_fp8': weight_fp8, 'bias': bias, 'input_scale': input_scale, 'weight_scale': weight_scale}
    _L0_ffn_in = _L0_ffn_setup()

    def _L1_attn_setup():
        import jax, jax.numpy as jnp
        import numpy as np
        D_MODEL = 256
        D_STATE = 16
        D_CONV = 4
        EXPAND = 2
        D_INNER = EXPAND * D_MODEL
        DT_RANK = (D_MODEL + 15) // 16
        D_FFN = 1024
        EPS = 1e-05

        def layer_norm(x, w):
            mu = jnp.mean(x, axis=-1, keepdims=True)
            var = jnp.mean(jnp.square(x - mu), axis=-1, keepdims=True)
            return (x - mu) * jax.lax.rsqrt(var + EPS) * w

        def silu(x):
            return x * jax.nn.sigmoid(x)

        def mamba_mixer(x, in_proj_w, conv_w, conv_b, x_proj_w, dt_proj_w, dt_proj_b, A_log, Dp, out_proj_w):
            B, L, _ = x.shape
            xz = jnp.einsum('bld,ed->ble', x, in_proj_w)
            xr, z = jnp.split(xz, 2, axis=-1)
            xr_t = jnp.transpose(xr, (0, 2, 1))
            xc = jax.lax.conv_general_dilated(xr_t, conv_w, window_strides=(1,), padding=[(D_CONV - 1, 0)], feature_group_count=D_INNER, dimension_numbers=('NCH', 'OIH', 'NCH'))
            xc = xc + conv_b[None, :, None]
            xc = silu(jnp.transpose(xc, (0, 2, 1)))
            x_dbl = jnp.einsum('bld,ed->ble', xc, x_proj_w)
            dt, Bc, Cc = jnp.split(x_dbl, [DT_RANK, DT_RANK + D_STATE], axis=-1)
            dt = jax.nn.softplus(jnp.einsum('blr,dr->bld', dt, dt_proj_w) + dt_proj_b)
            A = -jnp.exp(A_log)
            dA = jnp.exp(dt[..., None] * A)
            dBx = dt[..., None] * Bc[:, :, None, :] * xc[..., None]

            def step(h, inp):
                dA_t, dBx_t, C_t = inp
                h = dA_t * h + dBx_t
                y = jnp.einsum('bdn,bn->bd', h, C_t)
                return (h, y)
            h0 = jnp.zeros((B, D_INNER, D_STATE), dtype=x.dtype)
            _, ys = jax.lax.scan(step, h0, (jnp.swapaxes(dA, 0, 1), jnp.swapaxes(dBx, 0, 1), jnp.swapaxes(Cc, 0, 1)))
            y = jnp.swapaxes(ys, 0, 1) + Dp * xc
            y = y * silu(z)
            return jnp.einsum('bld,ed->ble', y, out_proj_w)

        def mlp(x, fc_w, proj_w):
            return jnp.einsum('blh,eh->ble', silu(jnp.einsum('bld,hd->blh', x, fc_w)), proj_w)
        key = jax.random.key(seed)
        ks = jax.random.split(key, 12)
        s = lambda k, shape, scale: jax.random.normal(k, shape, dtype=jnp.float32) * scale
        x = s(ks[0], (2, 256, D_MODEL), 1.0)
        inp = {'x': x, 'ln1_w': jnp.ones((D_MODEL,), jnp.float32), 'in_proj_w': s(ks[1], (2 * D_INNER, D_MODEL), 0.02), 'conv_w': s(ks[2], (D_INNER, 1, D_CONV), 0.2), 'conv_b': s(ks[3], (D_INNER,), 0.02), 'x_proj_w': s(ks[4], (DT_RANK + 2 * D_STATE, D_INNER), 0.02), 'dt_proj_w': s(ks[5], (D_INNER, DT_RANK), 0.1), 'dt_proj_b': s(ks[6], (D_INNER,), 0.5), 'A_log': jnp.log(jnp.broadcast_to(jnp.arange(1, D_STATE + 1, dtype=jnp.float32), (D_INNER, D_STATE))), 'Dp': jnp.ones((D_INNER,), jnp.float32), 'out_proj_w': s(ks[7], (D_MODEL, D_INNER), 0.02), 'ln2_w': jnp.ones((D_MODEL,), jnp.float32), 'fc_w': s(ks[8], (D_FFN, D_MODEL), 0.02), 'proj_w': s(ks[9], (D_MODEL, D_FFN), 0.02)}
        return inp
    _L1_attn_in = _L1_attn_setup()

    def _L1_ffn_setup():
        import jax, jax.numpy as jnp
        import numpy as np
        DIM = 256
        HIDDEN = 768
        SCALE = 1.0 / 127.0

        def _dequant(w_int, dtype):
            return w_int.astype(dtype) * jnp.asarray(SCALE, dtype)
        key = jax.random.key(seed)
        k_x, k_g, k_u, k_d = jax.random.split(key, 4)
        x = jax.random.normal(k_x, (4, 512, DIM), dtype=jnp.float32)
        w_gate = jax.random.randint(k_g, (HIDDEN, DIM), -127, 128, dtype=jnp.int32)
        w_up = jax.random.randint(k_u, (HIDDEN, DIM), -127, 128, dtype=jnp.int32)
        w_down = jax.random.randint(k_d, (DIM, HIDDEN), -127, 128, dtype=jnp.int32)
        return {'x': x, 'w_gate': w_gate, 'w_up': w_up, 'w_down': w_down}
    _L1_ffn_in = _L1_ffn_setup()
    _d = {'L0_attn_hidden_states': _L0_attn_in['hidden_states'], 'L0_attn_Wq': _L0_attn_in['Wq'], 'L0_attn_bq': _L0_attn_in['bq'], 'L0_attn_Wk': _L0_attn_in['Wk'], 'L0_attn_bk': _L0_attn_in['bk'], 'L0_attn_Wv': _L0_attn_in['Wv'], 'L0_attn_bv': _L0_attn_in['bv'], 'L0_attn_Wo': _L0_attn_in['Wo'], 'L0_attn_bo': _L0_attn_in['bo'], 'L0_attn_rel_W': _L0_attn_in['rel_W'], 'L0_attn_rel_b': _L0_attn_in['rel_b'], 'L0_attn_logical_bias': _L0_attn_in['logical_bias'], 'L0_attn_gate_W': _L0_attn_in['gate_W'], 'L0_attn_gate_b': _L0_attn_in['gate_b'], 'L0_ffn_weight_fp8': _L0_ffn_in['weight_fp8'], 'L0_ffn_bias': _L0_ffn_in['bias'], 'L0_ffn_input_scale': _L0_ffn_in['input_scale'], 'L0_ffn_weight_scale': _L0_ffn_in['weight_scale'], 'L1_attn_ln1_w': _L1_attn_in['ln1_w'], 'L1_attn_in_proj_w': _L1_attn_in['in_proj_w'], 'L1_attn_conv_w': _L1_attn_in['conv_w'], 'L1_attn_conv_b': _L1_attn_in['conv_b'], 'L1_attn_x_proj_w': _L1_attn_in['x_proj_w'], 'L1_attn_dt_proj_w': _L1_attn_in['dt_proj_w'], 'L1_attn_dt_proj_b': _L1_attn_in['dt_proj_b'], 'L1_attn_A_log': _L1_attn_in['A_log'], 'L1_attn_Dp': _L1_attn_in['Dp'], 'L1_attn_out_proj_w': _L1_attn_in['out_proj_w'], 'L1_attn_ln2_w': _L1_attn_in['ln2_w'], 'L1_attn_fc_w': _L1_attn_in['fc_w'], 'L1_attn_proj_w': _L1_attn_in['proj_w'], 'L1_ffn_w_gate': _L1_ffn_in['w_gate'], 'L1_ffn_w_up': _L1_ffn_in['w_up'], 'L1_ffn_w_down': _L1_ffn_in['w_down']}
    _x0 = _d['L0_attn_hidden_states']
    _d['L0_attn_hidden_states'] = jax.random.normal(jax.random.fold_in(jax.random.key(seed), 1), (8, 1024, 256), dtype=_x0.dtype)
    del _x0
    return _d

def reference(L0_attn_hidden_states, L0_attn_Wq, L0_attn_bq, L0_attn_Wk, L0_attn_bk, L0_attn_Wv, L0_attn_bv, L0_attn_Wo, L0_attn_bo, L0_attn_rel_W, L0_attn_rel_b, L0_attn_logical_bias, L0_attn_gate_W, L0_attn_gate_b, L0_ffn_weight_fp8, L0_ffn_bias, L0_ffn_input_scale, L0_ffn_weight_scale, L1_attn_ln1_w, L1_attn_in_proj_w, L1_attn_conv_w, L1_attn_conv_b, L1_attn_x_proj_w, L1_attn_dt_proj_w, L1_attn_dt_proj_b, L1_attn_A_log, L1_attn_Dp, L1_attn_out_proj_w, L1_attn_ln2_w, L1_attn_fc_w, L1_attn_proj_w, L1_ffn_w_gate, L1_ffn_w_up, L1_ffn_w_down):

    def _L0_attn_ref(hidden_states, Wq, bq, Wk, bk, Wv, bv, Wo, bo, rel_W, rel_b, logical_bias, gate_W, gate_b):
        import jax, jax.numpy as jnp
        import numpy as np
        B, S, D, H = (2, 512, 256, 16)
        HD = D // H
        x = hidden_states
        b, s, d = x.shape
        h = gate_W.shape[0]
        hd = d // h
        scale = hd ** 0.5
        q = (x @ Wq.T + bq).reshape(b, s, h, hd)
        k = (x @ Wk.T + bk).reshape(b, s, h, hd)
        v = (x @ Wv.T + bv).reshape(b, s, h, hd)
        attn_scores = jnp.einsum('bihd,bjhd->bhij', q, k) / scale
        li = x @ rel_W[:, :d].T
        lj = x @ rel_W[:, d:].T
        logits = li[:, :, None, :] + lj[:, None, :, :] + rel_b
        relation_probs = jax.nn.softmax(logits, axis=-1)
        bias = jnp.einsum('bijk,hk->bhij', relation_probs, logical_bias)
        gate = jax.nn.sigmoid(x @ gate_W.T + gate_b)
        gate = jnp.transpose(gate, (0, 2, 1))[..., None]
        attn_scores = attn_scores + gate * bias
        attn_weights = jax.nn.softmax(attn_scores, axis=-1)
        out = jnp.einsum('bhij,bjhd->bihd', attn_weights, v).reshape(b, s, d)
        return out @ Wo.T + bo

    def _L0_ffn_ref(x, weight_fp8, bias, input_scale, weight_scale):
        import jax, jax.numpy as jnp
        import numpy as np
        FP8_MAX = 448.0
        x_q = jnp.clip(x / input_scale, -FP8_MAX, FP8_MAX)
        x_dq = x_q.astype(jnp.float8_e4m3fn).astype(x.dtype) * input_scale
        w_dq = weight_fp8 * weight_scale
        out = jnp.einsum('bsi,oi->bso', x_dq, w_dq) + bias
        return out

    def _L1_attn_ref(x, ln1_w, in_proj_w, conv_w, conv_b, x_proj_w, dt_proj_w, dt_proj_b, A_log, Dp, out_proj_w, ln2_w, fc_w, proj_w):
        import jax, jax.numpy as jnp
        import numpy as np
        D_MODEL = 256
        D_STATE = 16
        D_CONV = 4
        EXPAND = 2
        D_INNER = EXPAND * D_MODEL
        DT_RANK = (D_MODEL + 15) // 16
        D_FFN = 1024
        EPS = 1e-05

        def layer_norm(x, w):
            mu = jnp.mean(x, axis=-1, keepdims=True)
            var = jnp.mean(jnp.square(x - mu), axis=-1, keepdims=True)
            return (x - mu) * jax.lax.rsqrt(var + EPS) * w

        def silu(x):
            return x * jax.nn.sigmoid(x)

        def mamba_mixer(x, in_proj_w, conv_w, conv_b, x_proj_w, dt_proj_w, dt_proj_b, A_log, Dp, out_proj_w):
            B, L, _ = x.shape
            xz = jnp.einsum('bld,ed->ble', x, in_proj_w)
            xr, z = jnp.split(xz, 2, axis=-1)
            xr_t = jnp.transpose(xr, (0, 2, 1))
            xc = jax.lax.conv_general_dilated(xr_t, conv_w, window_strides=(1,), padding=[(D_CONV - 1, 0)], feature_group_count=D_INNER, dimension_numbers=('NCH', 'OIH', 'NCH'))
            xc = xc + conv_b[None, :, None]
            xc = silu(jnp.transpose(xc, (0, 2, 1)))
            x_dbl = jnp.einsum('bld,ed->ble', xc, x_proj_w)
            dt, Bc, Cc = jnp.split(x_dbl, [DT_RANK, DT_RANK + D_STATE], axis=-1)
            dt = jax.nn.softplus(jnp.einsum('blr,dr->bld', dt, dt_proj_w) + dt_proj_b)
            A = -jnp.exp(A_log)
            dA = jnp.exp(dt[..., None] * A)
            dBx = dt[..., None] * Bc[:, :, None, :] * xc[..., None]

            def step(h, inp):
                dA_t, dBx_t, C_t = inp
                h = dA_t * h + dBx_t
                y = jnp.einsum('bdn,bn->bd', h, C_t)
                return (h, y)
            h0 = jnp.zeros((B, D_INNER, D_STATE), dtype=x.dtype)
            _, ys = jax.lax.scan(step, h0, (jnp.swapaxes(dA, 0, 1), jnp.swapaxes(dBx, 0, 1), jnp.swapaxes(Cc, 0, 1)))
            y = jnp.swapaxes(ys, 0, 1) + Dp * xc
            y = y * silu(z)
            return jnp.einsum('bld,ed->ble', y, out_proj_w)

        def mlp(x, fc_w, proj_w):
            return jnp.einsum('blh,eh->ble', silu(jnp.einsum('bld,hd->blh', x, fc_w)), proj_w)
        x = x + mamba_mixer(layer_norm(x, ln1_w), in_proj_w, conv_w, conv_b, x_proj_w, dt_proj_w, dt_proj_b, A_log, Dp, out_proj_w)
        x = x + mlp(layer_norm(x, ln2_w), fc_w, proj_w)
        return x

    def _L1_ffn_ref(x, w_gate, w_up, w_down):
        import jax, jax.numpy as jnp
        import numpy as np
        DIM = 256
        HIDDEN = 768
        SCALE = 1.0 / 127.0

        def _dequant(w_int, dtype):
            return w_int.astype(dtype) * jnp.asarray(SCALE, dtype)
        wg = _dequant(w_gate, x.dtype)
        wu = _dequant(w_up, x.dtype)
        wd = _dequant(w_down, x.dtype)
        gate = jnp.einsum('bsd,hd->bsh', x, wg)
        up = jnp.einsum('bsd,hd->bsh', x, wu)
        h = jax.nn.silu(gate) * up
        return jnp.einsum('bsh,dh->bsd', h, wd)
    x = L0_attn_hidden_states
    x = x + _L0_attn_ref(_layernorm(x, axis=-1), L0_attn_Wq, L0_attn_bq, L0_attn_Wk, L0_attn_bk, L0_attn_Wv, L0_attn_bv, L0_attn_Wo, L0_attn_bo, L0_attn_rel_W, L0_attn_rel_b, L0_attn_logical_bias, L0_attn_gate_W, L0_attn_gate_b)
    x = x + _L0_ffn_ref(_layernorm(x, axis=-1), L0_ffn_weight_fp8, L0_ffn_bias, L0_ffn_input_scale, L0_ffn_weight_scale)
    x = x + _L1_attn_ref(_layernorm(x, axis=-1), L1_attn_ln1_w, L1_attn_in_proj_w, L1_attn_conv_w, L1_attn_conv_b, L1_attn_x_proj_w, L1_attn_dt_proj_w, L1_attn_dt_proj_b, L1_attn_A_log, L1_attn_Dp, L1_attn_out_proj_w, L1_attn_ln2_w, L1_attn_fc_w, L1_attn_proj_w)
    x = x + _L1_ffn_ref(_layernorm(x, axis=-1), L1_ffn_w_gate, L1_ffn_w_up, L1_ffn_w_down)
    return x

_drawn_inputs = setup_inputs


def setup_inputs(seed=0):
    import zlib

    import numpy as np

    out = dict(_drawn_inputs(seed))
    spreads = {'L0_attn_bq': (0.0, 0.1),
     'L0_attn_bk': (0.0, 0.1),
     'L0_attn_bv': (0.0, 0.1),
     'L0_attn_bo': (0.0, 0.1),
     'L0_attn_rel_b': (0.0, 0.1),
     'L0_attn_gate_b': (0.0, 0.1),
     'L1_attn_ln1_w': (1.0, 0.2),
     'L1_attn_Dp': (1.0, 0.2),
     'L1_attn_ln2_w': (1.0, 0.2)}
    factors = {}
    for name, (base, spread) in spreads.items():
        noise = np.random.default_rng([zlib.crc32(name.encode()), seed]).standard_normal(out[name].shape)
        drawn = base * np.exp(spread * noise) if base else spread * noise
        out[name] = jnp.asarray(drawn.astype(out[name].dtype))
    for name, factor in factors.items():
        out[name] = (out[name] * factor).astype(out[name].dtype)
    return out
```

```python
import concourse.bass as bass
from concourse import mybir
from concourse.alu_op_type import AluOpType as ALU
from contextlib import ExitStack

ACT = mybir.ActivationFunctionType
F32 = mybir.dt.float32
BF16 = mybir.dt.bfloat16
I32 = mybir.dt.int32
U32 = mybir.dt.uint32
P = 128
BIG = 3.0e38
LN_EPS = 1e-5

B, S, D = 8, 1024, 256
NT = S // P
TILES = B * NT
DC = D // P
H = 16
HD = D // H
HG = 4

Q_PART = [0, 0, 0, 1, 1, 2]
K_PART = [0, 1, 2, 0, 1, 0]
KROWS = HD * len(Q_PART)


def wait(eng, sem, value):
    if isinstance(value, int) and value <= 0:
        return
    eng.wait_ge(sem, value)


def alone(eng, sem, value, own):
    if isinstance(value, int) and value <= 0:
        return
    eng.wait_ge(sem, value)
    eng.sem_inc(own, 1)


def attention(nc, x_in, wqk, wvg, bqk, rows, ident_in, parts_d, x_out):
    NROW = 4
    NAT = 2 * HG
    with ExitStack() as ctx:
        sb = lambda name, shape, dt=F32: ctx.enter_context(nc.sbuf_tensor(name, shape, dt))
        sem = lambda name: ctx.enter_context(nc.semaphore(name))
        psum = lambda name, shape: ctx.enter_context(nc.psum_tensor(name, shape, F32))

        ident = sb("ident", [P, P])
        w_qk = sb("w_qk", [P, DC, 2 * D])
        w_vg = sb("w_vg", [P, DC, D + H + 6])
        w_o = sb("w_o", [P, DC, D])
        w_dj = sb("w_dj", [P, DC, 2, P])
        b_qk = sb("b_qk", [P, 4])
        row = sb("row", [P, 2 * D + H + 3 + 3 * H])
        b_v, b_o = row[:, 0:D], row[:, D:2 * D]
        b_g = row[:, 2 * D:2 * D + H + 3]
        lbk = row[:, 2 * D + H + 3:2 * D + H + 3 + 3 * H].rearrange("p (k h) -> p k h", k=3)
        b_misc = sb("b_misc", [P, H + 2])
        lbd = sb("lbd", [P, 3, H])
        xt = sb("xt", [P, 2, D])
        stats = sb("stats", [P, 6])
        mv = sb("mv", [P, 2])
        ve = sb("ve", [P, 1])
        mhalf = sb("mhalf", [P, 1])
        rstd = sb("rstd", [P, 1])
        xn = sb("xn", [P, D])
        xnT = sb("xnT", [P, DC, P])
        qkf = sb("qkf", [P, 4, P])
        parts = sb("parts", [P, 3, 4, P], BF16)
        zg = sb("zg", [P, H + 2])
        ge = sb("ge", [P, H])
        gate = sb("gate", [P, H])
        small = sb("small", [P, 2 * NT, 3 * H + 2])
        K6 = sb("K6", [KROWS, 2, H, S], BF16)
        V = [sb(f"V{i}", [P, NT, D + HD]) for i in range(2)]
        Dj = sb("Dj", [P, 2, 2, S])
        Q6 = [sb(f"Q6_{i}", [KROWS, H, P], BF16) for i in range(2)]
        R = [[sb(f"R{i}_{k}", [P, S]) for k in range(2)] for i in range(2)]
        RT = sb("RT", [P, S])
        R2 = sb("R2", [P, S])
        cur = [sb(f"cur{i}", [P, 3 * H + 2]) for i in range(2)]
        rows_sb = [sb(f"srow{i}", [P, S]) for i in range(NROW)]
        nmax = sb("nmax", [P, NROW])
        rsum = sb("rsum", [P, 2, H])
        AT = [sb(f"AT{i}", [P, NT, P]) for i in range(NAT)]
        O4 = sb("O4", [P, HG, P])
        rinv = sb("rinv", [P, H])
        attn, attnT = xn, xnT
        xr = sb("xr", [P, D])

        ps_s = psum("ps_s", [P, 2, S])
        ps_t = psum("ps_t", [P, 2, HG, P])
        ps_o = psum("ps_o", [P, HG, P])
        ps_m = psum("ps_m", [P, 4 * P])

        w_in = sem("w_in")
        w_ready = sem("w_ready")
        w_step = sem("w_step")
        x_in_s = sem("x_in_s")
        x_free = sem("x_free")
        ln_step = sem("ln_step")
        rstd_ok = sem("rstd_ok")
        pm = sem("pm")
        pm_free = sem("pm_free")
        om = sem("om")
        om_free = sem("om_free")
        hi_ok = sem("hi_ok")
        rem_ok = sem("rem_ok")
        mid_ok = sem("mid_ok")
        lo_ok = sem("lo_ok")
        parts_w = sem("parts_w")
        k6_in = sem("k6_in")
        q6_in = sem("q6_in")
        zg_ok = sem("zg_ok")
        ge_ok = sem("ge_ok")
        g_step = sem("g_step")
        v_ok = sem("v_ok")
        cur_ok = sem("cur_ok")
        rel_step = sem("rel_step")
        rel_exp = sem("rel_exp")
        rel_sum = sem("rel_sum")
        rel_y0 = sem("rel_y0")
        rel_t = sem("rel_t")
        rel_y = sem("rel_y")
        p_ok = sem("p_ok")
        u_ok = sem("u_ok")
        w_ok = sem("w_ok")
        qk_ok = sem("qk_ok")
        s_ok = sem("s_ok")
        e_ok = sem("e_ok")
        t_ok = sem("t_ok")
        at_ok = sem("at_ok")
        pv_ok = sem("pv_ok")
        o_ok = sem("o_ok")
        rinv_ok = sem("rinv_ok")
        xr_in = sem("xr_in")
        xrb_ok = sem("xrb_ok")
        st = sem("st")
        pool_own, dve_own, sp_own = sem("pool_own"), sem("dve_own"), sem("sp_own")

        def pool_rstd(pool, p):
            alone(pool, ln_step, 3 * p + 3, pool_own)
            nc.gpsimd.tensor_tensor(rstd[:], ve[:], mhalf[:], ALU.pow).then_inc(rstd_ok, 1)

        def pool_rem(pool, p):
            alone(pool, hi_ok, p + 1, pool_own)
            nc.gpsimd.tensor_tensor(qkf[:], qkf[:], parts[:, 0], ALU.subtract).then_inc(rem_ok, 1)

        def pool_lo(pool, p):
            alone(pool, mid_ok, p + 1, pool_own)
            nc.gpsimd.tensor_tensor(parts[:, 2], qkf[:], parts[:, 1], ALU.subtract).then_inc(lo_ok, 1)

        def pool_sum(pool, t, k, n):
            if n == 0:
                alone(pool, rel_exp, t + 1, pool_own)
                nc.gpsimd.tensor_tensor(RT[:], R[k][0][:], R[k][1][:], ALU.add).then_inc(rel_sum, 1)
            else:
                alone(pool, rel_sum, 2 * t + 1, pool_own)
                nc.gpsimd.tensor_tensor(RT[:], RT[:], R2[:], ALU.add).then_inc(rel_sum, 1)

        def pool_t(pool, t):
            alone(pool, rel_y0, 2 * t + 2, pool_own)
            nc.gpsimd.tensor_tensor(RT[:], RT[:], R2[:], ALU.mult).then_inc(rel_t, 1)

        def pool_p(pool, t, k, n):
            if n == 0:
                alone(pool, rel_y, t + 1, pool_own)
            nc.gpsimd.tensor_tensor(R[k][n][:], R[k][n][:], R2[:], ALU.mult).then_inc(p_ok, 1)

        def pool_u(pool, t, k, h):
            U = H * t + h
            if h == 0:
                alone(pool, p_ok, 2 * t + 2, pool_own)
            alone(pool, t_ok, 2 * U + 2, pool_own)
            nc.gpsimd.tensor_scalar(rows_sb[h % NROW][:], R[k][0][:], cur[k][:, h:h + 1],
                                    cur[k][:, 2 * H + h:2 * H + h + 1], ALU.mult, ALU.add).then_inc(u_ok, 1)

        def pool_xrb(pool, o):
            alone(pool, xr_in, 16 * o + 16, pool_own)
            nc.gpsimd.tensor_tensor(xr[:], xr[:], b_o, ALU.add).then_inc(xrb_ok, 1)

        def dve_ln(dve, p, k):
            wait(dve, x_in_s, 16 * p + 16)
            nc.vector.bn_stats(stats[:], xt[:, k, :]).then_inc(ln_step, 1)
            alone(dve, ln_step, 3 * p + 1, dve_own)
            nc.vector.bn_aggr(mv[:], stats[:]).then_inc(ln_step, 1)
            dve.wait_ge(ln_step, 3 * p + 2)
            nc.vector.tensor_scalar(ve[:], mv[:, 1:2], LN_EPS, None, ALU.add).then_inc(ln_step, 1)

        def dve_xn(dve, p, k):
            wait(dve, rstd_ok, p + 1)
            nc.vector.tensor_scalar(xn[:], xt[:, k, :], mv[:, 0:1], rstd[:, 0:1],
                                    ALU.subtract, ALU.mult).then_inc(x_free, 1)

        def dve_qk(dve, p):
            wait(dve, pm, 4 * p + 2)
            nc.vector.tensor_tensor(qkf[:], ps_m[:].rearrange("p (m t) -> p m t", m=4),
                                    b_qk[:].unsqueeze(2).broadcast_to([P, 4, P]), ALU.add).then_inc(pm_free, 1)

        def dve_d(dve, p, par, ib):
            wait(dve, pm, 4 * p + 3)
            nc.vector.tensor_scalar(Dj[:, par, :, bass.ds(ib * P, P)],
                                    ps_m[:, 0:2 * P].rearrange("p (k t) -> p k t", k=2),
                                    1.0, None, ALU.mult).then_inc(pm_free, 1)

        def dve_v(dve, p, par, ib):
            wait(dve, pm, 4 * p + 4)
            nc.vector.tensor_tensor(V[par][:, bass.ds(ib, 1), 0:D], ps_m[:, 0:D].unsqueeze(1),
                                    b_v.unsqueeze(1), ALU.add).then_inc(v_ok, 1)
            nc.vector.tensor_tensor(zg[:], ps_m[:, D:D + H + 2], b_misc[:], ALU.add).then_inc(pm_free, 1)

        def dve_gate(dve, p, par, ib):
            wait(dve, ge_ok, p + 1)
            nc.vector.tensor_scalar(ge[:], ge[:], 1.0, None, ALU.add).then_inc(g_step, 1)
            dve.wait_ge(g_step, 4 * p + 1)
            nc.vector.reciprocal(gate[:], ge[:]).then_inc(g_step, 1)
            dve.wait_ge(g_step, 4 * p + 2)
            idx = par * NT + ib
            nc.vector.tensor_tensor(small[:, bass.ds(idx, 1), 0:3 * H].rearrange("p o (k h) -> p (o k) h", k=3),
                                    lbd[:], gate[:].unsqueeze(1).broadcast_to([P, 3, H]), ALU.mult).then_inc(g_step, 1)
            nc.vector.tensor_scalar(small[:, bass.ds(idx, 1), 3 * H:3 * H + 2], zg[:, H:H + 2].unsqueeze(1),
                                    1.0, None, ALU.mult).then_inc(g_step, 1)

        def dve_rel(dve, t, k):
            par = (t // NT) % 2
            wait(dve, g_step, 4 * (t + 1))
            wait(dve, u_ok, H * (t - 1))
            nc.vector.tensor_scalar(cur[k][:].unsqueeze(1), small[:, bass.ds(t % (2 * NT), 1), :],
                                    1.0, None, ALU.mult).then_inc(cur_ok, 1)
            dve.wait_ge(cur_ok, t + 1)
            wait(dve, pm_free, 4 * (NT * (t // NT) + NT))
            wait(dve, p_ok, 2 * t)
            d10, d20 = (Dj[:, bass.ds(par, 1), i, :].rearrange("p a s -> p (a s)") for i in range(2))
            a10, a20 = (cur[k][:, 3 * H + i:3 * H + i + 1] for i in range(2))
            nc.vector.tensor_scalar(RT[:], d10, a10, 0.0, ALU.add, ALU.max).then_inc(rel_step, 1)
            dve.wait_ge(rel_step, 4 * t + 1)
            nc.vector.scalar_tensor_tensor(RT[:], d20, a20, RT[:], ALU.add, ALU.max).then_inc(rel_step, 1)
            dve.wait_ge(rel_step, 4 * t + 2)
            nc.vector.scalar_tensor_tensor(R[k][1][:], d10, a10, RT[:], ALU.add, ALU.subtract).then_inc(rel_step, 1)
            nc.vector.scalar_tensor_tensor(R2[:], d20, a20, RT[:], ALU.add, ALU.subtract).then_inc(rel_step, 1)

        def dve_y(dve, t):
            wait(dve, rel_t, t + 1)
            nc.vector.scalar_tensor_tensor(R2[:], RT[:], 2.0, R2[:], ALU.subtract, ALU.mult).then_inc(rel_y, 1)

        def dve_w(dve, t, k, h):
            wait(dve, u_ok, H * t + h + 1)
            r = rows_sb[h % NROW]
            nc.vector.scalar_tensor_tensor(r[:], R[k][1][:], cur[k][:, H + h:H + h + 1], r[:],
                                           ALU.mult, ALU.add).then_inc(w_ok, 1)

        def dve_s(dve, t, h):
            wait(dve, w_ok, H * t + h + 1)
            alone(dve, qk_ok, H * t + h + 1, dve_own)
            r = rows_sb[h % NROW]
            nc.vector.tensor_tensor_reduce(r[:], r[:], ps_s[:, h % 2, :], -1.0, BIG, ALU.add, ALU.min,
                                           nmax[:, h % NROW:h % NROW + 1]).then_inc(s_ok, 1)

        def dve_norm(dve, o, k):
            wait(dve, e_ok, H * (o + 1))
            nc.vector.reciprocal(rinv[:], rsum[:, k, :]).then_inc(rinv_ok, 1)
            dve.wait_ge(rinv_ok, o + 1)
            wait(dve, om, 3 * o + 1)
            nc.vector.tensor_tensor(attn[:].rearrange("p (h d) -> p h d", d=HD),
                                    ps_m[:].rearrange("p (h e) -> p h e", e=32)[:, :, 0:HD],
                                    rinv[:].unsqueeze(2).broadcast_to([P, H, HD]), ALU.mult).then_inc(om_free, 1)

        def dve_out(dve, o):
            wait(dve, xrb_ok, o + 1)
            wait(dve, om, 3 * o + 3)
            nc.vector.tensor_tensor(xr[:], ps_m[:, 0:D], xr[:], ALU.add).then_inc(om_free, 1)

        def act_xT(act, p):
            wait(act, pm, 4 * p + 1)
            nc.scalar.copy(xnT[:].rearrange("p c t -> p (c t)"), ps_m[:, 0:D]).then_inc(pm_free, 1)

        def act_hi(act, p):
            wait(act, parts_w, 16 * p + 16)
            wait(act, pm_free, 4 * p + 2 + 1)
            nc.scalar.copy(parts[:, 0], qkf[:]).then_inc(hi_ok, 1)

        def act_mid(act, p):
            wait(act, rem_ok, p + 1)
            nc.scalar.copy(parts[:, 1], qkf[:]).then_inc(mid_ok, 1)

        def act_gate(act, p):
            wait(act, pm_free, 4 * p + 4 + 1)
            nc.scalar.activation(ge[:], zg[:, 0:H], ACT.Exp, scale=-1.0).then_inc(ge_ok, 1)

        def act_rel(act, t, k):
            wait(act, rel_step, 4 * t + 4)
            nc.scalar.activation(R[k][0][:], RT[:], ACT.Exp, scale=-1.0)
            nc.scalar.activation(R[k][1][:], R[k][1][:], ACT.Exp)
            nc.scalar.activation(R2[:], R2[:], ACT.Exp).then_inc(rel_exp, 1)

        def act_y0(act, t):
            wait(act, rel_sum, 2 * t + 2)
            nc.scalar.activation(R2[:], RT[:], ACT.Ln).then_inc(rel_y0, 1)
            act.wait_ge(rel_y0, 2 * t + 1)
            nc.scalar.activation(R2[:], R2[:], ACT.Exp, scale=-1.0).then_inc(rel_y0, 1)

        def act_e(act, t, k, h):
            wait(act, s_ok, H * t + h + 1)
            r = rows_sb[h % NROW]
            nc.scalar.activation(r[:], r[:], ACT.Exp, scale=-1.0, bias=nmax[:, h % NROW:h % NROW + 1],
                                 accum_out=rsum[:, k, h:h + 1]).then_inc(e_ok, 1)

        def act_at(act, t, h):
            U = H * t + h
            if h % HG == 0:
                wait(act, pv_ok, U // HG + 1 if isinstance(U, int) else HG * t + h // HG + 1)
            for half in range(2):
                wait(act, t_ok, 8 + 2 * U + half + 1)
                nc.scalar.copy(AT[h % NAT][:, HG * half:HG * half + HG, :], ps_t[:, half]).then_inc(at_ok, 1)

        def act_o(act, o):
            wait(act, pv_ok, 2 + HG * (o + 1))
            nc.scalar.copy(O4[:], ps_o[:]).then_inc(o_ok, 1)

        def act_aT(act, o):
            wait(act, om, 3 * o + 2)
            nc.scalar.copy(attnT[:].rearrange("p c t -> p (c t)"), ps_m[:, 0:D]).then_inc(om_free, 1)

        def pe_m(pe, p, i, o_done):
            wait(pe, pm_free, 4 * p + i + 1)
            wait(pe, om_free, o_done + 1)

        def pe_xT(pe, p, o_done):
            wait(pe, x_free, p + 1 + 2)
            pe_m(pe, p, 0, o_done)
            for c in range(DC):
                last = nc.tensor.transpose(ps_m[:, c * P:(c + 1) * P], xn[:, c * P:(c + 1) * P], ident[:])
            last.then_inc(pm, 1)

        def pe_qk_proj(pe, p, o_done):
            pe_m(pe, p, 1, o_done)
            for m in range(4):
                for c in range(DC):
                    last = nc.tensor.matmul(ps_m[:, m * P:(m + 1) * P], w_qk[:, c, m * P:(m + 1) * P],
                                            xnT[:, c, :], start=(c == 0), stop=(c == DC - 1))
            last.then_inc(pm, 1)

        def pe_d(pe, p, o_done):
            pe_m(pe, p, 2, o_done)
            for i in range(2):
                for c in range(DC):
                    last = nc.tensor.matmul(ps_m[:, i * P:(i + 1) * P], w_dj[:, c, i, :],
                                            xnT[:, c, :], start=(c == 0), stop=(c == DC - 1))
            last.then_inc(pm, 1)

        def pe_v(pe, p, o_done):
            pe_m(pe, p, 3, o_done)
            for c in range(DC):
                last = nc.tensor.matmul(ps_m[:, 0:D + H + 2], xnT[:, c, :], w_vg[:, c, 0:D + H + 2],
                                        start=(c == 0), stop=(c == DC - 1))
            last.then_inc(pm, 1)

        def pe_s(pe, t, k, h, par):
            U = H * t + h
            if h == 0:
                wait(pe, q6_in, 96 * (t + 1))
                wait(pe, k6_in, 96 * NT * (t // NT + 1))
            wait(pe, s_ok, U - 1)
            for n in range(2):
                if par is None:
                    keys = K6[:, bass.ds((t // NT) % 2, 1), h, n * 512:(n + 1) * 512].rearrange("p a s -> p (a s)")
                else:
                    keys = K6[:, par, h, n * 512:(n + 1) * 512]
                last = nc.tensor.matmul(ps_s[:, h % 2, n * 512:(n + 1) * 512], Q6[k][:, h, :], keys,
                                        start=True, stop=True)
            last.then_inc(qk_ok, 1)

        def pe_t(pe, t, h):
            U = H * t + h
            wait(pe, e_ok, U + 1)
            for half in range(2):
                wait(pe, at_ok, 2 * U + half + 1)
                for i in range(HG):
                    j = HG * half + i
                    last = nc.tensor.transpose(ps_t[:, half, i, :], rows_sb[h % NROW][:, j * P:(j + 1) * P], ident[:])
                last.then_inc(t_ok, 1)

        def pe_pv(pe, t, par, j):
            if j == 0:
                wait(pe, o_ok, t)
                wait(pe, v_ok, 2 + NT * (t // NT + 1))
            wait(pe, at_ok, 2 + 2 * (H * t + HG * j + HG))
            for n in range(NT):
                for i in range(HG):
                    h = HG * j + i
                    last = nc.tensor.matmul(ps_o[32 * i:32 * i + 32, j, :], V[par][:, n, HD * h:HD * h + 32],
                                            AT[h % NAT][:, n, :], start=(n == 0), stop=(n == NT - 1))
            last.then_inc(pv_ok, 1)

        def pe_oT(pe, o, p_done):
            wait(pe, o_ok, o + 1)
            wait(pe, pm_free, p_done + 1)
            wait(pe, om_free, 3 * o + 1)
            for j in range(HG):
                last = nc.tensor.transpose(ps_m[:, j * P:(j + 1) * P], O4[:, j, :], ident[:])
            last.then_inc(om, 1)

        def pe_aT(pe, o, p_done):
            wait(pe, pm_free, p_done + 1)
            wait(pe, om_free, 3 * o + 2)
            for c in range(DC):
                last = nc.tensor.transpose(ps_m[:, c * P:(c + 1) * P], attn[:, c * P:(c + 1) * P], ident[:])
            last.then_inc(om, 1)

        def pe_wo(pe, o, p_done):
            wait(pe, pm_free, p_done + 1)
            wait(pe, om_free, 3 * o + 3)
            for c in range(DC):
                last = nc.tensor.matmul(ps_m[:, 0:D], attnT[:, c, :], w_o[:, c, :],
                                        start=(c == 0), stop=(c == DC - 1))
            last.then_inc(om, 1)

        parts_v = parts_d.rearrange("k (m p) t -> p k m t", p=P)

        def sp_x(sp, p, k):
            alone(sp, x_free, p + 1, sp_own)
            sp.dma_start(xt[:, k, :], x_in[bass.ds(p * P, P), :]).then_inc(x_in_s, 16)

        def sp_parts(sp, p, par, ib, k_free):
            alone(sp, x_in_s, 16 * p + 16, sp_own)
            alone(sp, lo_ok, p + 1, sp_own)
            sp.dma_start(parts_v[:, :, :, bass.ds(p * P, P)], parts[:]).then_inc(parts_w, 16)
            alone(sp, parts_w, 16 * p + 32, sp_own)
            alone(sp, qk_ok, k_free, sp_own)
            for s, part in enumerate(K_PART):
                sp.dma_start(K6[HD * s:HD * s + HD, par, :, bass.ds(ib * P, P)],
                             parts_d[part, D:2 * D, bass.ds(p * P, P)].rearrange("(h d) t -> d h t", d=HD)
                             ).then_inc(k6_in, 16)
            alone(sp, k6_in, 96 * (p + 1), sp_own)

        def sp_q6(sp, t, k):
            alone(sp, q6_in, 96 * t, sp_own)
            alone(sp, qk_ok, H * (t - 1), sp_own)
            for s, part in enumerate(Q_PART):
                sp.dma_start(Q6[k][HD * s:HD * s + HD, :, :],
                             parts_d[part, 0:D, bass.ds(t * P, P)].rearrange("(h d) t -> d h t", d=HD)
                             ).then_inc(q6_in, 16)

        def sp_xr(sp, o):
            alone(sp, st, 16 * o, sp_own)
            sp.dma_start(xr[:], x_in[bass.ds(o * P, P), :]).then_inc(xr_in, 16)

        def sp_out(sp, o):
            alone(sp, om_free, 3 * o + 4, sp_own)
            sp.dma_start(x_out[bass.ds(o * P, P), :], xr[:]).then_inc(st, 16)

        def run(eng, start, project, body, finish):
            with eng.Fori(0, NT // 2) as i:
                for k in range(2):
                    project(eng, 2 * i + k, k, 0, 2 * i + k)
            start(eng)
            for k in range(2):
                body(eng, k, k, 0, k, True, k > 0, True)
            with eng.Fori(1, NT // 2) as i:
                for k in range(2):
                    body(eng, 2 * i + k, k, 0, 2 * i + k, True, True, True)
            with eng.Fori(0, (B - 2) // 2) as j:
                for par in (1, 0):
                    first = (2 * j + (1 if par else 2)) * NT
                    with eng.Fori(0, NT // 2) as i:
                        for k in range(2):
                            body(eng, first + 2 * i + k, k, par, 2 * i + k, True, True, True)
            with eng.Fori(0, NT // 2 - 1) as i:
                for k in range(2):
                    body(eng, (B - 1) * NT + 2 * i + k, k, 1, 2 * i + k, False, True, True)
            for k in range(2):
                body(eng, TILES - 2 + k, k, 1, NT - 2 + k, False, True, k == 0)
            finish(eng)

        block = ctx.enter_context(nc.Block())

        @block.sync
        def _(sp):
            def project(sp, p, k, par, ib):
                sp_x(sp, p, k)
                sp_parts(sp, p, par, ib, 0)

            def start(sp):
                sp_q6(sp, 0, 0)

            def body(sp, t, k, par, ib, pro, post, look):
                if look:
                    sp_q6(sp, t + 1, 1 - k)
                if post:
                    sp_xr(sp, t - 1)
                if pro:
                    sp_x(sp, t + NT, k)
                    sp_parts(sp, t + NT, 1 - par, ib, H * NT * (t // NT))
                if post:
                    sp_out(sp, t - 1)

            def finish(sp):
                sp_xr(sp, TILES - 1)
                sp_out(sp, TILES - 1)
                sp.wait_ge(st, 16 * TILES)

            for dst, src in ((w_qk[:], wqk.rearrange("(c p) n -> p c n", p=P)),
                             (w_vg[:], wvg[:, 0:D + H + 6].rearrange("(c p) n -> p c n", p=P)),
                             (w_o[:], wvg[:, D + H + 6:].rearrange("(c p) n -> p c n", p=P)),
                             (b_qk[:], bqk), (row[:], rows.partition_broadcast(P)), (ident[:], ident_in)):
                sp.dma_start(dst, src).then_inc(w_in, 16)
            sp.sem_inc(parts_w, 16)
            run(sp, start, project, body, finish)

        @block.gpsimd
        def _(pool):
            def project(pool, p, k, par, ib):
                pool_rstd(pool, p)
                pool_rem(pool, p)
                pool_lo(pool, p)

            def start(pool):
                pool_sum(pool, 0, 0, 0)
                pool_sum(pool, 0, 0, 1)
                pool_t(pool, 0)
                pool_p(pool, 0, 0, 0)
                pool_p(pool, 0, 0, 1)
                pool_u(pool, 0, 0, 0)
                pool_u(pool, 0, 0, 1)

            def body(pool, t, k, par, ib, pro, post, look):
                for u in range(H):
                    if u + 2 < H:
                        pool_u(pool, t, k, u + 2)
                    elif look:
                        pool_u(pool, t + 1, 1 - k, u + 2 - H)
                    if pro and u == 0:
                        pool_rstd(pool, t + NT)
                    if pro and u == 5:
                        pool_rem(pool, t + NT)
                    if pro and u == 6:
                        pool_lo(pool, t + NT)
                    if look and u in (7, 8):
                        pool_sum(pool, t + 1, 1 - k, u - 7)
                    if post and u == 9:
                        pool_xrb(pool, t - 1)
                    if look and u == 10:
                        pool_t(pool, t + 1)
                    if look and u in (12, 13):
                        pool_p(pool, t + 1, 1 - k, u - 12)

            def finish(pool):
                pool_xrb(pool, TILES - 1)

            nc.gpsimd.memset(mhalf[:], -0.5)
            for v in V:
                nc.gpsimd.memset(v[:, :, D:D + HD], 0.0).then_inc(v_ok, 1)
            pool.wait_ge(v_ok, 2)
            run(pool, start, project, body, finish)

        @block.vector
        def _(dve):
            def project(dve, p, k, par, ib):
                dve_ln(dve, p, k)
                dve_xn(dve, p, k)
                dve_qk(dve, p)
                dve_d(dve, p, par, ib)
                dve_v(dve, p, par, ib)
                dve_gate(dve, p, par, ib)

            def start(dve):
                dve_rel(dve, 0, 0)
                dve_y(dve, 0)
                dve_w(dve, 0, 0, 0)

            def body(dve, t, k, par, ib, pro, post, look):
                for u in range(H):
                    if u + 1 < H:
                        dve_w(dve, t, k, u + 1)
                    elif look:
                        dve_w(dve, t + 1, 1 - k, 0)
                    dve_s(dve, t, u)
                    if pro and u == 0:
                        dve_ln(dve, t + NT, k)
                    if pro and u == 1:
                        dve_xn(dve, t + NT, k)
                    if pro and u == 3:
                        dve_qk(dve, t + NT)
                    if pro and u == 4:
                        dve_d(dve, t + NT, 1 - par, ib)
                    if post and u == 5:
                        dve_norm(dve, t - 1, 1 - k)
                    if look and u == 5:
                        dve_rel(dve, t + 1, 1 - k)
                    if pro and u == 7:
                        dve_v(dve, t + NT, 1 - par, ib)
                    if pro and u == 9:
                        dve_gate(dve, t + NT, 1 - par, ib)
                    if look and u == 11:
                        dve_y(dve, t + 1)
                    if post and u == 12:
                        dve_out(dve, t - 1)

            def finish(dve):
                dve_norm(dve, TILES - 1, 1)
                dve_out(dve, TILES - 1)

            dve.wait_ge(w_in, 16 * 6)
            nc.vector.tensor_scalar(w_qk[:, :, 0:D], w_qk[:, :, 0:D], 1.0 / HD ** 0.5, None, ALU.mult)
            nc.vector.tensor_scalar(b_qk[:, 0:DC], b_qk[:, 0:DC], 1.0 / HD ** 0.5, None, ALU.mult)
            ri, rj = D + H, D + H + 3
            for i in range(2):
                nc.vector.tensor_tensor(w_dj[:, :, i, :], w_vg[:, :, rj + 1 + i:rj + 2 + i].broadcast_to([P, DC, P]),
                                        w_vg[:, :, rj:rj + 1].broadcast_to([P, DC, P]), ALU.subtract)
                nc.vector.tensor_tensor(b_misc[:, H + i:H + i + 1], b_g[:, H + 1 + i:H + 2 + i], b_g[:, H:H + 1],
                                        ALU.subtract)
                nc.vector.tensor_tensor(lbd[:, i, :], lbk[:, 2, :], lbk[:, i, :], ALU.subtract)
            nc.vector.tensor_copy(b_misc[:, 0:H], b_g[:, 0:H])
            nc.vector.tensor_copy(lbd[:, 2, :], lbk[:, 2, :]).then_inc(w_step, 1)
            dve.wait_ge(w_step, 1)
            nc.vector.tensor_tensor(rinv[:, 0:DC], w_vg[:, :, ri + 1], w_vg[:, :, ri], ALU.subtract)
            nc.vector.tensor_tensor(rinv[:, DC:2 * DC], w_vg[:, :, ri + 2], w_vg[:, :, ri], ALU.subtract
                                    ).then_inc(w_step, 1)
            dve.wait_ge(w_step, 2)
            nc.vector.tensor_copy(w_vg[:, :, ri], rinv[:, 0:DC])
            nc.vector.tensor_copy(w_vg[:, :, ri + 1], rinv[:, DC:2 * DC]).then_inc(w_ready, 1)
            dve.wait_ge(w_ready, 1)
            dve.sem_inc(x_free, 2)
            dve.sem_inc(pm_free, 1)
            dve.sem_inc(om_free, 1)
            run(dve, start, project, body, finish)

        @block.scalar
        def _(act):
            def project(act, p, k, par, ib):
                act_xT(act, p)
                act_hi(act, p)
                act_mid(act, p)
                act_gate(act, p)

            def start(act):
                act_rel(act, 0, 0)
                act_y0(act, 0)

            def body(act, t, k, par, ib, pro, post, look):
                for u in range(H):
                    act_e(act, t, k, u)
                    if u:
                        act_at(act, t, u - 1)
                    if post and u == 1:
                        act_o(act, t - 1)
                    if pro and u == 2:
                        act_xT(act, t + NT)
                    if pro and u == 4:
                        act_hi(act, t + NT)
                    if pro and u == 6:
                        act_mid(act, t + NT)
                    if look and u == 6:
                        act_rel(act, t + 1, 1 - k)
                    if pro and u == 8:
                        act_gate(act, t + NT)
                    if post and u == 8:
                        act_aT(act, t - 1)
                    if look and u == 9:
                        act_y0(act, t + 1)
                act_at(act, t, H - 1)

            def finish(act):
                act_o(act, TILES - 1)
                act_aT(act, TILES - 1)

            act.preload_act_table_set("natural_log_exp_and_others")
            act.sem_inc(at_ok, 2)
            run(act, start, project, body, finish)

        @block.tensor
        def _(pe):
            def project(pe, p, k, par, ib):
                pe_xT(pe, p, 0)
                pe_qk_proj(pe, p, 0)
                pe_d(pe, p, 0)
                pe_v(pe, p, 0)

            def start(pe):
                pe_s(pe, 0, 0, 0, 0)
                pe_s(pe, 0, 0, 1, 0)

            def body(pe, t, k, par, ib, pro, post, look):
                o = t - 1
                p = t + NT
                done = 3 * o if post else 0
                last_p = 4 * TILES
                for u in range(H):
                    if u + 2 < H:
                        pe_s(pe, t, k, u + 2, par)
                    elif look:
                        pe_s(pe, t + 1, 1 - k, u + 2 - H, None)
                    pe_t(pe, t, u)
                    if u and u % HG == 0:
                        pe_pv(pe, t, par, u // HG - 1)
                    if pro and u == 2:
                        pe_xT(pe, p, done)
                    if pro and u == 3:
                        pe_qk_proj(pe, p, done)
                    if pro and u == 4:
                        pe_d(pe, p, done)
                    if post and u == 5:
                        pe_oT(pe, o, 4 * p + 3 if pro else last_p)
                    if pro and u == 6:
                        pe_v(pe, p, done + 1 if post else 0)
                    if post and u == 8:
                        pe_aT(pe, o, 4 * p + 4 if pro else last_p)
                    if post and u == 10:
                        pe_wo(pe, o, 4 * p + 4 if pro else last_p)
                pe_pv(pe, t, par, HG - 1)

            def finish(pe):
                pe_oT(pe, TILES - 1, 4 * TILES)
                pe_aT(pe, TILES - 1, 4 * TILES)
                pe_wo(pe, TILES - 1, 4 * TILES)

            pe.wait_ge(w_ready, 1)
            pe.sem_inc(t_ok, 8)
            pe.sem_inc(pv_ok, 2)
            run(pe, start, project, body, finish)


G = 4
GROUPS = TILES // G
GT = G * P


def norm_stats(nc, dve, x, stats, mv, ve, step, base, own):
    for i in range(G):
        last = nc.vector.bn_stats(stats[:, i, :], x[:, i, :])
    last.then_inc(step, 1)
    alone(dve, step, base + 1, own)
    for i in range(G):
        last = nc.vector.bn_aggr(mv[:, i, :], stats[:, i, :])
    last.then_inc(step, 1)
    dve.wait_ge(step, base + 2)
    nc.vector.tensor_scalar(ve[:].unsqueeze(2), mv[:, :, 1:2], LN_EPS, None, ALU.add).then_inc(step, 1)


def norm_apply(nc, dve, out, x, mv, rstd):
    for i in range(G):
        last = nc.vector.tensor_scalar(out[:, i, :], x[:, i, :], mv[:, i, 0:1], rstd[:, i:i + 1],
                                               ALU.subtract, ALU.mult)
    return last


def fp8_layer(nc, x_in, w8, scales, col, bias, ident_in, x_out, xc_out, xl_out):
    with ExitStack() as ctx:
        sb = lambda name, shape, dt=F32: ctx.enter_context(nc.sbuf_tensor(name, shape, dt))
        sem = lambda name: ctx.enter_context(nc.semaphore(name))
        ident = sb("b_ident", [P, P])
        w = sb("b_w", [P, DC, D])
        sc = sb("b_sc", [P, 2])
        rs = sb("b_rs", [P, 1])
        ln_w = sb("b_ln_w", [P, DC])
        b_row = sb("b_row", [P, 1, D])
        mhalf = sb("b_mhalf", [P, G])
        xt = [sb(f"b_xt{i}", [P, G, D]) for i in range(2)]
        xb = sb("b_xb", [P, G, D])
        stats = sb("b_stats", [P, G, 6])
        mv = sb("b_mv", [P, G, 2])
        ve = sb("b_ve", [P, G])
        rstd = sb("b_rstd", [P, G])
        xn = sb("b_xn", [P, G, D])
        mag = sb("b_mag", [P, G, D])
        xq = sb("b_xq", [P, G, D])
        xT = sb("b_xT", [P, G // 2, 2, DC, P])
        x2 = sb("b_x2", [P, G, D])
        xc = sb("b_xc", [P, G, D])
        x3 = sb("b_x3", [P, G, D])
        xl = sb("b_xl", [P, DC, G, P])
        ps_t = [ctx.enter_context(nc.psum_tensor(f"b_ps_t{i}", [P, 2, DC, P], F32)) for i in range(2)]
        ps_y = [ctx.enter_context(nc.psum_tensor(f"b_ps_y{i}", [P, 2, D], F32)) for i in range(2)]
        w_in, w_ok = sem("b_w_in"), sem("b_w_ok")
        x_in_s, x_free = sem("b_x_in"), sem("b_x_free")
        step, r_ok, q_step = sem("b_step"), sem("b_r_ok"), sem("b_q_step")
        xb_ok, xb_free = sem("b_xb_ok"), sem("b_xb_free")
        t_ok, t_free = sem("b_t_ok"), sem("b_t_free")
        y_ok, y_free = sem("b_y_ok"), sem("b_y_free")
        xc_ok, x3_ok = sem("b_xc_ok"), sem("b_x3_ok")
        stored = sem("b_stored")
        pool_own, dve_own, sp_own, act_own = (sem(f"b_{e}_own") for e in ("pool", "dve", "sp", "act"))
        block = ctx.enter_context(nc.Block())

        def loop(eng, body):
            with eng.Fori(0, GROUPS // 2) as i:
                for k in range(2):
                    body(2 * i + k, k)

        @block.sync
        def _(sp):
            for dst, src in ((w[:], w8.rearrange("(c p) n -> p c n", p=P)), (sc[:], scales.partition_broadcast(P)),
                             (ln_w[:], col), (b_row[:, 0], bias.partition_broadcast(P)), (ident[:], ident_in)):
                sp.dma_start(dst, src).then_inc(w_in, 16)
            sp.dma_start(xt[0][:], x_in[0:GT, :].rearrange("(i p) d -> p i d", p=P)).then_inc(x_in_s, 16)
            sp.sem_inc(stored, 48)

            def body(g, k):
                tok = bass.ds(g * GT, GT)
                nxt = bass.ds(((g + 1) % GROUPS) * GT, GT)
                alone(sp, x_in_s, 16 * g + 16, sp_own)
                alone(sp, x_free, g + 1, sp_own)
                sp.dma_start(xt[1 - k][:], x_in[nxt, :].rearrange("(i p) d -> p i d", p=P)).then_inc(x_in_s, 16)
                alone(sp, xc_ok, g + 1, sp_own)
                sp.dma_start(x_out[tok, :].rearrange("(i p) d -> p i d", p=P), x2[:]).then_inc(stored, 16)
                sp.dma_start(xc_out[tok, :].rearrange("(i p) d -> p i d", p=P), xc[:]).then_inc(stored, 16)
                alone(sp, t_free, 4 * g + 4 + 2, sp_own)
                sp.dma_start(xl_out[:, tok].rearrange("(c p) t -> p c t", p=P),
                             xl[:].rearrange("p c i t -> p c (i t)")).then_inc(stored, 16)
            loop(sp, body)
            sp.wait_ge(stored, 48 * GROUPS + 48)
            sp.wait_ge(x_in_s, 16 * GROUPS + 16)

        @block.gpsimd
        def _(pool):
            nc.gpsimd.memset(mhalf[:], -0.5).then_inc(pool_own, 1)
            pool.wait_ge(pool_own, 1)
            pool.wait_ge(w_in, 16 * 5)

            def body(g, k):
                alone(pool, x_in_s, 16 * g + 16, pool_own)
                alone(pool, xb_free, g + 1, pool_own)
                nc.gpsimd.tensor_tensor(xb[:], xt[k][:], b_row[:].broadcast_to([P, G, D]), ALU.add).then_inc(xb_ok, 1)
                for n in range(3):
                    alone(pool, step, 9 * g + 3 * n + 3, pool_own)
                    nc.gpsimd.tensor_tensor(rstd[:], ve[:], mhalf[:], ALU.pow).then_inc(r_ok, 1)
            loop(pool, body)

        @block.vector
        def _(dve):
            dve.wait_ge(w_in, 16 * 5)
            nc.vector.reciprocal(rs[:], sc[:, 0:1])
            nc.vector.tensor_scalar(w[:], w[:], sc[:, 1:2], None, ALU.mult).then_inc(w_ok, 1)
            dve.wait_ge(w_ok, 1)
            dve.sem_inc(x_free, 1)
            dve.sem_inc(xb_free, 1)
            dve.sem_inc(y_free, 2)

            def body(g, k):
                dve.wait_ge(x_in_s, 16 * g + 16)
                norm_stats(nc, dve, xt[k], stats, mv, ve, step, 9 * g, dve_own)
                dve.wait_ge(r_ok, 3 * g + 1)
                norm_apply(nc, dve, xn, xt[k], mv, rstd).then_inc(x_free, 1)
                dve.wait_ge(x_free, g + 2)
                nc.vector.tensor_scalar(xn[:], xn[:], rs[:, 0:1], 448.0, ALU.mult, ALU.min).then_inc(q_step, 1)
                dve.wait_ge(q_step, 5 * g + 1)
                nc.vector.tensor_scalar(xn[:], xn[:], -448.0, None, ALU.max).then_inc(q_step, 1)
                dve.wait_ge(q_step, 5 * g + 2)
                nc.vector.tensor_scalar(mag[:].bitcast(U32), xn[:].bitcast(U32), 0x7F800000, None,
                                        ALU.bitwise_and).then_inc(q_step, 1)
                dve.wait_ge(q_step, 5 * g + 3)
                nc.vector.tensor_scalar(mag[:], mag[:], 2.0 ** -6, 1.5 * 2.0 ** 20, ALU.max, ALU.mult).then_inc(q_step, 1)
                dve.wait_ge(q_step, 5 * g + 4)
                nc.vector.tensor_tensor(xn[:], xn[:], mag[:], ALU.add).then_inc(q_step, 1)
                dve.wait_ge(q_step, 5 * g + 5)
                nc.vector.tensor_tensor(xq[:], xn[:], mag[:], ALU.subtract).then_inc(x3_ok, 1)
                dve.wait_ge(xb_ok, g + 1)
                dve.wait_ge(stored, 48 * g + 48)
                for j in range(2):
                    dve.wait_ge(y_ok, 2 * g + j + 1)
                    nc.vector.tensor_tensor(x2[:, 2 * j:2 * j + 2, :], ps_y[j][:], xb[:, 2 * j:2 * j + 2, :],
                                            ALU.add).then_inc(y_free, 1)
                dve.wait_ge(y_free, 2 * g + 2 + 2)
                norm_stats(nc, dve, x2, stats, mv, ve, step, 9 * g + 3, dve_own)
                dve.wait_ge(r_ok, 3 * g + 2)
                norm_apply(nc, dve, xc, x2, mv, rstd).then_inc(xc_ok, 1)
                dve.wait_ge(xc_ok, g + 1)
                norm_stats(nc, dve, xc, stats, mv, ve, step, 9 * g + 6, dve_own)
                dve.wait_ge(r_ok, 3 * g + 3)
                norm_apply(nc, dve, x3, xc, mv, rstd).then_inc(xb_free, 1)
            loop(dve, body)

        @block.scalar
        def _(act):
            act.wait_ge(w_in, 16 * 5)
            act.sem_inc(t_free, 2)

            def body(g, k):
                for j in range(2):
                    act.wait_ge(t_ok, 4 * g + j + 1)
                    nc.scalar.activation(xT[:, j], ps_t[j][:], ACT.Copy, scale=sc[:, 0:1]).then_inc(t_free, 1)
                act.wait_ge(stored, 48 * g + 48)
                for j in range(2):
                    act.wait_ge(t_ok, 4 * g + 2 + j + 1)
                    for c in range(DC):
                        last = nc.scalar.activation(xl[:, c, 2 * j:2 * j + 2, :], ps_t[j][:, :, c, :], ACT.Copy,
                                                    scale=ln_w[:, c:c + 1])
                    last.then_inc(t_free, 1)
            loop(act, body)

        @block.tensor
        def _(pe):
            pe.wait_ge(w_ok, 1)

            def body(g, k):
                for n, src in enumerate((xq, x3)):
                    if n == 0:
                        pe.wait_ge(x3_ok, g + 1)
                    else:
                        pe.wait_ge(xb_free, g + 2)
                    for j in range(2):
                        pe.wait_ge(t_free, 4 * g + 2 * n + j + 1)
                        for i in range(2):
                            for c in range(DC):
                                last = nc.tensor.transpose(ps_t[j][:, i, c, :], src[:, 2 * j + i, c * P:(c + 1) * P],
                                                           ident[:])
                        last.then_inc(t_ok, 1)
                    if n == 0:
                        for j in range(2):
                            pe.wait_ge(t_free, 4 * g + j + 1 + 2)
                            pe.wait_ge(y_free, 2 * g + j + 1)
                            for i in range(2):
                                for c in range(DC):
                                    last = nc.tensor.matmul(ps_y[j][:, i, :], xT[:, j, i, c, :], w[:, c, :],
                                                            start=(c == 0), stop=(c == DC - 1))
                            last.then_inc(y_ok, 1)
            loop(pe, body)


DI = 512
CH = DI // P
NS = 16
DTR = 16
TAPS = 4
HALF = 512
NH = S // HALF
BC3 = 3 * 2 * NS


def mixer(nc, xl_in, w_in_d, w_x_d, w_dt_d, cols_d, sel_d, ident_in, y_out):
    with ExitStack() as ctx:
        sb = lambda name, shape, dt=F32: ctx.enter_context(nc.sbuf_tensor(name, shape, dt))
        sem = lambda name: ctx.enter_context(nc.semaphore(name))
        ident = sb("c_ident", [P, P])
        w_i = sb("c_w_i", [P, DC, 2 * DI])
        w_x = sb("c_w_x", [P, CH, BC3 + DTR])
        w_dt = sb("c_w_dt", [BC3 + DTR, DI])
        cols = sb("c_cols", [P, CH, TAPS + 3 + NS])
        taps, conv_b, dt_b, d_p = (cols[:, :, 0:TAPS], cols[:, :, TAPS:TAPS + 1], cols[:, :, TAPS + 1:TAPS + 2],
                                   cols[:, :, TAPS + 2:TAPS + 3])
        a_neg = sb("c_a_neg", [P, CH, NS])
        sel = sb("c_sel", [BC3, 2 * NS, P], BF16)
        xl = sb("c_xl", [P, DC, S])
        xpad = sb("c_xpad", [P, CH, TAPS - 1 + S])
        sz = sb("c_sz", [P, CH, S])
        xc = sb("c_xc", [P, CH, S])
        conv = sb("c_conv", [P, CH, S])
        dt = sb("c_dt", [P, CH, S])
        bc = sb("c_bc", [BC3 + DTR, S])
        bc_mid = sb("c_bc_mid", [BC3, S], BF16)
        stack = sb("c_stack", [BC3, S], BF16)
        NB = 4
        bs = [sb(f"c_bs{i}", [P, S]) for i in range(2)]
        da = [sb(f"c_da{i}", [P, S]) for i in range(NB)]
        db = [sb(f"c_db{i}", [P, S]) for i in range(NB)]
        ps_y = ctx.enter_context(nc.psum_tensor("c_ps_y", [P, 2, S], F32))
        ps_b = ctx.enter_context(nc.psum_tensor("c_ps_b", [P, S], F32))
        ps_c = ctx.enter_context(nc.psum_tensor("c_ps_c", [P, S], F32))

        w_in, w_ok = sem("c_w_in"), sem("c_w_ok")
        xl_in_s = sem("c_xl_in")
        pi_ok, pi_free = sem("c_pi_ok"), sem("c_pi_free")
        conv_ok, xc_ok = sem("c_conv_ok"), sem("c_xc_ok")
        bc_ok, bc_step = sem("c_bc_ok"), sem("c_bc_step")
        sp_a, sp_v, dt_ok, dtx_ok = sem("c_sp_a"), sem("c_sp_v"), sem("c_dt_ok"), sem("c_dtx_ok")
        b_ok, c_ok, b_free = sem("c_b_ok"), sem("c_c_ok"), sem("c_b_free")
        bs_ok, da_ok, db_ok = sem("c_bs_ok"), sem("c_da_ok"), sem("c_db_ok")
        h_ok, hc_ok, acc_ok = sem("c_h_ok"), sem("c_hc_ok"), sem("c_acc_ok")
        y_step, y_ok, stored = sem("c_y_step"), sem("c_y_ok"), sem("c_stored")
        pool_own, dve_own, act_own, sp_own = (sem(f"c_{e}_own") for e in ("pool", "dve", "act", "sp"))
        block = ctx.enter_context(nc.Block())
        FRONT = 2 * 2 * CH + NH + CH * NH
        UNITS = CH * NS
        front_ps = [ps_b, ps_c]

        def n_of(b, pair, n):
            return (2 * b + pair) * NS + n

        @block.sync
        def _(sp):
            for dst, src in ((w_i[:], w_in_d.rearrange("(c p) n -> p c n", p=P)),
                             (w_x[:], w_x_d.rearrange("(c p) n -> p c n", p=P)),
                             (w_dt[BC3:BC3 + DTR, :], w_dt_d), (cols[:], cols_d.rearrange("(c p) n -> p c n", p=P)),
                             (sel[:], sel_d.rearrange("r (n p) -> r n p", p=P)), (ident[:], ident_in)):
                sp.dma_start(dst, src).then_inc(w_in, 16)
            sp.sem_inc(stored, 16)
            with sp.Fori(0, B) as b:
                alone(sp, pi_free, FRONT * b + 2, sp_own)
                sp.dma_start(xl[:], xl_in[:, bass.ds(b * S, S)].rearrange("(c p) t -> p c t", p=P)).then_inc(xl_in_s, 16)
                for pair in range(CH // 2):
                    for c in range(2):
                        m = 2 * pair + c
                        alone(sp, y_ok, CH * b + m + 1, sp_own)
                        sp.dma_start(y_out[m * P:(m + 1) * P, bass.ds(b * S, S)], conv[:, m, :]).then_inc(stored, 16)
            sp.wait_ge(stored, 16 * CH * B + 16)

        @block.tensor
        def _(pe):
            pe.wait_ge(w_in, 16 * 6)

            def front(b):
                pe.wait_ge(xl_in_s, 16 * b + 16)
                n_out = 0

                def out(rows=P):
                    nonlocal n_out
                    pe.wait_ge(pi_free, FRONT * b + n_out + 1)
                    if n_out < 2:
                        pe.wait_ge(hc_ok, UNITS * b + 1)
                    n_out += 1
                    return front_ps[(n_out - 1) % 2][0:rows, 0:HALF]

                for m in range(2 * CH):
                    for n in range(NH):
                        o = out()
                        for c in range(DC):
                            last = nc.tensor.matmul(o, w_i[:, c, m * P:(m + 1) * P], xl[:, c, n * HALF:(n + 1) * HALF],
                                                    start=(c == 0), stop=(c == DC - 1))
                        last.then_inc(pi_ok, 1)
                pe.wait_ge(xc_ok, CH * b + CH)
                for n in range(NH):
                    o = out(BC3 + DTR)
                    for c in range(CH):
                        last = nc.tensor.matmul(o, w_x[:, c, :], xc[:, c, n * HALF:(n + 1) * HALF],
                                                start=(c == 0), stop=(c == CH - 1))
                    last.then_inc(pi_ok, 1)
                pe.wait_ge(bc_ok, NH * b + NH)
                for m in range(CH):
                    for n in range(NH):
                        o = out()
                        nc.tensor.matmul(o, w_dt[BC3:BC3 + DTR, m * P:(m + 1) * P],
                                         bc[BC3:BC3 + DTR, n * HALF:(n + 1) * HALF],
                                         start=True, stop=True).then_inc(pi_ok, 1)

            def broadcast(b, pair, n, k, first):
                N = n_of(b, pair, n)
                if first:
                    pe.wait_ge(bc_step, 5 * b + 5)
                    pe.wait_ge(pi_free, FRONT * (b + 1) + 2)
                pe.wait_ge(b_free, N + 1)
                for half in range(NH):
                    last = nc.tensor.matmul(ps_b[:, half * HALF:(half + 1) * HALF],
                                            sel[:, bass.ds(n, 1), :].rearrange("r a p -> r (a p)"),
                                            stack[:, half * HALF:(half + 1) * HALF], start=True, stop=True)
                last.then_inc(b_ok, 1)
                pe.wait_ge(hc_ok, 2 * N + 1)
                for half in range(NH):
                    last = nc.tensor.matmul(ps_c[:, half * HALF:(half + 1) * HALF],
                                            sel[:, bass.ds(NS + n, 1), :].rearrange("r a p -> r (a p)"),
                                            stack[:, half * HALF:(half + 1) * HALF], start=True, stop=True)
                last.then_inc(c_ok, 1)

            def sums(b, pair, n, k, start, stop):
                N = n_of(b, pair, n)
                for c in range(2):
                    pe.wait_ge(hc_ok, 2 * N + c + 1 + 1)
                    for half in range(NH):
                        cut = slice(half * HALF, (half + 1) * HALF)
                        last = nc.tensor.matmul(ps_y[:, c, cut], ident[:], da[(2 * k + c) % NB][:, cut],
                                                start=start, stop=stop)
                    last.then_inc(acc_ok, 1)

            with pe.Fori(0, B) as b:
                front(b)
                for pair in range(CH // 2):
                    pe.wait_ge(y_step, 2 * (2 * b + pair) + 1)
                    broadcast(b, pair, 0, 0, pair == 0)
                    broadcast(b, pair, 1, 1, False)
                    sums(b, pair, 0, 0, True, False)
                    with pe.Fori(0, NS // 2 - 1) as i:
                        for k in range(2):
                            broadcast(b, pair, 2 * i + 2 + k, k, False)
                            sums(b, pair, 2 * i + 1 + k, 1 - k, False, False)
                    sums(b, pair, NS - 1, 1, False, True)

        @block.gpsimd
        def _(pool):
            with pool.Fori(0, B) as b:
                for pair in range(CH // 2):
                    for c in range(2):
                        m = 2 * pair + c
                        alone(pool, dt_ok, CH * b + m + 1, pool_own)
                        nc.gpsimd.tensor_tensor(conv[:, m, :], dt[:, m, :], xc[:, m, :], ALU.mult).then_inc(dtx_ok, 1)
                    alone(pool, dtx_ok, CH * b + 2 * pair + 2, pool_own)
                    with pool.Fori(0, NS // 2) as i:
                        for k in range(2):
                            N = n_of(b, pair, 2 * i + k)
                            alone(pool, bs_ok, N + 1, pool_own)
                            for c in range(2):
                                alone(pool, h_ok, 2 * N + c + 1, pool_own)
                                nc.gpsimd.tensor_tensor(db[2 * k + c][:], conv[:, 2 * pair + c, :], bs[k][:],
                                                        ALU.mult).then_inc(db_ok, 1)

        @block.scalar
        def _(act):
            act.wait_ge(w_in, 16 * 6)
            nc.scalar.activation(a_neg[:], cols[:, :, TAPS + 3:], ACT.Exp).then_inc(w_ok, 1)
            act.sem_inc(b_free, 1)
            act.sem_inc(pi_free, 2)

            def front(b):
                for m in range(2 * CH):
                    for n in range(NH):
                        i = NH * m + n
                        act.wait_ge(pi_ok, FRONT * b + i + 1)
                        src = front_ps[i % 2][:, 0:HALF]
                        if m < CH:
                            nc.scalar.copy(xpad[:, m, TAPS - 1 + n * HALF:TAPS - 1 + (n + 1) * HALF], src
                                           ).then_inc(pi_free, 1)
                        else:
                            nc.scalar.activation(sz[:, m - CH, n * HALF:(n + 1) * HALF], src, ACT.Silu
                                                 ).then_inc(pi_free, 1)
                for m in range(CH):
                    act.wait_ge(conv_ok, CH * TAPS * b + CH * (TAPS - 1) + m + 1)
                    nc.scalar.activation(xc[:, m, :], conv[:, m, :], ACT.Silu, bias=conv_b[:, m, :]).then_inc(xc_ok, 1)
                base = 2 * 2 * CH
                for n in range(NH):
                    act.wait_ge(pi_ok, FRONT * b + base + n + 1)
                    nc.scalar.copy(bc[:, n * HALF:(n + 1) * HALF], front_ps[(base + n) % 2][0:BC3 + DTR, 0:HALF]
                                   ).then_inc(bc_ok, 1)
                    act.wait_ge(bc_ok, NH * b + n + 1)
                    act.sem_inc(pi_free, 1)
                base += NH
                for m in range(CH):
                    for n in range(NH):
                        i = NH * m + n
                        cut = slice(n * HALF, (n + 1) * HALF)
                        act.wait_ge(pi_ok, FRONT * b + base + i + 1)
                        nc.scalar.activation(dt[:, m, cut], front_ps[(base + i) % 2][:, 0:HALF], ACT.Abs,
                                             bias=dt_b[:, m, :]).then_inc(sp_a, 1)
                for m in range(CH):
                    act.wait_ge(sp_a, CH * (NH + 2) * b + CH * NH + m)
                    nc.scalar.activation(dt[:, m, :], dt[:, m, :], ACT.Exp, scale=-1.0).then_inc(sp_a, 1)
                for m in range(CH):
                    act.wait_ge(sp_a, CH * (NH + 2) * b + CH * NH + CH + m)
                    nc.scalar.activation(dt[:, m, :], dt[:, m, :], ACT.Ln, bias=1.0).then_inc(sp_a, 1)

            with act.Fori(0, B) as b:
                front(b)
                for pair in range(CH // 2):
                    with act.Fori(0, NS // 2) as i:
                        for k in range(2):
                            N = n_of(b, pair, 2 * i + k)
                            act.wait_ge(b_ok, N + 1)
                            act.wait_ge(db_ok, 2 * N + 1)
                            nc.scalar.copy(bs[k][:], ps_b[:]).then_inc(bs_ok, 1)
                            act.wait_ge(bs_ok, N + 1)
                            act.sem_inc(b_free, 1)
                            for c in range(2):
                                m = 2 * pair + c
                                act.wait_ge(dt_ok, CH * b + m + 1)
                                alone(act, acc_ok, 2 * N + c + 1, act_own)
                                nc.scalar.activation(da[2 * k + c][:], dt[:, m, :], ACT.Exp,
                                                     scale=a_neg[:, m, bass.ds(2 * i + k, 1)]).then_inc(da_ok, 1)

        @block.vector
        def _(dve):
            nc.vector.memset(xpad[:, :, 0:TAPS - 1], 0.0)
            dve.wait_ge(w_ok, 1)
            nc.vector.tensor_scalar(a_neg[:], a_neg[:], -1.0, None, ALU.mult).then_inc(w_ok, 1)
            dve.wait_ge(w_ok, 2)
            dve.sem_inc(h_ok, NB)
            dve.sem_inc(hc_ok, 1)
            dve.sem_inc(acc_ok, NB)
            dve.sem_inc(db_ok, 4)
            dve.sem_inc(y_step, 1)

            def front(b):
                dve.wait_ge(stored, 16 * CH * b + 16)
                for k in range(TAPS):
                    for m in range(CH):
                        src = xpad[:, m, k:k + S]
                        if k == 0:
                            dve.wait_ge(pi_free, FRONT * b + NH * (m + 1) + 2)
                            nc.vector.tensor_scalar(conv[:, m, :], src, taps[:, m, 0:1], None, ALU.mult
                                                    ).then_inc(conv_ok, 1)
                        else:
                            dve.wait_ge(conv_ok, CH * TAPS * b + CH * (k - 1) + m + 1)
                            nc.vector.scalar_tensor_tensor(conv[:, m, :], src, taps[:, m, k:k + 1], conv[:, m, :],
                                                           ALU.mult, ALU.add).then_inc(conv_ok, 1)
                dve.wait_ge(bc_ok, NH * b + NH)
                step = 5 * b
                nc.vector.tensor_copy(stack[:], bc[0:BC3, :]).then_inc(bc_step, 1)
                dve.wait_ge(bc_step, step + 1)
                nc.vector.tensor_tensor(bc[0:BC3, :], bc[0:BC3, :], stack[:], ALU.subtract).then_inc(bc_step, 1)
                dve.wait_ge(bc_step, step + 2)
                nc.vector.tensor_copy(bc_mid[:], bc[0:BC3, :]).then_inc(bc_step, 1)
                dve.wait_ge(bc_step, step + 3)
                r = 2 * NS
                nc.vector.tensor_copy(stack[r:2 * r, :], bc_mid[r:2 * r, :]).then_inc(bc_step, 1)
                nc.vector.tensor_tensor(stack[2 * r:3 * r, :], bc[2 * r:3 * r, :], bc_mid[2 * r:3 * r, :], ALU.subtract
                                        ).then_inc(bc_step, 1)
                base = 2 * 2 * CH + NH
                for m in range(CH):
                    for n in range(NH):
                        i = NH * m + n
                        cut = slice(n * HALF, (n + 1) * HALF)
                        dve.wait_ge(sp_a, CH * (NH + 2) * b + i + 1)
                        nc.vector.tensor_scalar(conv[:, m, cut], front_ps[(base + i) % 2][:, 0:HALF], dt_b[:, m, :], 0.0,
                                                ALU.add, ALU.max).then_inc(pi_free, 1)
                for m in range(CH):
                    dve.wait_ge(sp_a, CH * (NH + 2) * b + CH * NH + CH + m + 1)
                    dve.wait_ge(pi_free, FRONT * (b + 1) + 2)
                    nc.vector.tensor_tensor(dt[:, m, :], dt[:, m, :], conv[:, m, :], ALU.add).then_inc(dt_ok, 1)

            def scan(b, pair, n, k):
                N = n_of(b, pair, n)
                for c in range(2):
                    dve.wait_ge(db_ok, 4 + 2 * N + c + 1)
                    dve.wait_ge(da_ok, 2 * N + c + 1)
                    q = 2 * k + c
                    nc.vector.tensor_tensor_scan(da[q][:], da[q][:], db[q][:], 0.0, ALU.mult, ALU.add).then_inc(h_ok, 1)

            def times_c(b, pair, n, k):
                N = n_of(b, pair, n)
                dve.wait_ge(c_ok, N + 1)
                for c in range(2):
                    q = 2 * k + c
                    dve.wait_ge(h_ok, NB + 2 * N + c + 1)
                    nc.vector.tensor_tensor(da[q][:], da[q][:], ps_c[:], ALU.mult).then_inc(hc_ok, 1)

            with dve.Fori(0, B) as b:
                front(b)
                for pair in range(CH // 2):
                    with dve.Fori(0, NS // 2) as i:
                        for k in range(2):
                            scan(b, pair, 2 * i + k, k)
                            times_c(b, pair, 2 * i + k, k)
                    for c in range(2):
                        m = 2 * pair + c
                        dve.wait_ge(acc_ok, NB + 2 * NS * (2 * b + pair + 1))
                        nc.vector.scalar_tensor_tensor(conv[:, m, :], xc[:, m, :], d_p[:, m, :], ps_y[:, c, :],
                                                       ALU.mult, ALU.add).then_inc(y_step, 1)
                        dve.wait_ge(y_step, 2 * (2 * b + pair) + c + 2)
                        nc.vector.tensor_tensor(conv[:, m, :], conv[:, m, :], sz[:, m, :], ALU.mult).then_inc(y_ok, 1)


DF = 1024
DG = 768
MF, MG = DF // P, DG // P
INT_SCALE = 1.0 / 127.0


def tail(nc, ym_in, xc_in, x2_in, w_out_d, w_fc_d, w_pr_d, w_gu_d, w_dn_d, ln2_d, ident_in, out):
    with ExitStack() as ctx:
        sb = lambda name, shape, dt=F32: ctx.enter_context(nc.sbuf_tensor(name, shape, dt))
        sem = lambda name: ctx.enter_context(nc.semaphore(name))
        ident = sb("d_ident", [P, P])
        w_out = sb("d_w_out", [P, CH, D])
        w_fc = sb("d_w_fc", [P, DC, DF])
        w_pr = sb("d_w_pr", [P, MF, D])
        w_gi = sb("d_w_gi", [P, DC, 2 * DG], I32)
        w_di = sb("d_w_di", [P, MG, D], I32)
        w_gu = sb("d_w_gu", [P, DC, 2 * DG])
        w_dn = sb("d_w_dn", [P, MG, D])
        ln_w = sb("d_ln_w", [P, DC])
        mhalf = sb("d_mhalf", [P, G])
        ym = [sb(f"d_ym{i}", [P, CH, GT]) for i in range(2)]
        xc = [sb(f"d_xc{i}", [P, G, D]) for i in range(2)]
        x2 = [sb(f"d_x2{i}", [P, G, D]) for i in range(2)]
        y1 = sb("d_y1", [P, G, D])
        x3 = sb("d_x3", [P, G, D])
        stats = sb("d_stats", [P, G, 6])
        mv = sb("d_mv", [P, G, 2])
        ve = sb("d_ve", [P, G])
        rstd = sb("d_rstd", [P, G])
        xn = sb("d_xn", [P, G, D])
        nT = sb("d_nT", [P, DC, G, P])
        hT = sb("d_hT", [P, MF, GT])
        sg = [sb(f"d_sg{i}", [P, GT]) for i in range(2)]
        o = sb("d_o", [P, G, D])
        ps_t = [ctx.enter_context(nc.psum_tensor(f"d_ps_t{i}", [P, 2, DC, P], F32)) for i in range(2)]
        ps_y = [ctx.enter_context(nc.psum_tensor(f"d_ps_y{i}", [P, 2, D], F32)) for i in range(2)]
        ps_a = [ctx.enter_context(nc.psum_tensor(f"d_ps_a{i}", [P, GT], F32)) for i in range(2)]
        ps_u = [ctx.enter_context(nc.psum_tensor(f"d_ps_u{i}", [P, GT], F32)) for i in range(2)]
        w_in, w_ok, in_s, in_free = sem("d_w_in"), sem("d_w_ok"), sem("d_in"), sem("d_in_free")
        y_ok, y_free = sem("d_y_ok"), sem("d_y_free")
        t_ok, t_free = sem("d_t_ok"), sem("d_t_free")
        a_ok, a_free, u_ok, h_ok = sem("d_a_ok"), sem("d_a_free"), sem("d_u_ok"), sem("d_h_ok")
        step, r_ok, n_ok, s_ok, stored = sem("d_step"), sem("d_r_ok"), sem("d_n_ok"), sem("d_s_ok"), sem("d_stored")
        pool_own, dve_own, sp_own = (sem(f"d_{e}_own") for e in ("pool", "dve", "sp"))
        block = ctx.enter_context(nc.Block())
        NA = MF + MG

        def loop(eng, body):
            with eng.Fori(0, GROUPS // 2) as i:
                for k in range(2):
                    body(2 * i + k, k)

        def rows(x, g):
            return x[bass.ds(g * GT, GT), :].rearrange("(i p) d -> p i d", p=P)

        @block.sync
        def _(sp):
            for dst, src in ((w_out[:], w_out_d.rearrange("(c p) n -> p c n", p=P)),
                             (w_fc[:], w_fc_d.rearrange("(c p) n -> p c n", p=P)),
                             (w_pr[:], w_pr_d.rearrange("(c p) n -> p c n", p=P)),
                             (w_gi[:], w_gu_d.rearrange("(c p) n -> p c n", p=P)),
                             (w_di[:], w_dn_d.rearrange("(c p) n -> p c n", p=P)),
                             (ln_w[:], ln2_d), (ident[:], ident_in)):
                sp.dma_start(dst, src).then_inc(w_in, 16)

            def load(g, k):
                sp.dma_start(ym[k][:], ym_in[:, bass.ds(g * GT, GT)].rearrange("(c p) t -> p c t", p=P)).then_inc(in_s, 16)
                sp.dma_start(xc[k][:], rows(xc_in, g)).then_inc(in_s, 16)
                sp.dma_start(x2[k][:], rows(x2_in, g)).then_inc(in_s, 16)

            load(0, 0)

            def body(g, k):
                alone(sp, in_s, 48 * g + 48, sp_own)
                alone(sp, in_free, g + 1, sp_own)
                load((g + 1) % GROUPS, 1 - k)
                alone(sp, y_free, 6 * g + 6 + 2, sp_own)
                sp.dma_start(rows(out, g), o[:]).then_inc(stored, 16)
            sp.sem_inc(stored, 16)
            loop(sp, body)
            sp.wait_ge(stored, 16 * GROUPS + 16)
            sp.wait_ge(in_s, 48 * GROUPS + 48)

        @block.gpsimd
        def _(pool):
            nc.gpsimd.memset(mhalf[:], -0.5).then_inc(pool_own, 1)
            pool.wait_ge(pool_own, 1)

            def body(g, k):
                alone(pool, step, 6 * g + 3, pool_own)
                nc.gpsimd.tensor_tensor(rstd[:], ve[:], mhalf[:], ALU.pow).then_inc(r_ok, 1)
                alone(pool, n_ok, 2 * g + 1, pool_own)
                nc.gpsimd.tensor_tensor(y1[:], y1[:], x2[k][:], ALU.add).then_inc(s_ok, 1)
                alone(pool, step, 6 * g + 6, pool_own)
                nc.gpsimd.tensor_tensor(rstd[:], ve[:], mhalf[:], ALU.pow).then_inc(r_ok, 1)
            loop(pool, body)

        @block.vector
        def _(dve):
            dve.wait_ge(w_in, 16 * 7)
            nc.vector.tensor_scalar(w_gu[:], w_gi[:], INT_SCALE, None, ALU.mult)
            nc.vector.tensor_scalar(w_dn[:], w_di[:], INT_SCALE, None, ALU.mult).then_inc(w_ok, 1)
            dve.sem_inc(y_free, 2)
            dve.sem_inc(h_ok, 2)
            dve.sem_inc(in_free, 1)

            def body(g, k):
                dve.wait_ge(in_s, 48 * g + 48)
                for j in range(2):
                    dve.wait_ge(y_ok, 6 * g + j + 1)
                    nc.vector.tensor_tensor(y1[:, 2 * j:2 * j + 2, :], ps_y[j][:], xc[k][:, 2 * j:2 * j + 2, :],
                                            ALU.add).then_inc(y_free, 1)
                dve.wait_ge(y_free, 6 * g + 2 + 2)
                norm_stats(nc, dve, y1, stats, mv, ve, step, 6 * g, dve_own)
                dve.wait_ge(r_ok, 2 * g + 1)
                norm_apply(nc, dve, xn, y1, mv, rstd).then_inc(n_ok, 1)
                dve.wait_ge(s_ok, g + 1)
                for j in range(2):
                    dve.wait_ge(y_ok, 6 * g + 2 + j + 1)
                    nc.vector.tensor_tensor(x3[:, 2 * j:2 * j + 2, :], ps_y[j][:], y1[:, 2 * j:2 * j + 2, :],
                                            ALU.add).then_inc(y_free, 1)
                dve.wait_ge(y_free, 6 * g + 4 + 2)
                norm_stats(nc, dve, x3, stats, mv, ve, step, 6 * g + 3, dve_own)
                dve.wait_ge(r_ok, 2 * g + 2)
                norm_apply(nc, dve, xn, x3, mv, rstd).then_inc(n_ok, 1)
                for m in range(MG):
                    dve.wait_ge(a_free, NA * g + MF + m + 1 + 2)
                    dve.wait_ge(u_ok, MG * g + m + 1)
                    nc.vector.tensor_tensor(hT[:, m, :], ps_u[m % 2][:], sg[m % 2][:], ALU.mult).then_inc(h_ok, 1)
                dve.wait_ge(stored, 16 * g + 16)
                for j in range(2):
                    dve.wait_ge(y_ok, 6 * g + 4 + j + 1)
                    nc.vector.tensor_tensor(o[:, 2 * j:2 * j + 2, :], ps_y[j][:], x3[:, 2 * j:2 * j + 2, :],
                                            ALU.add).then_inc(y_free, 1)
                dve.sem_inc(in_free, 1)
            loop(dve, body)

        @block.scalar
        def _(act):
            act.wait_ge(w_in, 16 * 7)
            act.sem_inc(t_free, 2)
            act.sem_inc(a_free, 2)

            def body(g, k):
                for n in range(2):
                    for j in range(2):
                        act.wait_ge(t_ok, 4 * g + 2 * n + j + 1)
                        for c in range(DC):
                            scale = ln_w[:, c:c + 1] if n == 0 else 1.0
                            last = nc.scalar.activation(nT[:, c, 2 * j:2 * j + 2, :], ps_t[j][:, :, c, :], ACT.Copy,
                                                        scale=scale)
                        last.then_inc(t_free, 1)
                    if n == 0:
                        for m in range(MF):
                            act.wait_ge(a_ok, NA * g + m + 1)
                            nc.scalar.activation(hT[:, m, :], ps_a[m % 2][:], ACT.Silu).then_inc(a_free, 1)
                for m in range(MG):
                    act.wait_ge(a_ok, NA * g + MF + m + 1)
                    act.wait_ge(h_ok, MG * g + m + 1)
                    nc.scalar.activation(sg[m % 2][:], ps_a[m % 2][:], ACT.Silu).then_inc(a_free, 1)
            loop(act, body)

        @block.tensor
        def _(pe):
            pe.wait_ge(w_in, 16 * 7)
            pe.wait_ge(w_ok, 1)

            def turn(g, n):
                pe.wait_ge(n_ok, 2 * g + n + 1)
                for j in range(2):
                    pe.wait_ge(t_free, 4 * g + 2 * n + j + 1)
                    for i in range(2):
                        for c in range(DC):
                            last = nc.tensor.transpose(ps_t[j][:, i, c, :], xn[:, 2 * j + i, c * P:(c + 1) * P], ident[:])
                    last.then_inc(t_ok, 1)
                pe.wait_ge(t_free, 4 * g + 2 * n + 2 + 2)

            def rows_out(g, n, lhs, w, count):
                for j in range(2):
                    pe.wait_ge(y_free, 6 * g + 2 * n + j + 1)
                    for i in range(2):
                        for c in range(count):
                            at = (2 * j + i) * P
                            last = nc.tensor.matmul(ps_y[j][:, i, :], lhs[:, c, at:at + P], w[:, c, :],
                                                    start=(c == 0), stop=(c == count - 1))
                    last.then_inc(y_ok, 1)

            def hidden(dst, w, at):
                for c in range(DC):
                    last = nc.tensor.matmul(dst[:], w[:, c, at:at + P], nT[:, c].rearrange("p i t -> p (i t)"),
                                            start=(c == 0), stop=(c == DC - 1))
                return last

            def body(g, k):
                pe.wait_ge(in_s, 48 * g + 48)
                rows_out(g, 0, ym[k], w_out, CH)
                turn(g, 0)
                for m in range(MF):
                    pe.wait_ge(a_free, NA * g + m + 1)
                    hidden(ps_a[m % 2], w_fc, m * P).then_inc(a_ok, 1)
                pe.wait_ge(a_free, NA * g + MF + 2)
                rows_out(g, 1, hT, w_pr, MF)
                turn(g, 1)
                for m in range(MG):
                    pe.wait_ge(a_free, NA * g + MF + m + 1)
                    hidden(ps_a[m % 2], w_gu, m * P).then_inc(a_ok, 1)
                    pe.wait_ge(h_ok, MG * g + m + 1)
                    hidden(ps_u[m % 2], w_gu, DG + m * P).then_inc(u_ok, 1)
                pe.wait_ge(h_ok, MG * g + MG + 2)
                rows_out(g, 2, hT, w_dn, MG)
            loop(pe, body)


def kernel(**inputs):
    import ml_dtypes
    import numpy as np
    import concourse.bacc as bacc
    from concourse.bass_utils import run_bass_kernel_spmd as run

    f = {k: np.asarray(v) for k, v in inputs.items()}
    a = {k[8:]: v for k, v in f.items() if k.startswith("L0_attn_")}
    m = {k[8:]: v for k, v in f.items() if k.startswith("L1_attn_")}
    x_proj = m["x_proj_w"].T
    sel = np.zeros((BC3, 2 * NS, P), dtype=ml_dtypes.bfloat16)
    for n in range(2 * NS):
        sel[n::2 * NS, n] = 1
    arrays = {
        "x": a["hidden_states"].reshape(B * S, D),
        "w_qk": np.concatenate([a["Wq"].T, a["Wk"].T], axis=1),
        "w_vg": np.concatenate([a["Wv"].T, a["gate_W"].T, a["rel_W"][:, :D].T, a["rel_W"][:, D:].T, a["Wo"].T], axis=1),
        "b_qk": np.concatenate([a["bq"], a["bk"]]).reshape(4, P).T,
        "rows": np.concatenate([a["bv"], a["bo"], a["gate_b"], a["rel_b"], a["logical_bias"].T.reshape(-1)]),
        "w_fp8": f["L0_ffn_weight_fp8"].T,
        "scales": np.concatenate([f["L0_ffn_input_scale"], f["L0_ffn_weight_scale"]]),
        "b_fp8": f["L0_ffn_bias"],
        "ln1_w": m["ln1_w"].reshape(DC, P).T,
        "w_in": m["in_proj_w"].T,
        "w_x": np.concatenate([x_proj[:, DTR:]] * 3 + [x_proj[:, :DTR]], axis=1),
        "w_dt": m["dt_proj_w"].T,
        "cols": np.concatenate([m["conv_w"][:, 0], m["conv_b"][:, None], m["dt_proj_b"][:, None], m["Dp"][:, None],
                                m["A_log"]], axis=1),
        "sel": sel.reshape(BC3, -1),
        "w_out": m["out_proj_w"].T,
        "w_fc": m["fc_w"].T,
        "w_pr": m["proj_w"].T,
        "ln2_w": m["ln2_w"].reshape(DC, P).T,
        "w_gu": np.concatenate([f["L1_ffn_w_gate"].T, f["L1_ffn_w_up"].T], axis=1),
        "w_dn": f["L1_ffn_w_down"].T,
        "ident": np.eye(P, dtype=np.float32),
    }
    arrays = {"in_" + k: np.ascontiguousarray(v) for k, v in arrays.items()}
    nc = bacc.Bacc("TRN2", target_bir_lowering=False, num_devices=1)
    d = {k[3:]: nc.dram_tensor(k, v.shape, mybir.dt.from_np(v.dtype), kind="ExternalInput").ap()
         for k, v in arrays.items()}
    out = nc.dram_tensor("out", (B * S, D), F32, kind="ExternalOutput").ap()
    scratch = lambda name, shape, dt=F32: nc.dram_tensor(name + "_d", shape, dt, kind="Internal").ap()
    parts = scratch("parts", (3, 2 * D, B * S), BF16)
    x1, x2, xc = (scratch(n, (B * S, D)) for n in ("x1", "x2", "xc"))
    xl = scratch("xl", (D, B * S))
    ym = scratch("ym", (DI, B * S))
    attention(nc, d["x"], d["w_qk"], d["w_vg"], d["b_qk"], d["rows"], d["ident"], parts, x1)
    fp8_layer(nc, x1, d["w_fp8"], d["scales"], d["ln1_w"], d["b_fp8"], d["ident"], x2, xc, xl)
    mixer(nc, xl, d["w_in"], d["w_x"], d["w_dt"], d["cols"], d["sel"], d["ident"], ym)
    tail(nc, ym, xc, x2, d["w_out"], d["w_fc"], d["w_pr"], d["w_gu"], d["w_dn"], d["ln2_w"], d["ident"], out)
    r = run(nc, [arrays], core_ids=[0])
    return r.results[0]["out"].reshape(B, S, D)
```

```python
import concourse.bass as bass
from concourse import mybir
from concourse.alu_op_type import AluOpType as ALU
from contextlib import ExitStack

ACT = mybir.ActivationFunctionType
F32 = mybir.dt.float32
BF16 = mybir.dt.bfloat16
I32 = mybir.dt.int32
U32 = mybir.dt.uint32
P = 128
BIG = 3.0e38
LN_EPS = 1e-5

B, S, D = 8, 1024, 256
NT = S // P
TILES = B * NT
DC = D // P
H = 16
HD = D // H
HG = 4

Q_PART = [0, 0, 0, 1, 1, 2]
K_PART = [0, 1, 2, 0, 1, 0]
KROWS = HD * len(Q_PART)


def wait(eng, sem, value):
    if isinstance(value, int) and value <= 0:
        return
    eng.wait_ge(sem, value)


def alone(eng, sem, value, own):
    if isinstance(value, int) and value <= 0:
        return
    eng.wait_ge(sem, value)
    eng.sem_inc(own, 1)


def attention(nc, x_in, wqk, wvg, bqk, rows, ident_in, parts_d, x_out):
    AHEAD = NT + 1
    LEAD = 3
    NROW = 8
    NAT = 2 * HG
    with ExitStack() as ctx:
        sb = lambda name, shape, dt=F32: ctx.enter_context(nc.sbuf_tensor(name, shape, dt))
        sem = lambda name: ctx.enter_context(nc.semaphore(name))
        psum = lambda name, shape: ctx.enter_context(nc.psum_tensor(name, shape, F32))

        ident = sb("ident", [P, P])
        w_qk = sb("w_qk", [P, DC, 2 * D])
        w_vg = sb("w_vg", [P, DC, D + H + 6])
        w_o = sb("w_o", [P, DC, D])
        w_dj = sb("w_dj", [P, DC, 2, P])
        b_qk = sb("b_qk", [P, 4])
        row = sb("row", [P, 2 * D + H + 3 + 3 * H])
        b_v, b_o = row[:, 0:D], row[:, D:2 * D]
        b_g = row[:, 2 * D:2 * D + H + 3]
        lbk = row[:, 2 * D + H + 3:2 * D + H + 3 + 3 * H].rearrange("p (k h) -> p k h", k=3)
        b_misc = sb("b_misc", [P, H + 2])
        lbd = sb("lbd", [P, 3, H])
        xt = sb("xt", [P, 2, D])
        stats = sb("stats", [P, 6])
        mv = sb("mv", [P, 2])
        ve = sb("ve", [P, 1])
        mhalf = sb("mhalf", [P, 1])
        rstd = sb("rstd", [P, 1])
        xn = sb("xn", [P, D])
        xnT = sb("xnT", [P, DC, P])
        qkf = sb("qkf", [P, 4, P])
        parts = sb("parts", [P, 3, 4, P], BF16)
        zg = sb("zg", [P, H + 2])
        ge = sb("ge", [P, H])
        gate = sb("gate", [P, H])
        small = sb("small", [P, 2 * NT, 3 * H + 2])
        K6 = sb("K6", [KROWS, H, S], BF16)
        V = [sb(f"V{i}", [P, NT, D + HD]) for i in range(2)]
        Dj = sb("Dj", [P, 2, 2 * S])
        Q6 = [sb(f"Q6_{i}", [KROWS, H, P], BF16) for i in range(2)]
        R = [[sb(f"R{i}_{k}", [P, S]) for k in range(2)] for i in range(2)]
        RT = sb("RT", [P, S])
        R2 = sb("R2", [P, S])
        cur = [sb(f"cur{i}", [P, 3 * H + 2]) for i in range(2)]
        rows_sb = [sb(f"srow{i}", [P, S]) for i in range(NROW)]
        nmax = sb("nmax", [P, NROW])
        rsum = sb("rsum", [P, 2, H])
        AT = [sb(f"AT{i}", [P, NT, P]) for i in range(NAT)]
        O4 = sb("O4", [P, HG, P])
        rinv = sb("rinv", [P, H])
        attn = sb("attn", [P, D])
        attnT = sb("attnT", [P, DC, P])
        xr = sb("xr", [P, D])

        ps_s = psum("ps_s", [P, 2, S])
        ps_t = psum("ps_t", [P, 2, HG, P])
        ps_o = psum("ps_o", [P, HG, P])
        ps_m = psum("ps_m", [P, 4 * P])

        w_in = sem("w_in")
        w_ready = sem("w_ready")
        w_step = sem("w_step")
        x_in_s = sem("x_in_s")
        x_free = sem("x_free")
        ln_step = sem("ln_step")
        rstd_ok = sem("rstd_ok")
        pm = sem("pm")
        pm_free = sem("pm_free")
        om = sem("om")
        om_free = sem("om_free")
        hi_ok = sem("hi_ok")
        rem_ok = sem("rem_ok")
        mid_ok = sem("mid_ok")
        lo_ok = sem("lo_ok")
        parts_w = sem("parts_w")
        k6_in = sem("k6_in")
        q6_in = sem("q6_in")
        zg_ok = sem("zg_ok")
        ge_ok = sem("ge_ok")
        g_step = sem("g_step")
        v_ok = sem("v_ok")
        cur_ok = sem("cur_ok")
        rel_step = sem("rel_step")
        rel_exp = sem("rel_exp")
        rel_sum = sem("rel_sum")
        rel_y0 = sem("rel_y0")
        rel_t = sem("rel_t")
        rel_y = sem("rel_y")
        p_ok = sem("p_ok")
        u_ok = sem("u_ok")
        w_ok = sem("w_ok")
        qk_ok = sem("qk_ok")
        s_ok = sem("s_ok")
        e_ok = sem("e_ok")
        t_ok = sem("t_ok")
        at_ok = sem("at_ok")
        pv_ok = sem("pv_ok")
        o_ok = sem("o_ok")
        rinv_ok = sem("rinv_ok")
        xr_in = sem("xr_in")
        xrb_ok = sem("xrb_ok")
        st = sem("st")
        pool_own, dve_own, sp_own = sem("pool_own"), sem("dve_own"), sem("sp_own")

        def pool_rstd(pool, p):
            alone(pool, ln_step, 3 * p + 3, pool_own)
            nc.gpsimd.tensor_tensor(rstd[:], ve[:], mhalf[:], ALU.pow).then_inc(rstd_ok, 1)

        def pool_rem(pool, p):
            alone(pool, hi_ok, p + 1, pool_own)
            nc.gpsimd.tensor_tensor(qkf[:], qkf[:], parts[:, 0], ALU.subtract).then_inc(rem_ok, 1)

        def pool_lo(pool, p):
            alone(pool, mid_ok, p + 1, pool_own)
            nc.gpsimd.tensor_tensor(parts[:, 2], qkf[:], parts[:, 1], ALU.subtract).then_inc(lo_ok, 1)

        def pool_sum(pool, t, k, n):
            if n == 0:
                alone(pool, rel_exp, 3 * t + 3, pool_own)
                nc.gpsimd.tensor_tensor(RT[:], R[k][0][:], R[k][1][:], ALU.add).then_inc(rel_sum, 1)
            else:
                alone(pool, rel_sum, 2 * t + 1, pool_own)
                nc.gpsimd.tensor_tensor(RT[:], RT[:], R2[:], ALU.add).then_inc(rel_sum, 1)

        def pool_t(pool, t):
            alone(pool, rel_y0, 2 * t + 2, pool_own)
            nc.gpsimd.tensor_tensor(RT[:], RT[:], R2[:], ALU.mult).then_inc(rel_t, 1)

        def pool_p(pool, t, k, n):
            if n == 0:
                alone(pool, rel_y, t + 1, pool_own)
            nc.gpsimd.tensor_tensor(R[k][n][:], R[k][n][:], R2[:], ALU.mult).then_inc(p_ok, 1)

        def pool_u(pool, t, k, h):
            U = H * t + h
            if h == 0:
                alone(pool, p_ok, 2 * t + 2, pool_own)
            alone(pool, t_ok, 2 * U + 2, pool_own)
            nc.gpsimd.tensor_scalar(rows_sb[h % NROW][:], R[k][0][:], cur[k][:, h:h + 1],
                                    cur[k][:, 2 * H + h:2 * H + h + 1], ALU.mult, ALU.add).then_inc(u_ok, 1)

        def pool_xrb(pool, o):
            alone(pool, xr_in, 16 * o + 16, pool_own)
            nc.gpsimd.tensor_tensor(xr[:], xr[:], b_o, ALU.add).then_inc(xrb_ok, 1)

        def dve_ln(dve, p, k):
            wait(dve, x_in_s, 16 * p + 16)
            nc.vector.bn_stats(stats[:], xt[:, k, :]).then_inc(ln_step, 1)
            alone(dve, ln_step, 3 * p + 1, dve_own)
            nc.vector.bn_aggr(mv[:], stats[:]).then_inc(ln_step, 1)
            dve.wait_ge(ln_step, 3 * p + 2)
            nc.vector.tensor_scalar(ve[:], mv[:, 1:2], LN_EPS, None, ALU.add).then_inc(ln_step, 1)

        def dve_xn(dve, p, k):
            wait(dve, rstd_ok, p + 1)
            nc.vector.tensor_scalar(xn[:], xt[:, k, :], mv[:, 0:1], rstd[:, 0:1],
                                    ALU.subtract, ALU.mult).then_inc(x_free, 1)

        def dve_qk(dve, p):
            wait(dve, pm, 4 * p + 2)
            nc.vector.tensor_tensor(qkf[:], ps_m[:].rearrange("p (m t) -> p m t", m=4),
                                    b_qk[:].unsqueeze(2).broadcast_to([P, 4, P]), ALU.add).then_inc(pm_free, 1)

        def dve_d(dve, p):
            wait(dve, pm, 4 * p + 3)
            nc.vector.tensor_scalar(Dj[:, :, bass.ds((p % (2 * NT)) * P, P)],
                                    ps_m[:, 0:2 * P].rearrange("p (k t) -> p k t", k=2),
                                    1.0, None, ALU.mult).then_inc(pm_free, 1)

        def dve_v(dve, p, par, ib):
            wait(dve, pm, 4 * p + 4)
            nc.vector.tensor_tensor(V[par][:, bass.ds(ib, 1), 0:D], ps_m[:, 0:D].unsqueeze(1),
                                    b_v.unsqueeze(1), ALU.add).then_inc(v_ok, 1)
            nc.vector.tensor_tensor(zg[:], ps_m[:, D:D + H + 2], b_misc[:], ALU.add).then_inc(pm_free, 1)

        def dve_gate(dve, p, par, ib):
            wait(dve, ge_ok, p + 1)
            nc.vector.tensor_scalar(ge[:], ge[:], 1.0, None, ALU.add).then_inc(g_step, 1)
            dve.wait_ge(g_step, 4 * p + 1)
            nc.vector.reciprocal(gate[:], ge[:]).then_inc(g_step, 1)
            dve.wait_ge(g_step, 4 * p + 2)
            idx = par * NT + ib
            nc.vector.tensor_tensor(small[:, bass.ds(idx, 1), 0:3 * H].rearrange("p o (k h) -> p (o k) h", k=3),
                                    lbd[:], gate[:].unsqueeze(1).broadcast_to([P, 3, H]), ALU.mult).then_inc(g_step, 1)
            nc.vector.tensor_scalar(small[:, bass.ds(idx, 1), 3 * H:3 * H + 2], zg[:, H:H + 2].unsqueeze(1),
                                    1.0, None, ALU.mult).then_inc(g_step, 1)

        def dve_rel(dve, t, k, step):
            d10, d20 = (Dj[:, i:i + 1, bass.ds(((t // NT) % 2) * S, S)].rearrange("p a s -> p (a s)") for i in range(2))
            a10, a20 = (cur[k][:, 3 * H + i:3 * H + i + 1] for i in range(2))
            if step == 0:
                wait(dve, g_step, 4 * (t + 1))
                wait(dve, u_ok, H * (t - 1))
                nc.vector.tensor_scalar(cur[k][:].unsqueeze(1), small[:, bass.ds(t % (2 * NT), 1), :],
                                        1.0, None, ALU.mult).then_inc(cur_ok, 1)
                dve.wait_ge(cur_ok, t + 1)
                wait(dve, pm_free, 4 * (NT * (t // NT) + NT) - 1)
                wait(dve, p_ok, 2 * t)
                nc.vector.tensor_scalar(RT[:], d10, a10, 0.0, ALU.add, ALU.max).then_inc(rel_step, 1)
            elif step == 1:
                dve.wait_ge(rel_step, 4 * t + 1)
                nc.vector.scalar_tensor_tensor(RT[:], d20, a20, RT[:], ALU.add, ALU.max).then_inc(rel_step, 1)
            elif step == 2:
                dve.wait_ge(rel_step, 4 * t + 2)
                nc.vector.scalar_tensor_tensor(R[k][1][:], d10, a10, RT[:], ALU.add, ALU.subtract).then_inc(rel_step, 1)
            else:
                nc.vector.scalar_tensor_tensor(R2[:], d20, a20, RT[:], ALU.add, ALU.subtract).then_inc(rel_step, 1)

        def dve_y(dve, t):
            wait(dve, rel_t, t + 1)
            nc.vector.scalar_tensor_tensor(R2[:], RT[:], 2.0, R2[:], ALU.subtract, ALU.mult).then_inc(rel_y, 1)

        def dve_w(dve, t, k, h):
            wait(dve, u_ok, H * t + h + 1)
            r = rows_sb[h % NROW]
            nc.vector.scalar_tensor_tensor(r[:], R[k][1][:], cur[k][:, H + h:H + h + 1], r[:],
                                           ALU.mult, ALU.add).then_inc(w_ok, 1)

        def dve_s(dve, t, h):
            wait(dve, w_ok, H * t + h + 1)
            alone(dve, qk_ok, H * t + h + 1, dve_own)
            r = rows_sb[h % NROW]
            nc.vector.tensor_tensor_reduce(r[:], r[:], ps_s[:, h % 2, :], -1.0, BIG, ALU.add, ALU.min,
                                           nmax[:, h % NROW:h % NROW + 1]).then_inc(s_ok, 1)

        def dve_norm(dve, o, k):
            wait(dve, e_ok, H * (o + 1))
            nc.vector.reciprocal(rinv[:], rsum[:, k, :]).then_inc(rinv_ok, 1)
            dve.wait_ge(rinv_ok, o + 1)
            wait(dve, om, 3 * o + 1)
            nc.vector.tensor_tensor(attn[:].rearrange("p (h d) -> p h d", d=HD),
                                    ps_m[:].rearrange("p (h e) -> p h e", e=32)[:, :, 0:HD],
                                    rinv[:].unsqueeze(2).broadcast_to([P, H, HD]), ALU.mult).then_inc(om_free, 1)

        def dve_out(dve, o):
            wait(dve, xrb_ok, o + 1)
            wait(dve, om, 3 * o + 3)
            nc.vector.tensor_tensor(xr[:], ps_m[:, 0:D], xr[:], ALU.add).then_inc(om_free, 1)

        def act_xT(act, p):
            wait(act, pm, 4 * p + 1)
            nc.scalar.copy(xnT[:].rearrange("p c t -> p (c t)"), ps_m[:, 0:D]).then_inc(pm_free, 1)

        def act_hi(act, p):
            wait(act, parts_w, 16 * p + 16)
            wait(act, pm_free, 4 * p + 2 + 1)
            nc.scalar.copy(parts[:, 0], qkf[:]).then_inc(hi_ok, 1)

        def act_mid(act, p):
            wait(act, rem_ok, p + 1)
            nc.scalar.copy(parts[:, 1], qkf[:]).then_inc(mid_ok, 1)

        def act_gate(act, p):
            wait(act, pm_free, 4 * p + 4 + 1)
            nc.scalar.activation(ge[:], zg[:, 0:H], ACT.Exp, scale=-1.0).then_inc(ge_ok, 1)

        def act_rel(act, t, k, step):
            wait(act, rel_step, 4 * t + 2 + step)
            src, dst = ((RT, R[k][0]), (R[k][1], R[k][1]), (R2, R2))[step]
            nc.scalar.activation(dst[:], src[:], ACT.Exp, scale=-1.0 if step == 0 else 1.0).then_inc(rel_exp, 1)

        def act_y0(act, t, step):
            if step == 0:
                wait(act, rel_sum, 2 * t + 2)
                nc.scalar.activation(R2[:], RT[:], ACT.Ln).then_inc(rel_y0, 1)
            else:
                act.wait_ge(rel_y0, 2 * t + 1)
                nc.scalar.activation(R2[:], R2[:], ACT.Exp, scale=-1.0).then_inc(rel_y0, 1)

        def act_e(act, t, k, h):
            wait(act, s_ok, H * t + h + 1)
            r = rows_sb[h % NROW]
            nc.scalar.activation(r[:], r[:], ACT.Exp, scale=-1.0, bias=nmax[:, h % NROW:h % NROW + 1],
                                 accum_out=rsum[:, k, h:h + 1]).then_inc(e_ok, 1)

        def act_at(act, t, h):
            U = H * t + h
            if h % HG == 0:
                wait(act, pv_ok, U // HG + 1 if isinstance(U, int) else HG * t + h // HG + 1)
            for half in range(2):
                wait(act, t_ok, 2 * NROW + 2 * U + half + 1)
                nc.scalar.copy(AT[h % NAT][:, HG * half:HG * half + HG, :], ps_t[:, half]).then_inc(at_ok, 1)

        def act_o(act, o):
            wait(act, pv_ok, 2 + HG * (o + 1))
            nc.scalar.copy(O4[:], ps_o[:]).then_inc(o_ok, 1)

        def act_aT(act, o):
            wait(act, om, 3 * o + 2)
            nc.scalar.copy(attnT[:].rearrange("p c t -> p (c t)"), ps_m[:, 0:D]).then_inc(om_free, 1)

        def pe_m(pe, p, i, o_done):
            wait(pe, pm_free, 4 * p + i + 1)
            wait(pe, om_free, o_done + 1)

        def pe_xT(pe, p, o_done):
            wait(pe, x_free, p + 1 + 2)
            pe_m(pe, p, 0, o_done)
            for c in range(DC):
                last = nc.tensor.transpose(ps_m[:, c * P:(c + 1) * P], xn[:, c * P:(c + 1) * P], ident[:])
            last.then_inc(pm, 1)

        def pe_qk_proj(pe, p, o_done):
            pe_m(pe, p, 1, o_done)
            for m in range(4):
                for c in range(DC):
                    last = nc.tensor.matmul(ps_m[:, m * P:(m + 1) * P], w_qk[:, c, m * P:(m + 1) * P],
                                            xnT[:, c, :], start=(c == 0), stop=(c == DC - 1))
            last.then_inc(pm, 1)

        def pe_d(pe, p, o_done):
            pe_m(pe, p, 2, o_done)
            for i in range(2):
                for c in range(DC):
                    last = nc.tensor.matmul(ps_m[:, i * P:(i + 1) * P], w_dj[:, c, i, :],
                                            xnT[:, c, :], start=(c == 0), stop=(c == DC - 1))
            last.then_inc(pm, 1)

        def pe_v(pe, p, o_done):
            pe_m(pe, p, 3, o_done)
            for c in range(DC):
                last = nc.tensor.matmul(ps_m[:, 0:D + H + 2], xnT[:, c, :], w_vg[:, c, 0:D + H + 2],
                                        start=(c == 0), stop=(c == DC - 1))
            last.then_inc(pm, 1)

        def pe_s(pe, t, k, h):
            U = H * t + h
            if h == 0:
                wait(pe, q6_in, 96 * (t + 1))
            if h % HG == 0:
                wait(pe, k6_in, 96 * (HG * (t // NT) + h // HG + 1))
            wait(pe, s_ok, U - 1)
            for n in range(2):
                last = nc.tensor.matmul(ps_s[:, h % 2, n * 512:(n + 1) * 512], Q6[k][:, h, :],
                                        K6[:, h, n * 512:(n + 1) * 512], start=True, stop=True)
            last.then_inc(qk_ok, 1)

        def pe_t(pe, t, h):
            U = H * t + h
            wait(pe, e_ok, U + 1)
            for half in range(2):
                wait(pe, at_ok, 2 * U + half + 1)
                for i in range(HG):
                    j = HG * half + i
                    last = nc.tensor.transpose(ps_t[:, half, i, :], rows_sb[h % NROW][:, j * P:(j + 1) * P], ident[:])
                last.then_inc(t_ok, 1)

        def pe_pv(pe, t, par, j):
            if j == 0:
                wait(pe, o_ok, t)
                wait(pe, v_ok, 2 + NT * (t // NT + 1))
            wait(pe, at_ok, 2 + 2 * (H * t + HG * j + HG))
            for n in range(NT):
                for i in range(HG):
                    h = HG * j + i
                    last = nc.tensor.matmul(ps_o[32 * i:32 * i + 32, j, :], V[par][:, n, HD * h:HD * h + 32],
                                            AT[h % NAT][:, n, :], start=(n == 0), stop=(n == NT - 1))
            last.then_inc(pv_ok, 1)

        def pe_oT(pe, o, p_done):
            wait(pe, o_ok, o + 1)
            wait(pe, pm_free, p_done + 1)
            wait(pe, om_free, 3 * o + 1)
            for j in range(HG):
                last = nc.tensor.transpose(ps_m[:, j * P:(j + 1) * P], O4[:, j, :], ident[:])
            last.then_inc(om, 1)

        def pe_aT(pe, o, p_done):
            wait(pe, pm_free, p_done + 1)
            wait(pe, om_free, 3 * o + 2)
            for c in range(DC):
                last = nc.tensor.transpose(ps_m[:, c * P:(c + 1) * P], attn[:, c * P:(c + 1) * P], ident[:])
            last.then_inc(om, 1)

        def pe_wo(pe, o, p_done):
            wait(pe, pm_free, p_done + 1)
            wait(pe, om_free, 3 * o + 3)
            for c in range(DC):
                last = nc.tensor.matmul(ps_m[:, 0:D], attnT[:, c, :], w_o[:, c, :],
                                        start=(c == 0), stop=(c == DC - 1))
            last.then_inc(om, 1)

        parts_v = parts_d.rearrange("k (m p) t -> p k m t", p=P)

        def sp_x(sp, p, k):
            alone(sp, x_free, p + 1, sp_own)
            sp.dma_start(xt[:, k, :], x_in[bass.ds((p % TILES) * P, P), :]).then_inc(x_in_s, 16)

        def sp_parts(sp, p):
            alone(sp, parts_w, 16 * p + 16, sp_own)
            alone(sp, lo_ok, p + 1, sp_own)
            sp.dma_start(parts_v[:, :, :, bass.ds((p % TILES) * P, P)], parts[:]).then_inc(parts_w, 16)

        def sp_keys(sp, b):
            alone(sp, parts_w, 16 * NT * (b + 1) + 16, sp_own)
            for g in range(HG):
                alone(sp, k6_in, 96 * (HG * b + g), sp_own)
                alone(sp, qk_ok, H * (NT * b - 1) + HG * g + HG, sp_own)
                for s, part in enumerate(K_PART):
                    sp.dma_start(K6[HD * s:HD * s + HD, HG * g:HG * g + HG, :],
                                 parts_d[part, D + g * HG * HD:D + (g + 1) * HG * HD, bass.ds(b * S, S)
                                         ].rearrange("(h d) t -> d h t", d=HD)).then_inc(k6_in, 16)

        def sp_q6(sp, t, k):
            alone(sp, q6_in, 96 * t, sp_own)
            alone(sp, qk_ok, H * (t - 1), sp_own)
            for s, part in enumerate(Q_PART):
                sp.dma_start(Q6[k][HD * s:HD * s + HD, :, :],
                             parts_d[part, 0:D, bass.ds(t * P, P)].rearrange("(h d) t -> d h t", d=HD)
                             ).then_inc(q6_in, 16)

        def sp_xr(sp, o):
            alone(sp, st, 16 * o, sp_own)
            sp.dma_start(xr[:], x_in[bass.ds(o * P, P), :]).then_inc(xr_in, 16)

        def sp_out(sp, o):
            alone(sp, om_free, 3 * o + 4, sp_own)
            sp.dma_start(x_out[bass.ds(o * P, P), :], xr[:]).then_inc(st, 16)

        def run(eng, start, project, body, finish, keys=None):
            keys = keys or (lambda eng, b: None)
            with eng.Fori(0, NT // 2) as i:
                for k in range(2):
                    project(eng, 2 * i + k, k, 0, 2 * i + k)
            start(eng)
            for k in range(2):
                body(eng, k, k, 0, k, True, k > 0, True)
            with eng.Fori(1, NT // 2) as i:
                for k in range(2):
                    body(eng, 2 * i + k, k, 0, 2 * i + k, True, True, True)
            keys(eng, 1)
            with eng.Fori(0, (B - 2) // 2) as j:
                for par in (1, 0):
                    first = (2 * j + (1 if par else 2)) * NT
                    with eng.Fori(0, NT // 2) as i:
                        for k in range(2):
                            body(eng, first + 2 * i + k, k, par, 2 * i + k, True, True, True)
                    keys(eng, 2 * j + (2 if par else 3))
            with eng.Fori(0, NT // 2 - 1) as i:
                for k in range(2):
                    body(eng, (B - 1) * NT + 2 * i + k, k, 1, 2 * i + k, False, True, True)
            for k in range(2):
                body(eng, TILES - 2 + k, k, 1, NT - 2 + k, False, True, k == 0)
            finish(eng)

        block = ctx.enter_context(nc.Block())

        @block.sync
        def _(sp):
            def project(sp, p, k, par, ib):
                sp_x(sp, p, k)
                sp_parts(sp, p)

            def start(sp):
                sp_x(sp, NT, 0)
                sp_keys(sp, 0)
                sp_q6(sp, 0, 0)
                sp_parts(sp, NT)

            def body(sp, t, k, par, ib, pro, post, look):
                if pro:
                    sp_x(sp, t + AHEAD, 1 - k)
                if look:
                    sp_q6(sp, t + 1, 1 - k)
                if not isinstance(t, int) or t >= 2:
                    sp_out(sp, t - 2)
                if post:
                    sp_xr(sp, t - 1)
                if pro:
                    sp_parts(sp, t + AHEAD)

            def finish(sp):
                sp_out(sp, TILES - 2)
                sp_xr(sp, TILES - 1)
                sp_out(sp, TILES - 1)
                sp.wait_ge(st, 16 * TILES)

            for dst, src in ((w_qk[:], wqk.rearrange("(c p) n -> p c n", p=P)),
                             (w_vg[:], wvg[:, 0:D + H + 6].rearrange("(c p) n -> p c n", p=P)),
                             (w_o[:], wvg[:, D + H + 6:].rearrange("(c p) n -> p c n", p=P)),
                             (b_qk[:], bqk), (row[:], rows.partition_broadcast(P)), (ident[:], ident_in)):
                sp.dma_start(dst, src).then_inc(w_in, 16)
            sp.sem_inc(parts_w, 16)
            run(sp, start, project, body, finish, sp_keys)

        @block.gpsimd
        def _(pool):
            def project(pool, p, k, par, ib):
                pool_rstd(pool, p)
                pool_rem(pool, p)
                pool_lo(pool, p)

            def start(pool):
                project(pool, NT, 0, 1, 0)
                pool_sum(pool, 0, 0, 0)
                pool_sum(pool, 0, 0, 1)
                pool_t(pool, 0)
                pool_p(pool, 0, 0, 0)
                pool_p(pool, 0, 0, 1)
                for h in range(LEAD):
                    pool_u(pool, 0, 0, h)

            def body(pool, t, k, par, ib, pro, post, look):
                for u in range(H):
                    if u + LEAD < H:
                        pool_u(pool, t, k, u + LEAD)
                    elif look:
                        pool_u(pool, t + 1, 1 - k, u + LEAD - H)
                    if pro and u == 2:
                        pool_rstd(pool, t + AHEAD)
                    if look and u in (5, 6):
                        pool_sum(pool, t + 1, 1 - k, u - 5)
                    if look and u == 9:
                        pool_t(pool, t + 1)
                    if pro and u == 10:
                        pool_rem(pool, t + AHEAD)
                    if look and u in (11, 12):
                        pool_p(pool, t + 1, 1 - k, u - 11)
                    if pro and u == 12:
                        pool_lo(pool, t + AHEAD)
                    if post and u == 14:
                        pool_xrb(pool, t - 1)

            def finish(pool):
                pool_xrb(pool, TILES - 1)

            nc.gpsimd.memset(mhalf[:], -0.5)
            for v in V:
                nc.gpsimd.memset(v[:, :, D:D + HD], 0.0).then_inc(v_ok, 1)
            pool.wait_ge(v_ok, 2)
            run(pool, start, project, body, finish)

        @block.vector
        def _(dve):
            def front(dve, p, k):
                dve_ln(dve, p, k)
                dve_xn(dve, p, k)
                dve_qk(dve, p)
                dve_d(dve, p)

            def project(dve, p, k, par, ib):
                front(dve, p, k)
                dve_v(dve, p, par, ib)
                dve_gate(dve, p, par, ib)

            def start(dve):
                front(dve, NT, 0)
                for step in range(4):
                    dve_rel(dve, 0, 0, step)
                dve_y(dve, 0)
                dve_w(dve, 0, 0, 0)

            def body(dve, t, k, par, ib, pro, post, look):
                for u in range(H):
                    if u + 1 < H:
                        dve_w(dve, t, k, u + 1)
                    elif look:
                        dve_w(dve, t + 1, 1 - k, 0)
                    dve_s(dve, t, u)
                    if u == 0 and (not isinstance(t, int) or t >= 2):
                        dve_out(dve, t - 2)
                    if look and u < 4:
                        dve_rel(dve, t + 1, 1 - k, u)
                    if pro and u == 1:
                        dve_ln(dve, t + AHEAD, 1 - k)
                    if pro and u == 3:
                        dve_v(dve, t + NT, 1 - par, ib)
                    if pro and u == 4:
                        dve_xn(dve, t + AHEAD, 1 - k)
                    if post and u == 5:
                        dve_norm(dve, t - 1, 1 - k)
                    if pro and u == 7:
                        dve_gate(dve, t + NT, 1 - par, ib)
                    if pro and u == 9:
                        dve_qk(dve, t + AHEAD)
                    if pro and u == 11:
                        dve_d(dve, t + AHEAD)
                    if look and u == 12:
                        dve_y(dve, t + 1)

            def finish(dve):
                dve_out(dve, TILES - 2)
                dve_norm(dve, TILES - 1, 1)
                dve_out(dve, TILES - 1)

            dve.wait_ge(w_in, 16 * 6)
            nc.vector.tensor_scalar(w_qk[:, :, 0:D], w_qk[:, :, 0:D], 1.0 / HD ** 0.5, None, ALU.mult)
            nc.vector.tensor_scalar(b_qk[:, 0:DC], b_qk[:, 0:DC], 1.0 / HD ** 0.5, None, ALU.mult)
            ri, rj = D + H, D + H + 3
            for i in range(2):
                nc.vector.tensor_tensor(w_dj[:, :, i, :], w_vg[:, :, rj + 1 + i:rj + 2 + i].broadcast_to([P, DC, P]),
                                        w_vg[:, :, rj:rj + 1].broadcast_to([P, DC, P]), ALU.subtract)
                nc.vector.tensor_tensor(b_misc[:, H + i:H + i + 1], b_g[:, H + 1 + i:H + 2 + i], b_g[:, H:H + 1],
                                        ALU.subtract)
                nc.vector.tensor_tensor(lbd[:, i, :], lbk[:, 2, :], lbk[:, i, :], ALU.subtract)
            nc.vector.tensor_copy(b_misc[:, 0:H], b_g[:, 0:H])
            nc.vector.tensor_copy(lbd[:, 2, :], lbk[:, 2, :]).then_inc(w_step, 1)
            dve.wait_ge(w_step, 1)
            nc.vector.tensor_tensor(rinv[:, 0:DC], w_vg[:, :, ri + 1], w_vg[:, :, ri], ALU.subtract)
            nc.vector.tensor_tensor(rinv[:, DC:2 * DC], w_vg[:, :, ri + 2], w_vg[:, :, ri], ALU.subtract
                                    ).then_inc(w_step, 1)
            dve.wait_ge(w_step, 2)
            nc.vector.tensor_copy(w_vg[:, :, ri], rinv[:, 0:DC])
            nc.vector.tensor_copy(w_vg[:, :, ri + 1], rinv[:, DC:2 * DC]).then_inc(w_ready, 1)
            dve.wait_ge(w_ready, 1)
            dve.sem_inc(x_free, 2)
            dve.sem_inc(pm_free, 1)
            dve.sem_inc(om_free, 1)
            run(dve, start, project, body, finish)

        @block.scalar
        def _(act):
            def front(act, p):
                act_xT(act, p)
                act_hi(act, p)
                act_mid(act, p)

            def project(act, p, k, par, ib):
                front(act, p)
                act_gate(act, p)

            def start(act):
                front(act, NT)
                for step in range(3):
                    act_rel(act, 0, 0, step)
                act_y0(act, 0, 0)
                act_y0(act, 0, 1)

            def body(act, t, k, par, ib, pro, post, look):
                for u in range(H):
                    act_e(act, t, k, u)
                    if u:
                        act_at(act, t, u - 1)
                    if post and u == 1:
                        act_o(act, t - 1)
                    if look and u in (2, 3, 4):
                        act_rel(act, t + 1, 1 - k, u - 2)
                    if pro and u == 5:
                        act_gate(act, t + NT)
                    if pro and u == 6:
                        act_xT(act, t + AHEAD)
                    if look and u in (8, 9):
                        act_y0(act, t + 1, u - 8)
                    if pro and u == 9:
                        act_hi(act, t + AHEAD)
                    if pro and u == 11:
                        act_mid(act, t + AHEAD)
                    if post and u == 12:
                        act_aT(act, t - 1)
                act_at(act, t, H - 1)

            def finish(act):
                act_o(act, TILES - 1)
                act_aT(act, TILES - 1)

            act.preload_act_table_set("natural_log_exp_and_others")
            act.sem_inc(at_ok, 2)
            run(act, start, project, body, finish)

        @block.tensor
        def _(pe):
            def front(pe, p):
                pe_xT(pe, p, 0)
                pe_qk_proj(pe, p, 0)
                pe_d(pe, p, 0)

            def project(pe, p, k, par, ib):
                front(pe, p)
                pe_v(pe, p, 0)

            def start(pe):
                front(pe, NT)
                for h in range(3):
                    pe_s(pe, 0, 0, h)

            def body(pe, t, k, par, ib, pro, post, look):
                o = t - 1
                p = t + AHEAD
                om_done = 3 * o if post else 0
                om_next = om_done + 1 if post else 0
                last_p = 4 * TILES + 3
                for u in range(H):
                    if u and u + 2 < H:
                        pe_s(pe, t, k, u + 2)
                    elif u and look:
                        pe_s(pe, t + 1, 1 - k, u + 2 - H)
                    pe_t(pe, t, u)
                    if u and u % HG == 0:
                        pe_pv(pe, t, par, u // HG - 1)
                    if pro and u == 1:
                        pe_v(pe, p - 1, om_done)
                    if post and u == 3:
                        pe_oT(pe, o, 4 * p if pro else last_p)
                    if pro and u == 5:
                        pe_xT(pe, p, om_next)
                    if pro and u == 7:
                        pe_qk_proj(pe, p, om_next)
                    if pro and u == 9:
                        pe_d(pe, p, om_next)
                    if post and u == 11:
                        pe_aT(pe, o, 4 * p + 3 if pro else last_p)
                    if post and u == 13:
                        pe_wo(pe, o, 4 * p + 3 if pro else last_p)
                if look:
                    pe_s(pe, t + 1, 1 - k, 2)
                pe_pv(pe, t, par, HG - 1)

            def finish(pe):
                pe_oT(pe, TILES - 1, 4 * TILES + 3)
                pe_aT(pe, TILES - 1, 4 * TILES + 3)
                pe_wo(pe, TILES - 1, 4 * TILES + 3)

            pe.wait_ge(w_ready, 1)
            pe.sem_inc(t_ok, 2 * NROW)
            pe.sem_inc(pv_ok, 2)
            run(pe, start, project, body, finish)


G = 4
GROUPS = TILES // G
GT = G * P


def norm_stats(nc, dve, x, stats, mv, ve, step, base, own):
    for i in range(G):
        last = nc.vector.bn_stats(stats[:, i, :], x[:, i, :])
    last.then_inc(step, 1)
    alone(dve, step, base + 1, own)
    for i in range(G):
        last = nc.vector.bn_aggr(mv[:, i, :], stats[:, i, :])
    last.then_inc(step, 1)
    dve.wait_ge(step, base + 2)
    nc.vector.tensor_scalar(ve[:].unsqueeze(2), mv[:, :, 1:2], LN_EPS, None, ALU.add).then_inc(step, 1)


def norm_apply(nc, dve, out, x, mv, rstd):
    for i in range(G):
        last = nc.vector.tensor_scalar(out[:, i, :], x[:, i, :], mv[:, i, 0:1], rstd[:, i:i + 1],
                                               ALU.subtract, ALU.mult)
    return last


def fp8_layer(nc, x_in, w8, scales, col, bias, ident_in, x_out, xc_out, xl_out):
    with ExitStack() as ctx:
        sb = lambda name, shape, dt=F32: ctx.enter_context(nc.sbuf_tensor(name, shape, dt))
        sem = lambda name: ctx.enter_context(nc.semaphore(name))
        ident = sb("b_ident", [P, P])
        w = sb("b_w", [P, DC, D])
        sc = sb("b_sc", [P, 2])
        rs = sb("b_rs", [P, 1])
        ln_w = sb("b_ln_w", [P, DC])
        b_row = sb("b_row", [P, 1, D])
        mhalf = sb("b_mhalf", [P, G])
        xt = [sb(f"b_xt{i}", [P, G, D]) for i in range(2)]
        xb = sb("b_xb", [P, G, D])
        stats = sb("b_stats", [P, G, 6])
        mv = sb("b_mv", [P, G, 2])
        ve = sb("b_ve", [P, G])
        rstd = sb("b_rstd", [P, G])
        xn = sb("b_xn", [P, G, D])
        mag = sb("b_mag", [P, G, D])
        xq = sb("b_xq", [P, G, D])
        xT = sb("b_xT", [P, G // 2, 2, DC, P])
        x2 = sb("b_x2", [P, G, D])
        xc = sb("b_xc", [P, G, D])
        x3 = sb("b_x3", [P, G, D])
        xl = sb("b_xl", [P, DC, G, P])
        ps_t = [ctx.enter_context(nc.psum_tensor(f"b_ps_t{i}", [P, 2, DC, P], F32)) for i in range(2)]
        ps_y = [ctx.enter_context(nc.psum_tensor(f"b_ps_y{i}", [P, 2, D], F32)) for i in range(2)]
        w_in, w_ok = sem("b_w_in"), sem("b_w_ok")
        x_in_s, x_free = sem("b_x_in"), sem("b_x_free")
        step, r_ok, q_step = sem("b_step"), sem("b_r_ok"), sem("b_q_step")
        xb_ok, xb_free = sem("b_xb_ok"), sem("b_xb_free")
        t_ok, t_free = sem("b_t_ok"), sem("b_t_free")
        y_ok, y_free = sem("b_y_ok"), sem("b_y_free")
        xc_ok, x3_ok = sem("b_xc_ok"), sem("b_x3_ok")
        stored = sem("b_stored")
        pool_own, dve_own, sp_own, act_own = (sem(f"b_{e}_own") for e in ("pool", "dve", "sp", "act"))
        block = ctx.enter_context(nc.Block())

        def loop(eng, body):
            with eng.Fori(0, GROUPS // 2) as i:
                for k in range(2):
                    body(2 * i + k, k)

        @block.sync
        def _(sp):
            for dst, src in ((w[:], w8.rearrange("(c p) n -> p c n", p=P)), (sc[:], scales.partition_broadcast(P)),
                             (ln_w[:], col), (b_row[:, 0], bias.partition_broadcast(P)), (ident[:], ident_in)):
                sp.dma_start(dst, src).then_inc(w_in, 16)
            sp.dma_start(xt[0][:], x_in[0:GT, :].rearrange("(i p) d -> p i d", p=P)).then_inc(x_in_s, 16)
            sp.sem_inc(stored, 48)

            def body(g, k):
                tok = bass.ds(g * GT, GT)
                nxt = bass.ds(((g + 1) % GROUPS) * GT, GT)
                alone(sp, x_in_s, 16 * g + 16, sp_own)
                alone(sp, x_free, g + 1, sp_own)
                sp.dma_start(xt[1 - k][:], x_in[nxt, :].rearrange("(i p) d -> p i d", p=P)).then_inc(x_in_s, 16)
                alone(sp, xc_ok, g + 1, sp_own)
                sp.dma_start(x_out[tok, :].rearrange("(i p) d -> p i d", p=P), x2[:]).then_inc(stored, 16)
                sp.dma_start(xc_out[tok, :].rearrange("(i p) d -> p i d", p=P), xc[:]).then_inc(stored, 16)
                alone(sp, t_free, 4 * g + 4 + 2, sp_own)
                sp.dma_start(xl_out[:, tok].rearrange("(c p) t -> p c t", p=P),
                             xl[:].rearrange("p c i t -> p c (i t)")).then_inc(stored, 16)
            loop(sp, body)
            sp.wait_ge(stored, 48 * GROUPS + 48)
            sp.wait_ge(x_in_s, 16 * GROUPS + 16)

        @block.gpsimd
        def _(pool):
            nc.gpsimd.memset(mhalf[:], -0.5).then_inc(pool_own, 1)
            pool.wait_ge(pool_own, 1)
            pool.wait_ge(w_in, 16 * 5)

            def body(g, k):
                alone(pool, x_in_s, 16 * g + 16, pool_own)
                alone(pool, xb_free, g + 1, pool_own)
                nc.gpsimd.tensor_tensor(xb[:], xt[k][:], b_row[:].broadcast_to([P, G, D]), ALU.add).then_inc(xb_ok, 1)
                for n in range(3):
                    alone(pool, step, 9 * g + 3 * n + 3, pool_own)
                    nc.gpsimd.tensor_tensor(rstd[:], ve[:], mhalf[:], ALU.pow).then_inc(r_ok, 1)
            loop(pool, body)

        @block.vector
        def _(dve):
            dve.wait_ge(w_in, 16 * 5)
            nc.vector.reciprocal(rs[:], sc[:, 0:1])
            nc.vector.tensor_scalar(w[:], w[:], sc[:, 1:2], None, ALU.mult).then_inc(w_ok, 1)
            dve.wait_ge(w_ok, 1)
            dve.sem_inc(x_free, 1)
            dve.sem_inc(xb_free, 1)
            dve.sem_inc(y_free, 2)

            def body(g, k):
                dve.wait_ge(x_in_s, 16 * g + 16)
                norm_stats(nc, dve, xt[k], stats, mv, ve, step, 9 * g, dve_own)
                dve.wait_ge(r_ok, 3 * g + 1)
                norm_apply(nc, dve, xn, xt[k], mv, rstd).then_inc(x_free, 1)
                dve.wait_ge(x_free, g + 2)
                nc.vector.tensor_scalar(xn[:], xn[:], rs[:, 0:1], 448.0, ALU.mult, ALU.min).then_inc(q_step, 1)
                dve.wait_ge(q_step, 5 * g + 1)
                nc.vector.tensor_scalar(xn[:], xn[:], -448.0, None, ALU.max).then_inc(q_step, 1)
                dve.wait_ge(q_step, 5 * g + 2)
                nc.vector.tensor_scalar(mag[:].bitcast(U32), xn[:].bitcast(U32), 0x7F800000, None,
                                        ALU.bitwise_and).then_inc(q_step, 1)
                dve.wait_ge(q_step, 5 * g + 3)
                nc.vector.tensor_scalar(mag[:], mag[:], 2.0 ** -6, 1.5 * 2.0 ** 20, ALU.max, ALU.mult).then_inc(q_step, 1)
                dve.wait_ge(q_step, 5 * g + 4)
                nc.vector.tensor_tensor(xn[:], xn[:], mag[:], ALU.add).then_inc(q_step, 1)
                dve.wait_ge(q_step, 5 * g + 5)
                nc.vector.tensor_tensor(xq[:], xn[:], mag[:], ALU.subtract).then_inc(x3_ok, 1)
                dve.wait_ge(xb_ok, g + 1)
                dve.wait_ge(stored, 48 * g + 48)
                for j in range(2):
                    dve.wait_ge(y_ok, 2 * g + j + 1)
                    nc.vector.tensor_tensor(x2[:, 2 * j:2 * j + 2, :], ps_y[j][:], xb[:, 2 * j:2 * j + 2, :],
                                            ALU.add).then_inc(y_free, 1)
                dve.wait_ge(y_free, 2 * g + 2 + 2)
                norm_stats(nc, dve, x2, stats, mv, ve, step, 9 * g + 3, dve_own)
                dve.wait_ge(r_ok, 3 * g + 2)
                norm_apply(nc, dve, xc, x2, mv, rstd).then_inc(xc_ok, 1)
                dve.wait_ge(xc_ok, g + 1)
                norm_stats(nc, dve, xc, stats, mv, ve, step, 9 * g + 6, dve_own)
                dve.wait_ge(r_ok, 3 * g + 3)
                norm_apply(nc, dve, x3, xc, mv, rstd).then_inc(xb_free, 1)
            loop(dve, body)

        @block.scalar
        def _(act):
            act.wait_ge(w_in, 16 * 5)
            act.sem_inc(t_free, 2)

            def body(g, k):
                for j in range(2):
                    act.wait_ge(t_ok, 4 * g + j + 1)
                    nc.scalar.activation(xT[:, j], ps_t[j][:], ACT.Copy, scale=sc[:, 0:1]).then_inc(t_free, 1)
                act.wait_ge(stored, 48 * g + 48)
                for j in range(2):
                    act.wait_ge(t_ok, 4 * g + 2 + j + 1)
                    for c in range(DC):
                        last = nc.scalar.activation(xl[:, c, 2 * j:2 * j + 2, :], ps_t[j][:, :, c, :], ACT.Copy,
                                                    scale=ln_w[:, c:c + 1])
                    last.then_inc(t_free, 1)
            loop(act, body)

        @block.tensor
        def _(pe):
            pe.wait_ge(w_ok, 1)

            def body(g, k):
                for n, src in enumerate((xq, x3)):
                    if n == 0:
                        pe.wait_ge(x3_ok, g + 1)
                    else:
                        pe.wait_ge(xb_free, g + 2)
                    for j in range(2):
                        pe.wait_ge(t_free, 4 * g + 2 * n + j + 1)
                        for i in range(2):
                            for c in range(DC):
                                last = nc.tensor.transpose(ps_t[j][:, i, c, :], src[:, 2 * j + i, c * P:(c + 1) * P],
                                                           ident[:])
                        last.then_inc(t_ok, 1)
                    if n == 0:
                        for j in range(2):
                            pe.wait_ge(t_free, 4 * g + j + 1 + 2)
                            pe.wait_ge(y_free, 2 * g + j + 1)
                            for i in range(2):
                                for c in range(DC):
                                    last = nc.tensor.matmul(ps_y[j][:, i, :], xT[:, j, i, c, :], w[:, c, :],
                                                            start=(c == 0), stop=(c == DC - 1))
                            last.then_inc(y_ok, 1)
            loop(pe, body)


DI = 512
CH = DI // P
NS = 16
DTR = 16
TAPS = 4
HALF = 512
NH = S // HALF
BC3 = 3 * 2 * NS


def mixer(nc, xl_in, w_in_d, w_x_d, w_dt_d, cols_d, sel_d, ident_in, y_out):
    with ExitStack() as ctx:
        sb = lambda name, shape, dt=F32: ctx.enter_context(nc.sbuf_tensor(name, shape, dt))
        sem = lambda name: ctx.enter_context(nc.semaphore(name))
        ident = sb("c_ident", [P, P])
        w_i = sb("c_w_i", [P, DC, 2 * DI])
        w_x = sb("c_w_x", [P, CH, BC3 + DTR])
        w_dt = sb("c_w_dt", [BC3 + DTR, DI])
        cols = sb("c_cols", [P, CH, TAPS + 3 + NS])
        taps, conv_b, dt_b, d_p = (cols[:, :, 0:TAPS], cols[:, :, TAPS:TAPS + 1], cols[:, :, TAPS + 1:TAPS + 2],
                                   cols[:, :, TAPS + 2:TAPS + 3])
        a_neg = sb("c_a_neg", [P, CH, NS])
        sel = sb("c_sel", [BC3, 2 * NS, P], BF16)
        xl = sb("c_xl", [P, DC, S])
        xpad = sb("c_xpad", [P, CH, TAPS - 1 + S])
        sz = sb("c_sz", [P, CH, S])
        xc = sb("c_xc", [P, CH, S])
        conv = sb("c_conv", [P, CH, S])
        dt = sb("c_dt", [P, CH, S])
        bc = sb("c_bc", [BC3 + DTR, S])
        bc_mid = sb("c_bc_mid", [BC3, S], BF16)
        stack = sb("c_stack", [BC3, S], BF16)
        RING = 4
        NB = 2 * RING
        AHEAD = 3
        bs = [sb(f"c_bs{i}", [P, S]) for i in range(RING)]
        da = [sb(f"c_da{i}", [P, S]) for i in range(NB)]
        db = [sb(f"c_db{i}", [P, S]) for i in range(NB)]
        ps_y = ctx.enter_context(nc.psum_tensor("c_ps_y", [P, 2, S], F32))
        ps_b = ctx.enter_context(nc.psum_tensor("c_ps_b", [P, S], F32))
        ps_c = ctx.enter_context(nc.psum_tensor("c_ps_c", [P, S], F32))

        w_in, w_ok = sem("c_w_in"), sem("c_w_ok")
        xl_in_s = sem("c_xl_in")
        pi_ok, pi_free = sem("c_pi_ok"), sem("c_pi_free")
        conv_ok, xc_ok = sem("c_conv_ok"), sem("c_xc_ok")
        bc_ok, bc_step = sem("c_bc_ok"), sem("c_bc_step")
        sp_a, sp_v, dt_ok, dtx_ok = sem("c_sp_a"), sem("c_sp_v"), sem("c_dt_ok"), sem("c_dtx_ok")
        b_ok, c_ok, b_free = sem("c_b_ok"), sem("c_c_ok"), sem("c_b_free")
        bs_ok, da_ok, db_ok = sem("c_bs_ok"), sem("c_da_ok"), sem("c_db_ok")
        h_ok, hc_ok, acc_ok = sem("c_h_ok"), sem("c_hc_ok"), sem("c_acc_ok")
        y_step, y_ok, stored = sem("c_y_step"), sem("c_y_ok"), sem("c_stored")
        pool_own, dve_own, act_own, sp_own = (sem(f"c_{e}_own") for e in ("pool", "dve", "act", "sp"))
        block = ctx.enter_context(nc.Block())
        FRONT = 2 * 2 * CH + NH + CH * NH
        UNITS = CH * NS
        front_ps = [ps_b, ps_c]

        def n_of(b, pair, n):
            return (2 * b + pair) * NS + n

        @block.sync
        def _(sp):
            for dst, src in ((w_i[:], w_in_d.rearrange("(c p) n -> p c n", p=P)),
                             (w_x[:], w_x_d.rearrange("(c p) n -> p c n", p=P)),
                             (w_dt[BC3:BC3 + DTR, :], w_dt_d), (cols[:], cols_d.rearrange("(c p) n -> p c n", p=P)),
                             (sel[:], sel_d.rearrange("r (n p) -> r n p", p=P)), (ident[:], ident_in)):
                sp.dma_start(dst, src).then_inc(w_in, 16)
            sp.sem_inc(stored, 16)
            with sp.Fori(0, B) as b:
                alone(sp, pi_free, FRONT * b + 2, sp_own)
                sp.dma_start(xl[:], xl_in[:, bass.ds(b * S, S)].rearrange("(c p) t -> p c t", p=P)).then_inc(xl_in_s, 16)
                for pair in range(CH // 2):
                    for c in range(2):
                        m = 2 * pair + c
                        alone(sp, y_ok, CH * b + m + 1, sp_own)
                        sp.dma_start(y_out[m * P:(m + 1) * P, bass.ds(b * S, S)], conv[:, m, :]).then_inc(stored, 16)
            sp.wait_ge(stored, 16 * CH * B + 16)

        @block.tensor
        def _(pe):
            pe.wait_ge(w_in, 16 * 6)

            def front(b):
                pe.wait_ge(xl_in_s, 16 * b + 16)
                n_out = 0

                def out(rows=P):
                    nonlocal n_out
                    pe.wait_ge(pi_free, FRONT * b + n_out + 1)
                    if n_out < 2:
                        pe.wait_ge(hc_ok, UNITS * b + 1)
                    n_out += 1
                    return front_ps[(n_out - 1) % 2][0:rows, 0:HALF]

                for m in range(2 * CH):
                    for n in range(NH):
                        o = out()
                        for c in range(DC):
                            last = nc.tensor.matmul(o, w_i[:, c, m * P:(m + 1) * P], xl[:, c, n * HALF:(n + 1) * HALF],
                                                    start=(c == 0), stop=(c == DC - 1))
                        last.then_inc(pi_ok, 1)
                pe.wait_ge(xc_ok, CH * b + CH)
                for n in range(NH):
                    o = out(BC3 + DTR)
                    for c in range(CH):
                        last = nc.tensor.matmul(o, w_x[:, c, :], xc[:, c, n * HALF:(n + 1) * HALF],
                                                start=(c == 0), stop=(c == CH - 1))
                    last.then_inc(pi_ok, 1)
                pe.wait_ge(bc_ok, NH * b + NH)
                for m in range(CH):
                    for n in range(NH):
                        o = out()
                        nc.tensor.matmul(o, w_dt[BC3:BC3 + DTR, m * P:(m + 1) * P],
                                         bc[BC3:BC3 + DTR, n * HALF:(n + 1) * HALF],
                                         start=True, stop=True).then_inc(pi_ok, 1)

            def b_cast(b, pair, n):
                N = n_of(b, pair, n)
                pe.wait_ge(b_free, N + 1)
                for half in range(NH):
                    last = nc.tensor.matmul(ps_b[:, half * HALF:(half + 1) * HALF],
                                            sel[:, bass.ds(n % NS, 1), :].rearrange("r a p -> r (a p)"),
                                            stack[:, half * HALF:(half + 1) * HALF], start=True, stop=True)
                last.then_inc(b_ok, 1)

            def c_cast(b, pair, n):
                N = n_of(b, pair, n)
                pe.wait_ge(hc_ok, 2 * N + 1)
                for half in range(NH):
                    last = nc.tensor.matmul(ps_c[:, half * HALF:(half + 1) * HALF],
                                            sel[:, bass.ds(NS + n % NS, 1), :].rearrange("r a p -> r (a p)"),
                                            stack[:, half * HALF:(half + 1) * HALF], start=True, stop=True)
                last.then_inc(c_ok, 1)

            def sums(b, pair, n, k, start, stop):
                N = n_of(b, pair, n)
                for c in range(2):
                    if start:
                        pe.wait_ge(y_step, 2 * (2 * b + pair) + c + 1)
                    pe.wait_ge(hc_ok, 2 * N + c + 1 + 1)
                    for half in range(NH):
                        cut = slice(half * HALF, (half + 1) * HALF)
                        last = nc.tensor.matmul(ps_y[:, c, cut], ident[:], da[2 * k + c][:, cut],
                                                start=start, stop=stop)
                    last.then_inc(acc_ok, 1)

            def state(b, pair, n, k, first=False, last=False):
                if not (last and pair == 1):
                    c_cast(b, pair, n + 1)
                sums(b, pair, n, k, first, last)

            with pe.Fori(0, B) as b:
                front(b)
                pe.wait_ge(bc_step, 5 * b + 5)
                pe.wait_ge(pi_free, FRONT * (b + 1) + 2)
                for n in range(AHEAD):
                    b_cast(b, 0, n)
                c_cast(b, 0, 0)
                for pair in range(CH // 2):
                    for k in range(RING):
                        state(b, pair, k, k, first=k == 0)
                        b_cast(b, pair, k + AHEAD)
                    with pe.Fori(1, NS // RING - 1) as i:
                        for k in range(RING):
                            state(b, pair, RING * i + k, k)
                            b_cast(b, pair, RING * i + k + AHEAD)
                    for k in range(RING):
                        n = NS - RING + k
                        state(b, pair, n, k, last=n == NS - 1)
                        if pair == 0 or n + AHEAD < NS:
                            b_cast(b, pair, n + AHEAD)

        @block.gpsimd
        def _(pool):
            with pool.Fori(0, B) as b:
                for pair in range(CH // 2):
                    for c in range(2):
                        m = 2 * pair + c
                        alone(pool, dt_ok, CH * b + m + 1, pool_own)
                        nc.gpsimd.tensor_tensor(conv[:, m, :], dt[:, m, :], xc[:, m, :], ALU.mult).then_inc(dtx_ok, 1)
                    alone(pool, dtx_ok, CH * b + 2 * pair + 2, pool_own)
                    with pool.Fori(0, NS // RING) as i:
                        for k in range(RING):
                            N = n_of(b, pair, RING * i + k)
                            alone(pool, bs_ok, N + 1, pool_own)
                            for c in range(2):
                                alone(pool, h_ok, 2 * N + c + 1, pool_own)
                                nc.gpsimd.tensor_tensor(db[2 * k + c][:], conv[:, 2 * pair + c, :], bs[k][:],
                                                        ALU.mult).then_inc(db_ok, 1)

        @block.scalar
        def _(act):
            act.wait_ge(w_in, 16 * 6)
            nc.scalar.activation(a_neg[:], cols[:, :, TAPS + 3:], ACT.Exp).then_inc(w_ok, 1)
            act.sem_inc(b_free, 1)
            act.sem_inc(pi_free, 2)

            def front(b):
                def project(m):
                    for n in range(NH):
                        i = NH * m + n
                        act.wait_ge(pi_ok, FRONT * b + i + 1)
                        src = front_ps[i % 2][:, 0:HALF]
                        if m < CH:
                            nc.scalar.copy(xpad[:, m, TAPS - 1 + n * HALF:TAPS - 1 + (n + 1) * HALF], src
                                           ).then_inc(pi_free, 1)
                        else:
                            nc.scalar.activation(sz[:, m - CH, n * HALF:(n + 1) * HALF], src, ACT.Silu
                                                 ).then_inc(pi_free, 1)

                for m in range(CH):
                    project(m)
                for m in range(CH):
                    project(CH + m)
                    act.wait_ge(conv_ok, TAPS * (CH * b + 2 * (m // 2)) + 2 * (TAPS - 1) + m % 2 + 1)
                    nc.scalar.activation(xc[:, m, :], conv[:, m, :], ACT.Silu, bias=conv_b[:, m, :]).then_inc(xc_ok, 1)
                base = 2 * 2 * CH
                for n in range(NH):
                    act.wait_ge(pi_ok, FRONT * b + base + n + 1)
                    nc.scalar.copy(bc[:, n * HALF:(n + 1) * HALF], front_ps[(base + n) % 2][0:BC3 + DTR, 0:HALF]
                                   ).then_inc(bc_ok, 1)
                    act.wait_ge(bc_ok, NH * b + n + 1)
                    act.sem_inc(pi_free, 1)
                base += NH
                for m in range(CH):
                    for n in range(NH):
                        i = NH * m + n
                        cut = slice(n * HALF, (n + 1) * HALF)
                        act.wait_ge(pi_ok, FRONT * b + base + i + 1)
                        nc.scalar.activation(dt[:, m, cut], front_ps[(base + i) % 2][:, 0:HALF], ACT.Abs,
                                             bias=dt_b[:, m, :]).then_inc(sp_a, 1)
                    act.wait_ge(sp_a, NH * (CH * b + m + 1))
                    nc.scalar.activation(dt[:, m, :], dt[:, m, :], ACT.Exp, scale=-1.0).then_inc(sp_v, 1)
                    act.wait_ge(sp_v, 2 * (CH * b + m) + 1)
                    nc.scalar.activation(dt[:, m, :], dt[:, m, :], ACT.Ln, bias=1.0).then_inc(sp_v, 1)

            with act.Fori(0, B) as b:
                front(b)
                for pair in range(CH // 2):
                    with act.Fori(0, NS // RING) as i:
                        for k in range(RING):
                            N = n_of(b, pair, RING * i + k)
                            act.wait_ge(b_ok, N + 1)
                            act.wait_ge(db_ok, 2 * N + 2)
                            nc.scalar.copy(bs[k][:], ps_b[:]).then_inc(bs_ok, 1)
                            act.wait_ge(bs_ok, N + 1)
                            act.sem_inc(b_free, 1)
                            for c in range(2):
                                m = 2 * pair + c
                                act.wait_ge(dt_ok, CH * b + m + 1)
                                alone(act, acc_ok, 2 * N + c + 1, act_own)
                                nc.scalar.activation(da[2 * k + c][:], dt[:, m, :], ACT.Exp,
                                                     scale=a_neg[:, m, bass.ds(RING * i + k, 1)]).then_inc(da_ok, 1)

        @block.vector
        def _(dve):
            nc.vector.memset(xpad[:, :, 0:TAPS - 1], 0.0)
            dve.wait_ge(w_ok, 1)
            nc.vector.tensor_scalar(a_neg[:], a_neg[:], -1.0, None, ALU.mult).then_inc(w_ok, 1)
            dve.wait_ge(w_ok, 2)
            dve.sem_inc(h_ok, NB)
            dve.sem_inc(hc_ok, 1)
            dve.sem_inc(acc_ok, NB)
            dve.sem_inc(db_ok, 2 * RING)
            dve.sem_inc(y_step, 2)

            def front(b):
                dve.wait_ge(stored, 16 * CH * b + 16)
                for m0 in range(0, CH, 2):
                    for k in range(TAPS):
                        for m in (m0, m0 + 1):
                            src = xpad[:, m, k:k + S]
                            if k == 0:
                                dve.wait_ge(pi_free, FRONT * b + NH * (m + 1) + 2)
                                nc.vector.tensor_scalar(conv[:, m, :], src, taps[:, m, 0:1], None, ALU.mult
                                                        ).then_inc(conv_ok, 1)
                            else:
                                dve.wait_ge(conv_ok, TAPS * (CH * b + m0) + 2 * (k - 1) + m - m0 + 1)
                                nc.vector.scalar_tensor_tensor(conv[:, m, :], src, taps[:, m, k:k + 1], conv[:, m, :],
                                                               ALU.mult, ALU.add).then_inc(conv_ok, 1)
                dve.wait_ge(bc_ok, NH * b + NH)
                step = 5 * b
                nc.vector.tensor_copy(stack[:], bc[0:BC3, :]).then_inc(bc_step, 1)
                dve.wait_ge(bc_step, step + 1)
                nc.vector.tensor_tensor(bc[0:BC3, :], bc[0:BC3, :], stack[:], ALU.subtract).then_inc(bc_step, 1)
                dve.wait_ge(bc_step, step + 2)
                nc.vector.tensor_copy(bc_mid[:], bc[0:BC3, :]).then_inc(bc_step, 1)
                dve.wait_ge(bc_step, step + 3)
                r = 2 * NS
                nc.vector.tensor_copy(stack[r:2 * r, :], bc_mid[r:2 * r, :]).then_inc(bc_step, 1)
                nc.vector.tensor_tensor(stack[2 * r:3 * r, :], bc[2 * r:3 * r, :], bc_mid[2 * r:3 * r, :], ALU.subtract
                                        ).then_inc(bc_step, 1)
                base = 2 * 2 * CH + NH
                for m in range(CH):
                    for n in range(NH):
                        i = NH * m + n
                        cut = slice(n * HALF, (n + 1) * HALF)
                        dve.wait_ge(sp_a, CH * NH * b + i + 1)
                        nc.vector.tensor_scalar(conv[:, m, cut], front_ps[(base + i) % 2][:, 0:HALF], dt_b[:, m, :], 0.0,
                                                ALU.add, ALU.max).then_inc(pi_free, 1)
                    dve.wait_ge(sp_v, 2 * (CH * b + m + 1))
                    dve.wait_ge(pi_free, FRONT * b + base + NH * (m + 1) + 2)
                    nc.vector.tensor_tensor(dt[:, m, :], dt[:, m, :], conv[:, m, :], ALU.add).then_inc(dt_ok, 1)

            def scan(b, pair, n, k):
                N = n_of(b, pair, n)
                for c in range(2):
                    dve.wait_ge(db_ok, 2 * RING + 2 * N + c + 1)
                    dve.wait_ge(da_ok, 2 * N + c + 1)
                    q = 2 * k + c
                    nc.vector.tensor_tensor_scan(da[q][:], da[q][:], db[q][:], 0.0, ALU.mult, ALU.add).then_inc(h_ok, 1)

            def times_c(b, pair, n, k):
                N = n_of(b, pair, n)
                dve.wait_ge(c_ok, N + 1)
                for c in range(2):
                    q = 2 * k + c
                    dve.wait_ge(h_ok, NB + 2 * N + c + 1)
                    nc.vector.tensor_tensor(da[q][:], da[q][:], ps_c[:], ALU.mult).then_inc(hc_ok, 1)

            def gated(b, pair):
                for c in range(2):
                    m = 2 * pair + c
                    dve.wait_ge(acc_ok, NB + 2 * NS * (2 * b + pair + 1) - 1 + c)
                    nc.vector.scalar_tensor_tensor(conv[:, m, :], xc[:, m, :], d_p[:, m, :], ps_y[:, c, :],
                                                   ALU.mult, ALU.add).then_inc(y_step, 1)
                for c in range(2):
                    m = 2 * pair + c
                    dve.wait_ge(y_step, 2 * (2 * b + pair) + c + 3)
                    nc.vector.tensor_tensor(conv[:, m, :], conv[:, m, :], sz[:, m, :], ALU.mult).then_inc(y_ok, 1)

            def state(b, pair, n, k):
                scan(b, pair, n, k)
                times_c(b, pair, n, k)

            with dve.Fori(0, B) as b:
                front(b)
                for pair in range(CH // 2):
                    for k in range(RING):
                        state(b, pair, k, k)
                        if pair and k == 1:
                            gated(b, pair - 1)
                    with dve.Fori(1, NS // RING) as i:
                        for k in range(RING):
                            state(b, pair, RING * i + k, k)
                gated(b, CH // 2 - 1)


DF = 1024
DG = 768
MF, MG = DF // P, DG // P
INT_SCALE = 1.0 / 127.0


def tail(nc, ym_in, xc_in, x2_in, w_out_d, w_fc_d, w_pr_d, w_gu_d, w_dn_d, ln2_d, ident_in, out):
    with ExitStack() as ctx:
        sb = lambda name, shape, dt=F32: ctx.enter_context(nc.sbuf_tensor(name, shape, dt))
        sem = lambda name: ctx.enter_context(nc.semaphore(name))
        ident = sb("d_ident", [P, P])
        w_out = sb("d_w_out", [P, CH, D])
        w_fc = sb("d_w_fc", [P, DC, DF])
        w_pr = sb("d_w_pr", [P, MF, D])
        w_gi = sb("d_w_gi", [P, DC, 2 * DG], I32)
        w_di = sb("d_w_di", [P, MG, D], I32)
        w_gu = sb("d_w_gu", [P, DC, 2 * DG])
        w_dn = sb("d_w_dn", [P, MG, D])
        ln_w = sb("d_ln_w", [P, DC])
        mhalf = sb("d_mhalf", [P, G])
        ym = [sb(f"d_ym{i}", [P, CH, GT]) for i in range(2)]
        xc = [sb(f"d_xc{i}", [P, G, D]) for i in range(2)]
        x2 = [sb(f"d_x2{i}", [P, G, D]) for i in range(2)]
        y1 = sb("d_y1", [P, G, D])
        x3 = sb("d_x3", [P, G, D])
        stats = sb("d_stats", [P, G, 6])
        mv = sb("d_mv", [P, G, 2])
        ve = sb("d_ve", [P, G])
        rstd = sb("d_rstd", [P, G])
        xn = sb("d_xn", [P, G, D])
        nT = sb("d_nT", [P, DC, G, P])
        hT = sb("d_hT", [P, MF, GT])
        sg = [sb(f"d_sg{i}", [P, GT]) for i in range(2)]
        o = sb("d_o", [P, G, D])
        ps_t = [ctx.enter_context(nc.psum_tensor(f"d_ps_t{i}", [P, 2, DC, P], F32)) for i in range(2)]
        ps_y = [ctx.enter_context(nc.psum_tensor(f"d_ps_y{i}", [P, 2, D], F32)) for i in range(2)]
        ps_a = [ctx.enter_context(nc.psum_tensor(f"d_ps_a{i}", [P, GT], F32)) for i in range(2)]
        ps_u = [ctx.enter_context(nc.psum_tensor(f"d_ps_u{i}", [P, GT], F32)) for i in range(2)]
        w_in, w_ok, in_s, in_free = sem("d_w_in"), sem("d_w_ok"), sem("d_in"), sem("d_in_free")
        y_ok, y_free = sem("d_y_ok"), sem("d_y_free")
        t_ok, t_free = sem("d_t_ok"), sem("d_t_free")
        a_ok, a_free, u_ok, h_ok = sem("d_a_ok"), sem("d_a_free"), sem("d_u_ok"), sem("d_h_ok")
        step, r_ok, n_ok, s_ok, stored = sem("d_step"), sem("d_r_ok"), sem("d_n_ok"), sem("d_s_ok"), sem("d_stored")
        pool_own, dve_own, sp_own = (sem(f"d_{e}_own") for e in ("pool", "dve", "sp"))
        block = ctx.enter_context(nc.Block())
        NA = MF + MG

        def loop(eng, body):
            with eng.Fori(0, GROUPS // 2) as i:
                for k in range(2):
                    body(2 * i + k, k)

        def rows(x, g):
            return x[bass.ds(g * GT, GT), :].rearrange("(i p) d -> p i d", p=P)

        @block.sync
        def _(sp):
            for dst, src in ((w_out[:], w_out_d.rearrange("(c p) n -> p c n", p=P)),
                             (w_fc[:], w_fc_d.rearrange("(c p) n -> p c n", p=P)),
                             (w_pr[:], w_pr_d.rearrange("(c p) n -> p c n", p=P)),
                             (w_gi[:], w_gu_d.rearrange("(c p) n -> p c n", p=P)),
                             (w_di[:], w_dn_d.rearrange("(c p) n -> p c n", p=P)),
                             (ln_w[:], ln2_d), (ident[:], ident_in)):
                sp.dma_start(dst, src).then_inc(w_in, 16)

            def load(g, k):
                sp.dma_start(ym[k][:], ym_in[:, bass.ds(g * GT, GT)].rearrange("(c p) t -> p c t", p=P)).then_inc(in_s, 16)
                sp.dma_start(xc[k][:], rows(xc_in, g)).then_inc(in_s, 16)
                sp.dma_start(x2[k][:], rows(x2_in, g)).then_inc(in_s, 16)

            load(0, 0)

            def body(g, k):
                alone(sp, in_s, 48 * g + 48, sp_own)
                alone(sp, in_free, g + 1, sp_own)
                load((g + 1) % GROUPS, 1 - k)
                alone(sp, y_free, 6 * g + 6 + 2, sp_own)
                sp.dma_start(rows(out, g), o[:]).then_inc(stored, 16)
            sp.sem_inc(stored, 16)
            loop(sp, body)
            sp.wait_ge(stored, 16 * GROUPS + 16)
            sp.wait_ge(in_s, 48 * GROUPS + 48)

        @block.gpsimd
        def _(pool):
            nc.gpsimd.memset(mhalf[:], -0.5).then_inc(pool_own, 1)
            pool.wait_ge(pool_own, 1)

            def body(g, k):
                alone(pool, step, 6 * g + 3, pool_own)
                nc.gpsimd.tensor_tensor(rstd[:], ve[:], mhalf[:], ALU.pow).then_inc(r_ok, 1)
                alone(pool, n_ok, 2 * g + 1, pool_own)
                nc.gpsimd.tensor_tensor(y1[:], y1[:], x2[k][:], ALU.add).then_inc(s_ok, 1)
                alone(pool, step, 6 * g + 6, pool_own)
                nc.gpsimd.tensor_tensor(rstd[:], ve[:], mhalf[:], ALU.pow).then_inc(r_ok, 1)
            loop(pool, body)

        @block.vector
        def _(dve):
            dve.wait_ge(w_in, 16 * 7)
            nc.vector.tensor_scalar(w_gu[:], w_gi[:], INT_SCALE, None, ALU.mult)
            nc.vector.tensor_scalar(w_dn[:], w_di[:], INT_SCALE, None, ALU.mult).then_inc(w_ok, 1)
            dve.sem_inc(y_free, 2)
            dve.sem_inc(h_ok, 2)
            dve.sem_inc(in_free, 1)

            def body(g, k):
                dve.wait_ge(in_s, 48 * g + 48)
                for j in range(2):
                    dve.wait_ge(y_ok, 6 * g + j + 1)
                    nc.vector.tensor_tensor(y1[:, 2 * j:2 * j + 2, :], ps_y[j][:], xc[k][:, 2 * j:2 * j + 2, :],
                                            ALU.add).then_inc(y_free, 1)
                dve.wait_ge(y_free, 6 * g + 2 + 2)
                norm_stats(nc, dve, y1, stats, mv, ve, step, 6 * g, dve_own)
                dve.wait_ge(r_ok, 2 * g + 1)
                norm_apply(nc, dve, xn, y1, mv, rstd).then_inc(n_ok, 1)
                dve.wait_ge(s_ok, g + 1)
                for j in range(2):
                    dve.wait_ge(y_ok, 6 * g + 2 + j + 1)
                    nc.vector.tensor_tensor(x3[:, 2 * j:2 * j + 2, :], ps_y[j][:], y1[:, 2 * j:2 * j + 2, :],
                                            ALU.add).then_inc(y_free, 1)
                dve.wait_ge(y_free, 6 * g + 4 + 2)
                norm_stats(nc, dve, x3, stats, mv, ve, step, 6 * g + 3, dve_own)
                dve.wait_ge(r_ok, 2 * g + 2)
                norm_apply(nc, dve, xn, x3, mv, rstd).then_inc(n_ok, 1)
                for m in range(MG):
                    dve.wait_ge(a_free, NA * g + MF + m + 1 + 2)
                    dve.wait_ge(u_ok, MG * g + m + 1)
                    nc.vector.tensor_tensor(hT[:, m, :], ps_u[m % 2][:], sg[m % 2][:], ALU.mult).then_inc(h_ok, 1)
                dve.wait_ge(stored, 16 * g + 16)
                for j in range(2):
                    dve.wait_ge(y_ok, 6 * g + 4 + j + 1)
                    nc.vector.tensor_tensor(o[:, 2 * j:2 * j + 2, :], ps_y[j][:], x3[:, 2 * j:2 * j + 2, :],
                                            ALU.add).then_inc(y_free, 1)
                dve.sem_inc(in_free, 1)
            loop(dve, body)

        @block.scalar
        def _(act):
            act.wait_ge(w_in, 16 * 7)
            act.sem_inc(t_free, 2)
            act.sem_inc(a_free, 2)

            def body(g, k):
                for n in range(2):
                    for j in range(2):
                        act.wait_ge(t_ok, 4 * g + 2 * n + j + 1)
                        for c in range(DC):
                            scale = ln_w[:, c:c + 1] if n == 0 else 1.0
                            last = nc.scalar.activation(nT[:, c, 2 * j:2 * j + 2, :], ps_t[j][:, :, c, :], ACT.Copy,
                                                        scale=scale)
                        last.then_inc(t_free, 1)
                    if n == 0:
                        for m in range(MF):
                            act.wait_ge(a_ok, NA * g + m + 1)
                            nc.scalar.activation(hT[:, m, :], ps_a[m % 2][:], ACT.Silu).then_inc(a_free, 1)
                for m in range(MG):
                    act.wait_ge(a_ok, NA * g + MF + m + 1)
                    act.wait_ge(h_ok, MG * g + m + 1)
                    nc.scalar.activation(sg[m % 2][:], ps_a[m % 2][:], ACT.Silu).then_inc(a_free, 1)
            loop(act, body)

        @block.tensor
        def _(pe):
            pe.wait_ge(w_in, 16 * 7)
            pe.wait_ge(w_ok, 1)

            def turn(g, n):
                pe.wait_ge(n_ok, 2 * g + n + 1)
                for j in range(2):
                    pe.wait_ge(t_free, 4 * g + 2 * n + j + 1)
                    for i in range(2):
                        for c in range(DC):
                            last = nc.tensor.transpose(ps_t[j][:, i, c, :], xn[:, 2 * j + i, c * P:(c + 1) * P], ident[:])
                    last.then_inc(t_ok, 1)
                pe.wait_ge(t_free, 4 * g + 2 * n + 2 + 2)

            def rows_out(g, n, lhs, w, count):
                for j in range(2):
                    pe.wait_ge(y_free, 6 * g + 2 * n + j + 1)
                    for i in range(2):
                        for c in range(count):
                            at = (2 * j + i) * P
                            last = nc.tensor.matmul(ps_y[j][:, i, :], lhs[:, c, at:at + P], w[:, c, :],
                                                    start=(c == 0), stop=(c == count - 1))
                    last.then_inc(y_ok, 1)

            def hidden(dst, w, at):
                for c in range(DC):
                    last = nc.tensor.matmul(dst[:], w[:, c, at:at + P], nT[:, c].rearrange("p i t -> p (i t)"),
                                            start=(c == 0), stop=(c == DC - 1))
                return last

            def body(g, k):
                pe.wait_ge(in_s, 48 * g + 48)
                rows_out(g, 0, ym[k], w_out, CH)
                turn(g, 0)
                for m in range(MF):
                    pe.wait_ge(a_free, NA * g + m + 1)
                    hidden(ps_a[m % 2], w_fc, m * P).then_inc(a_ok, 1)
                pe.wait_ge(a_free, NA * g + MF + 2)
                rows_out(g, 1, hT, w_pr, MF)
                turn(g, 1)
                for m in range(MG):
                    pe.wait_ge(a_free, NA * g + MF + m + 1)
                    hidden(ps_a[m % 2], w_gu, m * P).then_inc(a_ok, 1)
                    pe.wait_ge(h_ok, MG * g + m + 1)
                    hidden(ps_u[m % 2], w_gu, DG + m * P).then_inc(u_ok, 1)
                pe.wait_ge(h_ok, MG * g + MG + 2)
                rows_out(g, 2, hT, w_dn, MG)
            loop(pe, body)


def kernel(**inputs):
    import ml_dtypes
    import numpy as np
    import concourse.bacc as bacc
    from concourse.bass_utils import run_bass_kernel_spmd as run

    f = {k: np.asarray(v) for k, v in inputs.items()}
    a = {k[8:]: v for k, v in f.items() if k.startswith("L0_attn_")}
    m = {k[8:]: v for k, v in f.items() if k.startswith("L1_attn_")}
    x_proj = m["x_proj_w"].T
    sel = np.zeros((BC3, 2 * NS, P), dtype=ml_dtypes.bfloat16)
    for n in range(2 * NS):
        sel[n::2 * NS, n] = 1
    arrays = {
        "x": a["hidden_states"].reshape(B * S, D),
        "w_qk": np.concatenate([a["Wq"].T, a["Wk"].T], axis=1),
        "w_vg": np.concatenate([a["Wv"].T, a["gate_W"].T, a["rel_W"][:, :D].T, a["rel_W"][:, D:].T, a["Wo"].T], axis=1),
        "b_qk": np.concatenate([a["bq"], a["bk"]]).reshape(4, P).T,
        "rows": np.concatenate([a["bv"], a["bo"], a["gate_b"], a["rel_b"], a["logical_bias"].T.reshape(-1)]),
        "w_fp8": f["L0_ffn_weight_fp8"].T,
        "scales": np.concatenate([f["L0_ffn_input_scale"], f["L0_ffn_weight_scale"]]),
        "b_fp8": f["L0_ffn_bias"],
        "ln1_w": m["ln1_w"].reshape(DC, P).T,
        "w_in": m["in_proj_w"].T,
        "w_x": np.concatenate([x_proj[:, DTR:]] * 3 + [x_proj[:, :DTR]], axis=1),
        "w_dt": m["dt_proj_w"].T,
        "cols": np.concatenate([m["conv_w"][:, 0], m["conv_b"][:, None], m["dt_proj_b"][:, None], m["Dp"][:, None],
                                m["A_log"]], axis=1),
        "sel": sel.reshape(BC3, -1),
        "w_out": m["out_proj_w"].T,
        "w_fc": m["fc_w"].T,
        "w_pr": m["proj_w"].T,
        "ln2_w": m["ln2_w"].reshape(DC, P).T,
        "w_gu": np.concatenate([f["L1_ffn_w_gate"].T, f["L1_ffn_w_up"].T], axis=1),
        "w_dn": f["L1_ffn_w_down"].T,
        "ident": np.eye(P, dtype=np.float32),
    }
    arrays = {"in_" + k: np.ascontiguousarray(v) for k, v in arrays.items()}
    nc = bacc.Bacc("TRN2", target_bir_lowering=False, num_devices=1)
    d = {k[3:]: nc.dram_tensor(k, v.shape, mybir.dt.from_np(v.dtype), kind="ExternalInput").ap()
         for k, v in arrays.items()}
    out = nc.dram_tensor("out", (B * S, D), F32, kind="ExternalOutput").ap()
    scratch = lambda name, shape, dt=F32: nc.dram_tensor(name + "_d", shape, dt, kind="Internal").ap()
    parts = scratch("parts", (3, 2 * D, B * S), BF16)
    x1, x2, xc = (scratch(n, (B * S, D)) for n in ("x1", "x2", "xc"))
    xl = scratch("xl", (D, B * S))
    ym = scratch("ym", (DI, B * S))
    attention(nc, d["x"], d["w_qk"], d["w_vg"], d["b_qk"], d["rows"], d["ident"], parts, x1)
    fp8_layer(nc, x1, d["w_fp8"], d["scales"], d["ln1_w"], d["b_fp8"], d["ident"], x2, xc, xl)
    mixer(nc, xl, d["w_in"], d["w_x"], d["w_dt"], d["cols"], d["sel"], d["ident"], ym)
    tail(nc, ym, xc, x2, d["w_out"], d["w_fc"], d["w_pr"], d["w_gu"], d["w_dn"], d["ln2_w"], d["ident"], out)
    r = run(nc, [arrays], core_ids=[0])
    return r.results[0]["out"].reshape(B, S, D)
```

```python
import concourse.bass as bass
from concourse import mybir
from concourse.alu_op_type import AluOpType as ALU
from contextlib import ExitStack

ACT = mybir.ActivationFunctionType
F32 = mybir.dt.float32
BF16 = mybir.dt.bfloat16
I32 = mybir.dt.int32
U32 = mybir.dt.uint32
P = 128
BIG = 3.0e38
LN_EPS = 1e-5

B, S, D = 8, 1024, 256
NT = S // P
TILES = B * NT
DC = D // P
H = 16
HD = D // H
HG = 4

Q_PART = [0, 0, 0, 1, 1, 2]
K_PART = [0, 1, 2, 0, 1, 0]
KROWS = HD * len(Q_PART)


def wait(eng, sem, value):
    if isinstance(value, int) and value <= 0:
        return
    eng.wait_ge(sem, value)


def alone(eng, sem, value, own):
    if isinstance(value, int) and value <= 0:
        return
    eng.wait_ge(sem, value)
    eng.sem_inc(own, 1)


def attention(nc, x_in, wqk, wvg, bqk, rows, ident_in, parts_d, x_out):
    AHEAD = NT + 1
    LEAD = 4
    NROW = 8
    NAT = 2 * HG
    with ExitStack() as ctx:
        sb = lambda name, shape, dt=F32: ctx.enter_context(nc.sbuf_tensor(name, shape, dt))
        sem = lambda name: ctx.enter_context(nc.semaphore(name))
        psum = lambda name, shape: ctx.enter_context(nc.psum_tensor(name, shape, F32))

        ident = sb("ident", [P, P])
        w_qk = sb("w_qk", [P, DC, 2 * D])
        w_vg = sb("w_vg", [P, DC, D + H + 6])
        w_o = sb("w_o", [P, DC, D])
        w_dj = sb("w_dj", [P, DC, 2, P])
        b_qk = sb("b_qk", [P, 4])
        row = sb("row", [P, 2 * D + H + 3 + 3 * H])
        b_v, b_o = row[:, 0:D], row[:, D:2 * D]
        b_g = row[:, 2 * D:2 * D + H + 3]
        lbk = row[:, 2 * D + H + 3:2 * D + H + 3 + 3 * H].rearrange("p (k h) -> p k h", k=3)
        b_misc = sb("b_misc", [P, H + 2])
        lbd = sb("lbd", [P, 3, H])
        xt = sb("xt", [P, 2, D])
        stats = sb("stats", [P, 6])
        mv = sb("mv", [P, 2])
        ve = sb("ve", [P, 1])
        mhalf = sb("mhalf", [P, 1])
        rstd = sb("rstd", [P, 1])
        xn = sb("xn", [P, D])
        xnT = sb("xnT", [P, DC, P])
        qkf = sb("qkf", [P, 4, P])
        parts = sb("parts", [P, 3, 4, P], BF16)
        zg = sb("zg", [P, H + 2])
        ge = sb("ge", [P, H])
        gate = sb("gate", [P, H])
        small = sb("small", [P, 2 * NT, 3 * H + 2])
        K6 = sb("K6", [KROWS, H, S], BF16)
        V = [sb(f"V{i}", [P, NT, D + HD]) for i in range(2)]
        Dj = sb("Dj", [P, 2, 2 * S])
        Q6 = [sb(f"Q6_{i}", [KROWS, H, P], BF16) for i in range(2)]
        R = [[sb(f"R{i}_{k}", [P, S]) for k in range(2)] for i in range(2)]
        RT = sb("RT", [P, S])
        R2 = sb("R2", [P, S])
        cur = [sb(f"cur{i}", [P, 3 * H + 2]) for i in range(2)]
        rows_sb = [sb(f"srow{i}", [P, S]) for i in range(NROW)]
        nmax = sb("nmax", [P, NROW])
        rsum = sb("rsum", [P, 2, H])
        AT = [sb(f"AT{i}", [P, NT, P]) for i in range(NAT)]
        O4 = sb("O4", [P, HG, P])
        rinv = sb("rinv", [P, H])
        attn = sb("attn", [P, D])
        attnT = sb("attnT", [P, DC, P])
        xr = sb("xr", [P, D])

        ps_s = psum("ps_s", [P, 2, S])
        ps_t = psum("ps_t", [P, 2, HG, P])
        ps_o = psum("ps_o", [P, HG, P])
        ps_m = psum("ps_m", [P, 4 * P])

        w_in = sem("w_in")
        w_ready = sem("w_ready")
        w_step = sem("w_step")
        x_in_s = sem("x_in_s")
        x_free = sem("x_free")
        ln_step = sem("ln_step")
        rstd_ok = sem("rstd_ok")
        pm = sem("pm")
        pm_free = sem("pm_free")
        om = sem("om")
        om_free = sem("om_free")
        hi_ok = sem("hi_ok")
        rem_ok = sem("rem_ok")
        mid_ok = sem("mid_ok")
        lo_ok = sem("lo_ok")
        parts_w = sem("parts_w")
        k6_in = sem("k6_in")
        q6_in = sem("q6_in")
        ge_ok = sem("ge_ok")
        g_step = sem("g_step")
        v_ok = sem("v_ok")
        cur_ok = sem("cur_ok")
        rel_step = sem("rel_step")
        rel_d = sem("rel_d")
        rel_exp = sem("rel_exp")
        rel_sum = sem("rel_sum")
        rel_y0 = sem("rel_y0")
        rel_t = sem("rel_t")
        rel_y = sem("rel_y")
        p_ok = sem("p_ok")
        u_ok = sem("u_ok")
        w_ok = sem("w_ok")
        qk_ok = sem("qk_ok")
        s_ok = sem("s_ok")
        e_ok = sem("e_ok")
        t_ok = sem("t_ok")
        at_ok = sem("at_ok")
        pv_ok = sem("pv_ok")
        o_ok = sem("o_ok")
        rinv_ok = sem("rinv_ok")
        xr_in = sem("xr_in")
        xrb_ok = sem("xrb_ok")
        st = sem("st")
        pool_own, dve_own, sp_own, act_own = (sem(f"{e}_own") for e in ("pool", "dve", "sp", "act"))

        def pool_rstd(pool, p):
            alone(pool, ln_step, 3 * p + 3, pool_own)
            nc.gpsimd.tensor_tensor(rstd[:], ve[:], mhalf[:], ALU.pow).then_inc(rstd_ok, 1)

        def pool_rem(pool, p):
            alone(pool, hi_ok, p + 1, pool_own)
            nc.gpsimd.tensor_tensor(qkf[:], qkf[:], parts[:, 0], ALU.subtract).then_inc(rem_ok, 1)

        def pool_lo(pool, p):
            alone(pool, mid_ok, p + 1, pool_own)
            nc.gpsimd.tensor_tensor(parts[:, 2], qkf[:], parts[:, 1], ALU.subtract).then_inc(lo_ok, 1)

        def pool_rel(pool, t, k, n):
            alone(pool, rel_step, 2 * t + 2, pool_own)
            d = Dj[:, n:n + 1, bass.ds(((t // NT) % 2) * S, S)].rearrange("p a s -> p (a s)")
            nc.gpsimd.tensor_tensor((R[k][1], R2)[n][:], d, RT[:], ALU.subtract).then_inc(rel_d, 1)

        def pool_sum(pool, t, k, n):
            if n == 0:
                alone(pool, rel_exp, 3 * t + 3, pool_own)
                nc.gpsimd.tensor_tensor(RT[:], R[k][0][:], R[k][1][:], ALU.add).then_inc(rel_sum, 1)
            else:
                alone(pool, rel_sum, 2 * t + 1, pool_own)
                nc.gpsimd.tensor_tensor(RT[:], RT[:], R2[:], ALU.add).then_inc(rel_sum, 1)

        def pool_t(pool, t):
            alone(pool, rel_y0, 2 * t + 2, pool_own)
            nc.gpsimd.tensor_tensor(RT[:], RT[:], R2[:], ALU.mult).then_inc(rel_t, 1)

        def pool_p(pool, t, k, n):
            if n == 0:
                alone(pool, rel_y, t + 1, pool_own)
            nc.gpsimd.tensor_tensor(R[k][n][:], R[k][n][:], R2[:], ALU.mult).then_inc(p_ok, 1)

        def pool_u(pool, t, k, h):
            U = H * t + h
            if h == 0:
                alone(pool, p_ok, 2 * t + 2, pool_own)
            alone(pool, t_ok, 2 * U + 2, pool_own)
            nc.gpsimd.tensor_scalar(rows_sb[h % NROW][:], R[k][0][:], cur[k][:, h:h + 1],
                                    cur[k][:, 2 * H + h:2 * H + h + 1], ALU.mult, ALU.add).then_inc(u_ok, 1)

        def pool_xrb(pool, o):
            alone(pool, xr_in, 16 * o + 16, pool_own)
            nc.gpsimd.tensor_tensor(xr[:], xr[:], b_o, ALU.add).then_inc(xrb_ok, 1)

        def dve_ln(dve, p, k):
            wait(dve, x_in_s, 16 * p + 16)
            nc.vector.bn_stats(stats[:], xt[:, k, :]).then_inc(ln_step, 1)
            alone(dve, ln_step, 3 * p + 1, dve_own)
            nc.vector.bn_aggr(mv[:], stats[:]).then_inc(ln_step, 1)
            dve.wait_ge(ln_step, 3 * p + 2)
            nc.vector.tensor_scalar(ve[:], mv[:, 1:2], LN_EPS, None, ALU.add).then_inc(ln_step, 1)

        def dve_xn(dve, p, k):
            wait(dve, rstd_ok, p + 1)
            nc.vector.tensor_scalar(xn[:], xt[:, k, :], mv[:, 0:1], rstd[:, 0:1],
                                    ALU.subtract, ALU.mult).then_inc(x_free, 1)

        def dve_qk(dve, p):
            wait(dve, pm, 4 * p + 2)
            nc.vector.tensor_tensor(qkf[:], ps_m[:].rearrange("p (m t) -> p m t", m=4),
                                    b_qk[:].unsqueeze(2).broadcast_to([P, 4, P]), ALU.add).then_inc(pm_free, 1)

        def dve_v(dve, p, par, ib):
            wait(dve, pm, 4 * p + 4)
            nc.vector.tensor_tensor(V[par][:, bass.ds(ib, 1), 0:D], ps_m[:, 0:D].unsqueeze(1),
                                    b_v.unsqueeze(1), ALU.add).then_inc(v_ok, 1)
            nc.vector.tensor_tensor(zg[:], ps_m[:, D:D + H + 2], b_misc[:], ALU.add).then_inc(pm_free, 1)

        def dve_gate(dve, p, par, ib):
            wait(dve, ge_ok, p + 1)
            nc.vector.tensor_scalar(ge[:], ge[:], 1.0, None, ALU.add).then_inc(g_step, 1)
            dve.wait_ge(g_step, 4 * p + 1)
            nc.vector.reciprocal(gate[:], ge[:]).then_inc(g_step, 1)
            dve.wait_ge(g_step, 4 * p + 2)
            idx = par * NT + ib
            nc.vector.tensor_tensor(small[:, bass.ds(idx, 1), 0:3 * H].rearrange("p o (k h) -> p (o k) h", k=3),
                                    lbd[:], gate[:].unsqueeze(1).broadcast_to([P, 3, H]), ALU.mult).then_inc(g_step, 1)
            nc.vector.tensor_scalar(small[:, bass.ds(idx, 1), 3 * H:3 * H + 2], zg[:, H:H + 2].unsqueeze(1),
                                    1.0, None, ALU.mult).then_inc(g_step, 1)

        def dve_rel(dve, t, k, step):
            d10, d20 = (Dj[:, i:i + 1, bass.ds(((t // NT) % 2) * S, S)].rearrange("p a s -> p (a s)") for i in range(2))
            a10, a20 = (cur[k][:, 3 * H + i:3 * H + i + 1] for i in range(2))
            if step == 0:
                wait(dve, g_step, 4 * (t + 1))
                wait(dve, u_ok, H * (t - 1))
                nc.vector.tensor_scalar(cur[k][:].unsqueeze(1), small[:, bass.ds(t % (2 * NT), 1), :],
                                        1.0, None, ALU.mult).then_inc(cur_ok, 1)
                dve.wait_ge(cur_ok, t + 1)
                wait(dve, pm_free, 4 * (NT * (t // NT) + NT) - 1)
                wait(dve, p_ok, 2 * t)
                nc.vector.tensor_scalar(RT[:], d10, a10, 0.0, ALU.add, ALU.max).then_inc(rel_step, 1)
            elif step == 1:
                dve.wait_ge(rel_step, 2 * t + 1)
                nc.vector.scalar_tensor_tensor(RT[:], d20, a20, RT[:], ALU.add, ALU.max).then_inc(rel_step, 1)

        def dve_y(dve, t):
            wait(dve, rel_t, t + 1)
            nc.vector.scalar_tensor_tensor(R2[:], RT[:], 2.0, R2[:], ALU.subtract, ALU.mult).then_inc(rel_y, 1)

        def dve_w(dve, t, k, h):
            wait(dve, u_ok, H * t + h + 1)
            r = rows_sb[h % NROW]
            nc.vector.scalar_tensor_tensor(r[:], R[k][1][:], cur[k][:, H + h:H + h + 1], r[:],
                                           ALU.mult, ALU.add).then_inc(w_ok, 1)

        def dve_s(dve, t, h):
            wait(dve, w_ok, H * t + h + 1)
            alone(dve, qk_ok, H * t + h + 1, dve_own)
            r = rows_sb[h % NROW]
            nc.vector.tensor_tensor_reduce(r[:], r[:], ps_s[:, h % 2, :], -1.0, BIG, ALU.add, ALU.min,
                                           nmax[:, h % NROW:h % NROW + 1]).then_inc(s_ok, 1)

        def dve_norm(dve, o, k):
            wait(dve, e_ok, H * (o + 1))
            nc.vector.reciprocal(rinv[:], rsum[:, k, :]).then_inc(rinv_ok, 1)
            dve.wait_ge(rinv_ok, o + 1)
            wait(dve, om, 3 * o + 1)
            nc.vector.tensor_tensor(attn[:].rearrange("p (h d) -> p h d", d=HD),
                                    ps_m[:].rearrange("p (h e) -> p h e", e=32)[:, :, 0:HD],
                                    rinv[:].unsqueeze(2).broadcast_to([P, H, HD]), ALU.mult).then_inc(om_free, 1)

        def dve_out(dve, o):
            wait(dve, xrb_ok, o + 1)
            wait(dve, om, 3 * o + 3)
            nc.vector.tensor_tensor(xr[:], ps_m[:, 0:D], xr[:], ALU.add).then_inc(om_free, 1)

        def act_xT(act, p):
            wait(act, pm, 4 * p + 1)
            nc.scalar.copy(xnT[:].rearrange("p c t -> p (c t)"), ps_m[:, 0:D]).then_inc(pm_free, 1)

        def act_d(act, p):
            alone(act, pm, 4 * p + 3, act_own)
            nc.scalar.copy(Dj[:, :, bass.ds((p % (2 * NT)) * P, P)],
                           ps_m[:, 0:2 * P].rearrange("p (k t) -> p k t", k=2)).then_inc(pm_free, 1)

        def act_hi(act, p):
            wait(act, parts_w, 16 * p + 16)
            wait(act, pm_free, 4 * p + 2 + 1)
            nc.scalar.copy(parts[:, 0], qkf[:]).then_inc(hi_ok, 1)

        def act_mid(act, p):
            wait(act, rem_ok, p + 1)
            nc.scalar.copy(parts[:, 1], qkf[:]).then_inc(mid_ok, 1)

        def act_gate(act, p):
            wait(act, pm_free, 4 * p + 4 + 1)
            nc.scalar.activation(ge[:], zg[:, 0:H], ACT.Exp, scale=-1.0).then_inc(ge_ok, 1)

        def act_rel(act, t, k, step):
            if step == 0:
                wait(act, rel_step, 2 * t + 2)
                nc.scalar.activation(R[k][0][:], RT[:], ACT.Exp, scale=-1.0).then_inc(rel_exp, 1)
            else:
                wait(act, rel_d, 2 * t + step)
                dst = (R[k][1], R2)[step - 1]
                nc.scalar.activation(dst[:], dst[:], ACT.Exp,
                                     bias=cur[k][:, 3 * H + step - 1:3 * H + step]).then_inc(rel_exp, 1)

        def act_y0(act, t):
            wait(act, rel_sum, 2 * t + 2)
            nc.scalar.activation(R2[:], RT[:], ACT.Ln).then_inc(rel_y0, 1)
            act.wait_ge(rel_y0, 2 * t + 1)
            nc.scalar.activation(R2[:], R2[:], ACT.Exp, scale=-1.0).then_inc(rel_y0, 1)

        def act_e(act, t, k, h):
            wait(act, s_ok, H * t + h + 1)
            r = rows_sb[h % NROW]
            nc.scalar.activation(r[:], r[:], ACT.Exp, scale=-1.0, bias=nmax[:, h % NROW:h % NROW + 1],
                                 accum_out=rsum[:, k, h:h + 1]).then_inc(e_ok, 1)

        def act_at(act, t, h):
            U = H * t + h
            if h % HG == 0:
                wait(act, pv_ok, U // HG + 1 if isinstance(U, int) else HG * t + h // HG + 1)
            for half in range(2):
                wait(act, t_ok, 2 * NROW + 2 * U + half + 1)
                nc.scalar.copy(AT[h % NAT][:, HG * half:HG * half + HG, :], ps_t[:, half]).then_inc(at_ok, 1)

        def act_o(act, o):
            wait(act, pv_ok, 2 + HG * (o + 1))
            nc.scalar.copy(O4[:], ps_o[:]).then_inc(o_ok, 1)

        def act_aT(act, o):
            wait(act, om, 3 * o + 2)
            nc.scalar.copy(attnT[:].rearrange("p c t -> p (c t)"), ps_m[:, 0:D]).then_inc(om_free, 1)

        def pe_m(pe, p, i, o_done):
            wait(pe, pm_free, 4 * p + i + 1)
            wait(pe, om_free, o_done + 1)

        def pe_xT(pe, p, o_done):
            wait(pe, x_free, p + 1 + 2)
            pe_m(pe, p, 0, o_done)
            for c in range(DC):
                last = nc.tensor.transpose(ps_m[:, c * P:(c + 1) * P], xn[:, c * P:(c + 1) * P], ident[:])
            last.then_inc(pm, 1)

        def pe_qk_proj(pe, p, o_done):
            pe_m(pe, p, 1, o_done)
            for m in range(4):
                for c in range(DC):
                    last = nc.tensor.matmul(ps_m[:, m * P:(m + 1) * P], w_qk[:, c, m * P:(m + 1) * P],
                                            xnT[:, c, :], start=(c == 0), stop=(c == DC - 1))
            last.then_inc(pm, 1)

        def pe_d(pe, p, o_done):
            pe_m(pe, p, 2, o_done)
            for i in range(2):
                for c in range(DC):
                    last = nc.tensor.matmul(ps_m[:, i * P:(i + 1) * P], w_dj[:, c, i, :],
                                            xnT[:, c, :], start=(c == 0), stop=(c == DC - 1))
            last.then_inc(pm, 1)

        def pe_v(pe, p, o_done):
            pe_m(pe, p, 3, o_done)
            for c in range(DC):
                last = nc.tensor.matmul(ps_m[:, 0:D + H + 2], xnT[:, c, :], w_vg[:, c, 0:D + H + 2],
                                        start=(c == 0), stop=(c == DC - 1))
            last.then_inc(pm, 1)

        def pe_s(pe, t, k, h):
            U = H * t + h
            if h == 0:
                wait(pe, q6_in, 96 * (t + 1))
            if h % HG == 0:
                wait(pe, k6_in, 96 * (HG * (t // NT) + h // HG + 1))
            wait(pe, s_ok, U - 1)
            for n in range(2):
                last = nc.tensor.matmul(ps_s[:, h % 2, n * 512:(n + 1) * 512], Q6[k][:, h, :],
                                        K6[:, h, n * 512:(n + 1) * 512], start=True, stop=True)
            last.then_inc(qk_ok, 1)

        def pe_t(pe, t, h):
            U = H * t + h
            wait(pe, e_ok, U + 1)
            for half in range(2):
                wait(pe, at_ok, 2 * U + half + 1)
                for i in range(HG):
                    j = HG * half + i
                    last = nc.tensor.transpose(ps_t[:, half, i, :], rows_sb[h % NROW][:, j * P:(j + 1) * P], ident[:])
                last.then_inc(t_ok, 1)

        def pe_pv(pe, t, par, j):
            if j == 0:
                wait(pe, o_ok, t)
                wait(pe, v_ok, 2 + NT * (t // NT + 1))
            wait(pe, at_ok, 2 + 2 * (H * t + HG * j + HG))
            for n in range(NT):
                for i in range(HG):
                    h = HG * j + i
                    last = nc.tensor.matmul(ps_o[32 * i:32 * i + 32, j, :], V[par][:, n, HD * h:HD * h + 32],
                                            AT[h % NAT][:, n, :], start=(n == 0), stop=(n == NT - 1))
            last.then_inc(pv_ok, 1)

        def pe_oT(pe, o, p_done):
            wait(pe, o_ok, o + 1)
            wait(pe, pm_free, p_done + 1)
            wait(pe, om_free, 3 * o + 1)
            for j in range(HG):
                last = nc.tensor.transpose(ps_m[:, j * P:(j + 1) * P], O4[:, j, :], ident[:])
            last.then_inc(om, 1)

        def pe_aT(pe, o, p_done):
            wait(pe, pm_free, p_done + 1)
            wait(pe, om_free, 3 * o + 2)
            for c in range(DC):
                last = nc.tensor.transpose(ps_m[:, c * P:(c + 1) * P], attn[:, c * P:(c + 1) * P], ident[:])
            last.then_inc(om, 1)

        def pe_wo(pe, o, p_done):
            wait(pe, pm_free, p_done + 1)
            wait(pe, om_free, 3 * o + 3)
            for c in range(DC):
                last = nc.tensor.matmul(ps_m[:, 0:D], attnT[:, c, :], w_o[:, c, :],
                                        start=(c == 0), stop=(c == DC - 1))
            last.then_inc(om, 1)

        parts_v = parts_d.rearrange("k (m p) t -> p k m t", p=P)

        def sp_x(sp, p, k):
            alone(sp, x_in_s, 16 * p, sp_own)
            alone(sp, x_free, p + 1, sp_own)
            sp.dma_start(xt[:, k, :], x_in[bass.ds((p % TILES) * P, P), :]).then_inc(x_in_s, 16)

        def sp_parts(sp, p):
            alone(sp, parts_w, 16 * p + 16, sp_own)
            alone(sp, lo_ok, p + 1, sp_own)
            sp.dma_start(parts_v[:, :, :, bass.ds((p % TILES) * P, P)], parts[:]).then_inc(parts_w, 16)

        def sp_keys(sp, b):
            alone(sp, parts_w, 16 * NT * (b + 1) + 16, sp_own)
            for g in range(HG):
                alone(sp, k6_in, 96 * (HG * b + g), sp_own)
                alone(sp, qk_ok, H * (NT * b - 1) + HG * g + HG, sp_own)
                for s, part in enumerate(K_PART):
                    sp.dma_start(K6[HD * s:HD * s + HD, HG * g:HG * g + HG, :],
                                 parts_d[part, D + g * HG * HD:D + (g + 1) * HG * HD, bass.ds(b * S, S)
                                         ].rearrange("(h d) t -> d h t", d=HD)).then_inc(k6_in, 16)

        def sp_q6(sp, t, k):
            alone(sp, q6_in, 96 * t, sp_own)
            alone(sp, qk_ok, H * (t - 1), sp_own)
            for s, part in enumerate(Q_PART):
                sp.dma_start(Q6[k][HD * s:HD * s + HD, :, :],
                             parts_d[part, 0:D, bass.ds(t * P, P)].rearrange("(h d) t -> d h t", d=HD)
                             ).then_inc(q6_in, 16)

        def sp_xr(sp, o):
            alone(sp, st, 16 * o, sp_own)
            sp.dma_start(xr[:], x_in[bass.ds(o * P, P), :]).then_inc(xr_in, 16)

        def sp_out(sp, o):
            alone(sp, om_free, 3 * o + 4, sp_own)
            sp.dma_start(x_out[bass.ds(o * P, P), :], xr[:]).then_inc(st, 16)

        def run(eng, start, project, body, finish, ends=False):
            def pairs(first, start_i, par, b):
                with eng.Fori(start_i, NT // 2 - ends) as i:
                    for k in range(2):
                        body(eng, first + 2 * i + k, k, par, 2 * i + k, True, True, True)
                for k in range(2 * ends):
                    t = first + NT - 2 + k
                    body(eng, t, k, par, NT - 2 + k, True, True, True, **({"batch": b + 1} if k else {}))

            with eng.Fori(0, NT // 2) as i:
                for k in range(2):
                    project(eng, 2 * i + k, k, 0, 2 * i + k)
            start(eng)
            for k in range(2):
                body(eng, k, k, 0, k, True, k > 0, True)
            pairs(0, 1, 0, 0)
            with eng.Fori(0, (B - 2) // 2) as j:
                for par in (1, 0):
                    b = 2 * j + (1 if par else 2)
                    pairs(b * NT, 0, par, b)
            with eng.Fori(0, NT // 2 - 1) as i:
                for k in range(2):
                    body(eng, (B - 1) * NT + 2 * i + k, k, 1, 2 * i + k, False, True, True)
            for k in range(2):
                body(eng, TILES - 2 + k, k, 1, NT - 2 + k, False, True, k == 0)
            finish(eng)

        block = ctx.enter_context(nc.Block())

        @block.sync
        def _(sp):
            def project(sp, p, k, par, ib):
                sp_x(sp, p + 1, 1 - k)
                sp_parts(sp, p)

            def start(sp):
                sp_keys(sp, 0)
                sp_q6(sp, 0, 0)
                sp_parts(sp, NT)

            def body(sp, t, k, par, ib, pro, post, look, batch=None):
                if pro:
                    sp_x(sp, t + AHEAD, 1 - k)
                if look:
                    sp_q6(sp, t + 1, 1 - k)
                if not isinstance(t, int) or t >= 2:
                    sp_out(sp, t - 2)
                if post:
                    sp_xr(sp, t - 1)
                if batch is not None:
                    sp_keys(sp, batch)
                if pro:
                    sp_parts(sp, t + AHEAD)

            def finish(sp):
                sp_out(sp, TILES - 2)
                sp_xr(sp, TILES - 1)
                sp_out(sp, TILES - 1)
                sp.wait_ge(st, 16 * TILES)

            for dst, src in ((w_qk[:], wqk.rearrange("(c p) n -> p c n", p=P)),
                             (w_vg[:], wvg[:, 0:D + H + 6].rearrange("(c p) n -> p c n", p=P)),
                             (w_o[:], wvg[:, D + H + 6:].rearrange("(c p) n -> p c n", p=P)),
                             (b_qk[:], bqk), (row[:], rows.partition_broadcast(P)), (ident[:], ident_in)):
                sp.dma_start(dst, src).then_inc(w_in, 16)
            sp.sem_inc(parts_w, 16)
            sp_x(sp, 0, 0)
            run(sp, start, project, body, finish, ends=True)

        @block.gpsimd
        def _(pool):
            def project(pool, p, k, par, ib):
                pool_rstd(pool, p)
                pool_rem(pool, p)
                pool_lo(pool, p)

            def start(pool):
                project(pool, NT, 0, 1, 0)
                pool_rel(pool, 0, 0, 0)
                pool_rel(pool, 0, 0, 1)
                pool_sum(pool, 0, 0, 0)
                pool_sum(pool, 0, 0, 1)
                pool_t(pool, 0)
                pool_p(pool, 0, 0, 0)
                pool_p(pool, 0, 0, 1)
                for h in range(LEAD):
                    pool_u(pool, 0, 0, h)

            def body(pool, t, k, par, ib, pro, post, look):
                for u in range(H):
                    if u + LEAD < H:
                        pool_u(pool, t, k, u + LEAD)
                    elif look:
                        pool_u(pool, t + 1, 1 - k, u + LEAD - H)
                    if pro and u == 2:
                        pool_rstd(pool, t + AHEAD)
                    if look and u in (1, 2):
                        pool_rel(pool, t + 1, 1 - k, u - 1)
                    if look and u in (5, 6):
                        pool_sum(pool, t + 1, 1 - k, u - 5)
                    if look and u == 7:
                        pool_t(pool, t + 1)
                    if pro and u == 10:
                        pool_rem(pool, t + AHEAD)
                    if look and u in (9, 11):
                        pool_p(pool, t + 1, 1 - k, (u - 9) // 2)
                    if pro and u == 12:
                        pool_lo(pool, t + AHEAD)
                    if post and u == 4:
                        pool_xrb(pool, t - 1)

            def finish(pool):
                pool_xrb(pool, TILES - 1)

            nc.gpsimd.memset(mhalf[:], -0.5)
            for v in V:
                nc.gpsimd.memset(v[:, :, D:D + HD], 0.0).then_inc(v_ok, 1)
            pool.wait_ge(v_ok, 2)
            run(pool, start, project, body, finish)

        @block.vector
        def _(dve):
            def front(dve, p, k):
                dve_ln(dve, p, k)
                dve_xn(dve, p, k)
                dve_qk(dve, p)

            def project(dve, p, k, par, ib):
                front(dve, p, k)
                dve_v(dve, p, par, ib)
                dve_gate(dve, p, par, ib)

            def start(dve):
                front(dve, NT, 0)
                for step in range(2):
                    dve_rel(dve, 0, 0, step)
                dve_y(dve, 0)
                dve_w(dve, 0, 0, 0)

            def body(dve, t, k, par, ib, pro, post, look):
                for u in range(H):
                    if u + 1 < H:
                        dve_w(dve, t, k, u + 1)
                    elif look:
                        dve_w(dve, t + 1, 1 - k, 0)
                    dve_s(dve, t, u)
                    if u == 0 and (not isinstance(t, int) or t >= 2):
                        dve_out(dve, t - 2)
                    if look and u < 2:
                        dve_rel(dve, t + 1, 1 - k, u)
                    if pro and u == 1:
                        dve_ln(dve, t + AHEAD, 1 - k)
                    if pro and u == 3:
                        dve_v(dve, t + NT, 1 - par, ib)
                    if pro and u == 4:
                        dve_xn(dve, t + AHEAD, 1 - k)
                    if post and u == 6:
                        dve_norm(dve, t - 1, 1 - k)
                    if pro and u == 7:
                        dve_gate(dve, t + NT, 1 - par, ib)
                    if pro and u == 9:
                        dve_qk(dve, t + AHEAD)
                    if look and u == 9:
                        dve_y(dve, t + 1)

            def finish(dve):
                dve_out(dve, TILES - 2)
                dve_norm(dve, TILES - 1, 1)
                dve_out(dve, TILES - 1)

            dve.wait_ge(w_in, 16 * 6)
            nc.vector.tensor_scalar(w_qk[:, :, 0:D], w_qk[:, :, 0:D], 1.0 / HD ** 0.5, None, ALU.mult)
            nc.vector.tensor_scalar(b_qk[:, 0:DC], b_qk[:, 0:DC], 1.0 / HD ** 0.5, None, ALU.mult)
            ri, rj = D + H, D + H + 3
            for i in range(2):
                nc.vector.tensor_tensor(w_dj[:, :, i, :], w_vg[:, :, rj + 1 + i:rj + 2 + i].broadcast_to([P, DC, P]),
                                        w_vg[:, :, rj:rj + 1].broadcast_to([P, DC, P]), ALU.subtract)
                nc.vector.tensor_tensor(b_misc[:, H + i:H + i + 1], b_g[:, H + 1 + i:H + 2 + i], b_g[:, H:H + 1],
                                        ALU.subtract)
                nc.vector.tensor_tensor(lbd[:, i, :], lbk[:, 2, :], lbk[:, i, :], ALU.subtract)
            nc.vector.tensor_copy(b_misc[:, 0:H], b_g[:, 0:H])
            nc.vector.tensor_copy(lbd[:, 2, :], lbk[:, 2, :]).then_inc(w_step, 1)
            dve.wait_ge(w_step, 1)
            nc.vector.tensor_tensor(rinv[:, 0:DC], w_vg[:, :, ri + 1], w_vg[:, :, ri], ALU.subtract)
            nc.vector.tensor_tensor(rinv[:, DC:2 * DC], w_vg[:, :, ri + 2], w_vg[:, :, ri], ALU.subtract
                                    ).then_inc(w_step, 1)
            dve.wait_ge(w_step, 2)
            nc.vector.tensor_copy(w_vg[:, :, ri], rinv[:, 0:DC])
            nc.vector.tensor_copy(w_vg[:, :, ri + 1], rinv[:, DC:2 * DC]).then_inc(w_ready, 1)
            dve.wait_ge(w_ready, 1)
            dve.sem_inc(x_free, 2)
            dve.sem_inc(pm_free, 1)
            dve.sem_inc(om_free, 1)
            run(dve, start, project, body, finish)

        @block.scalar
        def _(act):
            def front(act, p):
                act_xT(act, p)
                act_hi(act, p)
                act_d(act, p)
                act_mid(act, p)

            def project(act, p, k, par, ib):
                act_xT(act, p)
                act_hi(act, p)
                act_d(act, p)
                act_gate(act, p)
                act_mid(act, p)

            def start(act):
                front(act, NT)
                for step in range(3):
                    act_rel(act, 0, 0, step)
                act_y0(act, 0)

            def body(act, t, k, par, ib, pro, post, look):
                for u in range(H):
                    act_e(act, t, k, u)
                    if u:
                        act_at(act, t, u - 1)
                    if post and u == 1:
                        act_o(act, t - 1)
                    if look and u in (1, 3, 4):
                        act_rel(act, t + 1, 1 - k, (1, 3, 4).index(u))
                    if pro and u == 5:
                        act_gate(act, t + NT)
                    if pro and u == 6:
                        act_xT(act, t + AHEAD)
                    if look and u == 7:
                        act_y0(act, t + 1)
                    if pro and u == 9:
                        act_hi(act, t + AHEAD)
                    if pro and u == 10:
                        act_d(act, t + AHEAD)
                    if pro and u == 11:
                        act_mid(act, t + AHEAD)
                    if post and u == 12:
                        act_aT(act, t - 1)
                act_at(act, t, H - 1)

            def finish(act):
                act_o(act, TILES - 1)
                act_aT(act, TILES - 1)

            act.preload_act_table_set("natural_log_exp_and_others")
            act.sem_inc(at_ok, 2)
            run(act, start, project, body, finish)

        @block.tensor
        def _(pe):
            def front(pe, p):
                pe_xT(pe, p, 0)
                pe_qk_proj(pe, p, 0)
                pe_d(pe, p, 0)

            def project(pe, p, k, par, ib):
                front(pe, p)
                pe_v(pe, p, 0)

            def start(pe):
                front(pe, NT)
                for h in range(3):
                    pe_s(pe, 0, 0, h)

            def body(pe, t, k, par, ib, pro, post, look):
                o = t - 1
                p = t + AHEAD
                om_done = 3 * o if post else 0
                om_next = om_done + 1 if post else 0
                last_p = 4 * TILES + 3
                for u in range(H):
                    if u and u + 2 < H:
                        pe_s(pe, t, k, u + 2)
                    elif u and look:
                        pe_s(pe, t + 1, 1 - k, u + 2 - H)
                    pe_t(pe, t, u)
                    if u and u % HG == 0:
                        pe_pv(pe, t, par, u // HG - 1)
                    if pro and u == 1:
                        pe_v(pe, p - 1, om_done)
                    if post and u == 3:
                        pe_oT(pe, o, 4 * p if pro else last_p)
                    if pro and u == 5:
                        pe_xT(pe, p, om_next)
                    if pro and u == 7:
                        pe_qk_proj(pe, p, om_next)
                    if pro and u == 9:
                        pe_d(pe, p, om_next)
                    if post and u == 11:
                        pe_aT(pe, o, 4 * p + 3 if pro else last_p)
                    if post and u == 13:
                        pe_wo(pe, o, 4 * p + 3 if pro else last_p)
                if look:
                    pe_s(pe, t + 1, 1 - k, 2)
                pe_pv(pe, t, par, HG - 1)

            def finish(pe):
                pe_oT(pe, TILES - 1, 4 * TILES + 3)
                pe_aT(pe, TILES - 1, 4 * TILES + 3)
                pe_wo(pe, TILES - 1, 4 * TILES + 3)

            pe.wait_ge(w_ready, 1)
            pe.sem_inc(t_ok, 2 * NROW)
            pe.sem_inc(pv_ok, 2)
            run(pe, start, project, body, finish)


G = 4
GROUPS = TILES // G
GT = G * P


def norm_stats(nc, dve, x, stats, mv, ve, step, base, own):
    for i in range(G):
        last = nc.vector.bn_stats(stats[:, i, :], x[:, i, :])
    last.then_inc(step, 1)
    alone(dve, step, base + 1, own)
    for i in range(G):
        last = nc.vector.bn_aggr(mv[:, i, :], stats[:, i, :])
    last.then_inc(step, 1)
    dve.wait_ge(step, base + 2)
    nc.vector.tensor_scalar(ve[:].unsqueeze(2), mv[:, :, 1:2], LN_EPS, None, ALU.add).then_inc(step, 1)


def norm_apply(nc, dve, out, x, mv, rstd):
    for i in range(G):
        last = nc.vector.tensor_scalar(out[:, i, :], x[:, i, :], mv[:, i, 0:1], rstd[:, i:i + 1],
                                               ALU.subtract, ALU.mult)
    return last


def fp8_layer(nc, x_in, w8, scales, col, bias, ident_in, x_out, xc_out, xl_out):
    with ExitStack() as ctx:
        sb = lambda name, shape, dt=F32: ctx.enter_context(nc.sbuf_tensor(name, shape, dt))
        sem = lambda name: ctx.enter_context(nc.semaphore(name))
        ident = sb("b_ident", [P, P])
        w = sb("b_w", [P, DC, D])
        sc = sb("b_sc", [P, 2])
        rs = sb("b_rs", [P, 1])
        ln_w = sb("b_ln_w", [P, DC])
        b_row = sb("b_row", [P, 1, D])
        mhalf = sb("b_mhalf", [P, G])
        xt = [sb(f"b_xt{i}", [P, G, D]) for i in range(2)]
        xb = sb("b_xb", [P, G, D])
        stats = sb("b_stats", [P, G, 6])
        mv = sb("b_mv", [P, G, 2])
        ve = sb("b_ve", [P, G])
        rstd = sb("b_rstd", [P, G])
        xn = sb("b_xn", [P, G, D])
        mag = sb("b_mag", [P, G, D])
        xq = sb("b_xq", [P, G, D])
        xT = sb("b_xT", [P, G // 2, 2, DC, P])
        x2 = sb("b_x2", [P, G, D])
        xc = sb("b_xc", [P, G, D])
        x3 = sb("b_x3", [P, G, D])
        xl = sb("b_xl", [P, DC, G, P])
        ps_t = [ctx.enter_context(nc.psum_tensor(f"b_ps_t{i}", [P, 2, DC, P], F32)) for i in range(2)]
        ps_y = [ctx.enter_context(nc.psum_tensor(f"b_ps_y{i}", [P, 2, D], F32)) for i in range(2)]
        w_in, w_ok = sem("b_w_in"), sem("b_w_ok")
        x_in_s, x_free = sem("b_x_in"), sem("b_x_free")
        step, r_ok, q_step = sem("b_step"), sem("b_r_ok"), sem("b_q_step")
        xb_ok, xb_free = sem("b_xb_ok"), sem("b_xb_free")
        t_ok, t_free = sem("b_t_ok"), sem("b_t_free")
        y_ok, y_free = sem("b_y_ok"), sem("b_y_free")
        xc_ok, xq_ok = sem("b_xc_ok"), sem("b_xq_ok")
        stored = sem("b_stored")
        pool_own, dve_own, sp_own, act_own = (sem(f"b_{e}_own") for e in ("pool", "dve", "sp", "act"))
        block = ctx.enter_context(nc.Block())

        def loop(eng, body):
            with eng.Fori(0, GROUPS // 2 - 1) as i:
                for k in range(2):
                    body(2 * i + k, k, 2)
            for k in range(2):
                body(GROUPS - 2 + k, k, 1 - k)

        FIRST = lambda g, per: per * g - (per - 1) if not isinstance(g, int) or g else 0
        LATER = lambda g, per, ahead: per * g + (2 if ahead else 1)

        @block.sync
        def _(sp):
            for dst, src in ((w[:], w8.rearrange("(c p) n -> p c n", p=P)), (sc[:], scales.partition_broadcast(P)),
                             (ln_w[:], col), (b_row[:, 0], bias.partition_broadcast(P)), (ident[:], ident_in)):
                sp.dma_start(dst, src).then_inc(w_in, 16)
            sp.sem_inc(stored, 48)

            def load(g, k):
                alone(sp, x_in_s, 16 * g, sp_own)
                sp.dma_start(xt[k][:], x_in[bass.ds(g * GT, GT), :].rearrange("(i p) d -> p i d", p=P)).then_inc(x_in_s, 16)

            def body(g, k, ahead):
                tok = bass.ds(g * GT, GT)
                if ahead == 2:
                    alone(sp, x_free, g + 1, sp_own)
                    alone(sp, xb_ok, g + 1, sp_own)
                    load(g + 2, k)
                alone(sp, xc_ok, g + 1, sp_own)
                sp.dma_start(x_out[tok, :].rearrange("(i p) d -> p i d", p=P), x2[:]).then_inc(stored, 16)
                sp.dma_start(xc_out[tok, :].rearrange("(i p) d -> p i d", p=P), xc[:]).then_inc(stored, 16)
                alone(sp, t_free, 2 * LATER(g, 2, ahead) + 2 + 2, sp_own)
                sp.dma_start(xl_out[:, tok].rearrange("(c p) t -> p c t", p=P),
                             xl[:].rearrange("p c i t -> p c (i t)")).then_inc(stored, 16)

            load(0, 0)
            load(1, 1)
            loop(sp, body)
            sp.wait_ge(stored, 48 * GROUPS + 48)

        @block.gpsimd
        def _(pool):
            nc.gpsimd.memset(mhalf[:], -0.5).then_inc(pool_own, 1)
            pool.wait_ge(pool_own, 1)
            pool.wait_ge(w_in, 16 * 5)

            def power(n):
                alone(pool, step, 3 * n + 3, pool_own)
                nc.gpsimd.tensor_tensor(rstd[:], ve[:], mhalf[:], ALU.pow).then_inc(r_ok, 1)

            def body(g, k, ahead):
                alone(pool, x_in_s, 16 * g + 16, pool_own)
                alone(pool, xb_free, g + 1, pool_own)
                nc.gpsimd.tensor_tensor(xb[:], xt[k][:], b_row[:].broadcast_to([P, G, D]), ALU.add).then_inc(xb_ok, 1)
                if ahead:
                    power(FIRST(g + 1, 3))
                power(LATER(g, 3, ahead))
                power(LATER(g, 3, ahead) + 1)

            power(0)
            loop(pool, body)

        @block.vector
        def _(dve):
            dve.wait_ge(w_in, 16 * 5)
            nc.vector.reciprocal(rs[:], sc[:, 0:1])
            nc.vector.tensor_scalar(w[:], w[:], sc[:, 1:2], None, ALU.mult).then_inc(w_ok, 1)
            dve.wait_ge(w_ok, 1)
            dve.sem_inc(xb_free, 1)
            dve.sem_inc(y_free, 2)

            def first(g, k):
                n = FIRST(g, 3)
                dve.wait_ge(x_in_s, 16 * g + 16)
                norm_stats(nc, dve, xt[k], stats, mv, ve, step, 3 * n, dve_own)
                dve.wait_ge(r_ok, n + 1)
                norm_apply(nc, dve, xn, xt[k], mv, rstd).then_inc(x_free, 1)
                dve.wait_ge(x_free, g + 1)
                nc.vector.tensor_scalar(xn[:], xn[:], rs[:, 0:1], 448.0, ALU.mult, ALU.min).then_inc(q_step, 1)
                dve.wait_ge(q_step, 5 * g + 1)
                nc.vector.tensor_scalar(xn[:], xn[:], -448.0, None, ALU.max).then_inc(q_step, 1)
                dve.wait_ge(q_step, 5 * g + 2)
                nc.vector.tensor_scalar(mag[:].bitcast(U32), xn[:].bitcast(U32), 0x7F800000, None,
                                        ALU.bitwise_and).then_inc(q_step, 1)
                dve.wait_ge(q_step, 5 * g + 3)
                nc.vector.tensor_scalar(mag[:], mag[:], 2.0 ** -6, 1.5 * 2.0 ** 20, ALU.max, ALU.mult).then_inc(q_step, 1)
                dve.wait_ge(q_step, 5 * g + 4)
                nc.vector.tensor_tensor(xn[:], xn[:], mag[:], ALU.add).then_inc(q_step, 1)
                dve.wait_ge(q_step, 5 * g + 5)
                wait(dve, y_ok, 2 * g)
                nc.vector.tensor_tensor(xq[:], xn[:], mag[:], ALU.subtract).then_inc(xq_ok, 1)

            def body(g, k, ahead):
                n = LATER(g, 3, ahead)
                if ahead:
                    first(g + 1, 1 - k)
                dve.wait_ge(xb_ok, g + 1)
                dve.wait_ge(stored, 48 * g + 48)
                for j in range(2):
                    dve.wait_ge(y_ok, 2 * g + j + 1)
                    nc.vector.tensor_tensor(x2[:, 2 * j:2 * j + 2, :], ps_y[j][:], xb[:, 2 * j:2 * j + 2, :],
                                            ALU.add).then_inc(y_free, 1)
                dve.wait_ge(y_free, 2 * g + 2 + 2)
                norm_stats(nc, dve, x2, stats, mv, ve, step, 3 * n, dve_own)
                dve.wait_ge(r_ok, n + 1)
                norm_apply(nc, dve, xc, x2, mv, rstd).then_inc(xc_ok, 1)
                dve.wait_ge(xc_ok, g + 1)
                norm_stats(nc, dve, xc, stats, mv, ve, step, 3 * n + 3, dve_own)
                dve.wait_ge(r_ok, n + 2)
                dve.wait_ge(t_ok, 4 * g + 2)
                norm_apply(nc, dve, x3, xc, mv, rstd).then_inc(xb_free, 1)

            first(0, 0)
            loop(dve, body)

        @block.scalar
        def _(act):
            act.wait_ge(w_in, 16 * 5)
            act.sem_inc(t_free, 2)

            def first(g):
                for j in range(2):
                    act.wait_ge(t_ok, 2 * FIRST(g, 2) + j + 1)
                    nc.scalar.activation(xT[:, j], ps_t[j][:], ACT.Copy, scale=sc[:, 0:1]).then_inc(t_free, 1)

            def body(g, k, ahead):
                if ahead:
                    first(g + 1)
                act.wait_ge(stored, 48 * g + 48)
                for j in range(2):
                    act.wait_ge(t_ok, 2 * LATER(g, 2, ahead) + j + 1)
                    for c in range(DC):
                        last = nc.scalar.activation(xl[:, c, 2 * j:2 * j + 2, :], ps_t[j][:, :, c, :], ACT.Copy,
                                                    scale=ln_w[:, c:c + 1])
                    last.then_inc(t_free, 1)

            first(0)
            loop(act, body)

        @block.tensor
        def _(pe):
            pe.wait_ge(w_ok, 1)

            def turn(use, src):
                for j in range(2):
                    pe.wait_ge(t_free, 2 * use + j + 1)
                    for i in range(2):
                        for c in range(DC):
                            last = nc.tensor.transpose(ps_t[j][:, i, c, :], src[:, 2 * j + i, c * P:(c + 1) * P],
                                                       ident[:])
                    last.then_inc(t_ok, 1)

            def first(g):
                pe.wait_ge(xq_ok, g + 1)
                turn(FIRST(g, 2), xq)
                for j in range(2):
                    pe.wait_ge(t_free, 2 * FIRST(g, 2) + j + 1 + 2)
                    pe.wait_ge(y_free, 2 * g + j + 1)
                    for i in range(2):
                        for c in range(DC):
                            last = nc.tensor.matmul(ps_y[j][:, i, :], xT[:, j, i, c, :], w[:, c, :],
                                                    start=(c == 0), stop=(c == DC - 1))
                    last.then_inc(y_ok, 1)

            def body(g, k, ahead):
                if ahead:
                    first(g + 1)
                pe.wait_ge(xb_free, g + 2)
                turn(LATER(g, 2, ahead), x3)

            first(0)
            loop(pe, body)


DI = 512
CH = DI // P
NS = 16
DTR = 16
TAPS = 4
HALF = 512
NH = S // HALF
BC3 = 3 * 2 * NS


def mixer(nc, xl_in, w_in_d, w_x_d, w_dt_d, cols_d, sel_d, ident_in, y_out):
    with ExitStack() as ctx:
        sb = lambda name, shape, dt=F32: ctx.enter_context(nc.sbuf_tensor(name, shape, dt))
        sem = lambda name: ctx.enter_context(nc.semaphore(name))
        ident = sb("c_ident", [P, P])
        w_i = sb("c_w_i", [P, DC, 2 * DI])
        w_x = sb("c_w_x", [P, CH, BC3 + DTR])
        w_dt = sb("c_w_dt", [BC3 + DTR, DI])
        cols = sb("c_cols", [P, CH, TAPS + 3 + NS])
        taps, conv_b, dt_b, d_p = (cols[:, :, 0:TAPS], cols[:, :, TAPS:TAPS + 1], cols[:, :, TAPS + 1:TAPS + 2],
                                   cols[:, :, TAPS + 2:TAPS + 3])
        a_neg = sb("c_a_neg", [P, CH, NS])
        sel = sb("c_sel", [BC3, 2 * NS, P], BF16)
        xl = sb("c_xl", [P, DC, S])
        xpad = sb("c_xpad", [P, CH, TAPS - 1 + S])
        sz = sb("c_sz", [P, CH, S])
        xc = sb("c_xc", [P, CH, S])
        conv = sb("c_conv", [P, CH, S])
        dt = sb("c_dt", [P, CH, S])
        bc = sb("c_bc", [BC3 + DTR, S])
        bc_mid = sb("c_bc_mid", [BC3, S], BF16)
        stack = sb("c_stack", [BC3, S], BF16)
        RING = 4
        NB = 2 * RING
        AHEAD = 3
        bs = [sb(f"c_bs{i}", [P, S]) for i in range(RING)]
        da = [sb(f"c_da{i}", [P, S]) for i in range(NB)]
        db = [sb(f"c_db{i}", [P, S]) for i in range(NB)]
        ps_y = ctx.enter_context(nc.psum_tensor("c_ps_y", [P, 2, S], F32))
        ps_b = ctx.enter_context(nc.psum_tensor("c_ps_b", [P, S], F32))
        ps_c = ctx.enter_context(nc.psum_tensor("c_ps_c", [P, S], F32))

        w_in, w_ok = sem("c_w_in"), sem("c_w_ok")
        xl_in_s = sem("c_xl_in")
        pi_ok, pi_free = sem("c_pi_ok"), sem("c_pi_free")
        conv_ok, xc_ok = sem("c_conv_ok"), sem("c_xc_ok")
        bc_ok, bc_step = sem("c_bc_ok"), sem("c_bc_step")
        sp_a, sp_v, dt_ok, dtx_ok = sem("c_sp_a"), sem("c_sp_v"), sem("c_dt_ok"), sem("c_dtx_ok")
        b_ok, c_ok, b_free = sem("c_b_ok"), sem("c_c_ok"), sem("c_b_free")
        bs_ok, da_ok, db_ok = sem("c_bs_ok"), sem("c_da_ok"), sem("c_db_ok")
        h_ok, hc_ok, acc_ok = sem("c_h_ok"), sem("c_hc_ok"), sem("c_acc_ok")
        y_step, y_ok, stored = sem("c_y_step"), sem("c_y_ok"), sem("c_stored")
        pool_own, dve_own, act_own, sp_own = (sem(f"c_{e}_own") for e in ("pool", "dve", "act", "sp"))
        block = ctx.enter_context(nc.Block())
        FRONT = 2 * 2 * CH + NH + CH * NH
        UNITS = CH * NS
        IN = 2 * CH * NH
        FB = 4

        def front_ps(i):
            bank = i % FB
            cut = slice((bank % NH) * HALF, (bank % NH + 1) * HALF)
            return (ps_b, ps_c)[bank // NH][:, cut] if i < IN else ps_y[:, bank // NH, cut]

        def n_of(b, pair, n):
            return (2 * b + pair) * NS + n

        @block.sync
        def _(sp):
            for dst, src in ((w_i[:], w_in_d.rearrange("(c p) n -> p c n", p=P)),
                             (w_x[:], w_x_d.rearrange("(c p) n -> p c n", p=P)),
                             (w_dt[BC3:BC3 + DTR, :], w_dt_d), (cols[:], cols_d.rearrange("(c p) n -> p c n", p=P)),
                             (sel[:], sel_d.rearrange("r (n p) -> r n p", p=P)), (ident[:], ident_in)):
                sp.dma_start(dst, src).then_inc(w_in, 16)
            sp.sem_inc(stored, 16 * CH + 16)

            def load(b):
                alone(sp, xl_in_s, 16 * b, sp_own)
                sp.dma_start(xl[:], xl_in[:, bass.ds(b * S, S)].rearrange("(c p) t -> p c t", p=P)).then_inc(xl_in_s, 16)

            def store(b):
                for m in range(CH):
                    alone(sp, stored, 16 * (CH * b + m + CH) + 16, sp_own)
                    alone(sp, y_ok, CH * b + m + 1, sp_own)
                    sp.dma_start(y_out[m * P:(m + 1) * P, bass.ds(b * S, S)], conv[:, m, :]).then_inc(stored, 16)

            load(0)
            with sp.Fori(0, B - 1) as b:
                alone(sp, pi_free, FRONT * b + IN + FB, sp_own)
                load(b + 1)
                store(b)
            store(B - 1)
            sp.wait_ge(stored, 16 * CH * (B + 1) + 16)

        @block.tensor
        def _(pe):
            pe.wait_ge(w_in, 16 * 6)

            def front(b):
                pe.wait_ge(xl_in_s, 16 * b + 16)
                n_out = 0

                def out(rows=P):
                    nonlocal n_out
                    pe.wait_ge(pi_free, FRONT * b + n_out + 1)
                    if n_out == 0:
                        pe.wait_ge(b_free, UNITS // 2 * b + 1)
                        pe.wait_ge(hc_ok, UNITS * b + 1)
                    if n_out == IN:
                        pe.wait_ge(y_step, 4 * b + 2)
                    n_out += 1
                    return front_ps(n_out - 1)[0:rows, :]

                for m in range(2 * CH):
                    for n in range(NH):
                        o = out()
                        for c in range(DC):
                            last = nc.tensor.matmul(o, w_i[:, c, m * P:(m + 1) * P], xl[:, c, n * HALF:(n + 1) * HALF],
                                                    start=(c == 0), stop=(c == DC - 1))
                        last.then_inc(pi_ok, 1)
                outs = [out(BC3 + DTR) for n in range(NH)]
                for c in range(CH):
                    pe.wait_ge(xc_ok, CH * b + c + 1)
                    for n in range(NH):
                        last = nc.tensor.matmul(outs[n], w_x[:, c, :], xc[:, c, n * HALF:(n + 1) * HALF],
                                                start=(c == 0), stop=(c == CH - 1))
                        if c == CH - 1:
                            last.then_inc(pi_ok, 1)
                pe.wait_ge(bc_ok, NH * b + NH)
                for m in range(CH):
                    for n in range(NH):
                        o = out()
                        nc.tensor.matmul(o, w_dt[BC3:BC3 + DTR, m * P:(m + 1) * P],
                                         bc[BC3:BC3 + DTR, n * HALF:(n + 1) * HALF],
                                         start=True, stop=True).then_inc(pi_ok, 1)
                    if m == 0:
                        pe.wait_ge(bc_step, 5 * b + 5)
                        pe.wait_ge(pi_free, FRONT * b + IN + FB)
                    if m < AHEAD:
                        b_cast(b, 0, m)
                c_cast(b, 0, 0)

            def b_cast(b, pair, n):
                N = n_of(b, pair, n)
                pe.wait_ge(b_free, N + 1)
                for half in range(NH):
                    last = nc.tensor.matmul(ps_b[:, half * HALF:(half + 1) * HALF],
                                            sel[:, bass.ds(n % NS, 1), :].rearrange("r a p -> r (a p)"),
                                            stack[:, half * HALF:(half + 1) * HALF], start=True, stop=True)
                last.then_inc(b_ok, 1)

            def c_cast(b, pair, n):
                N = n_of(b, pair, n)
                pe.wait_ge(hc_ok, 2 * N + 1)
                for half in range(NH):
                    last = nc.tensor.matmul(ps_c[:, half * HALF:(half + 1) * HALF],
                                            sel[:, bass.ds(NS + n % NS, 1), :].rearrange("r a p -> r (a p)"),
                                            stack[:, half * HALF:(half + 1) * HALF], start=True, stop=True)
                last.then_inc(c_ok, 1)

            def sums(b, pair, n, k, start, stop):
                N = n_of(b, pair, n)
                for c in range(2):
                    if start:
                        pe.wait_ge(y_step, 2 * (2 * b + pair) + c + 1)
                        pe.wait_ge(pi_free, FRONT * (b + 1) + FB)
                    pe.wait_ge(hc_ok, 2 * N + c + 1 + 1)
                    for half in range(NH):
                        cut = slice(half * HALF, (half + 1) * HALF)
                        last = nc.tensor.matmul(ps_y[:, c, cut], ident[:], da[2 * k + c][:, cut],
                                                start=start, stop=stop)
                    last.then_inc(acc_ok, 1)

            def state(b, pair, n, k, first=False, last=False):
                end = pair == CH // 2 - 1 and isinstance(n, int)
                if not (end and n + 1 >= NS):
                    c_cast(b, pair, n + 1)
                if not (end and n + AHEAD >= NS):
                    b_cast(b, pair, n + AHEAD)
                sums(b, pair, n, k, first, last)

            with pe.Fori(0, B) as b:
                front(b)
                for pair in range(CH // 2):
                    for k in range(RING):
                        state(b, pair, k, k, first=k == 0)
                    with pe.Fori(1, NS // RING - 1) as i:
                        for k in range(RING):
                            state(b, pair, RING * i + k, k)
                    for n in range(NS - RING, NS):
                        state(b, pair, n, n % RING, last=n == NS - 1)

        @block.gpsimd
        def _(pool):
            with pool.Fori(0, B) as b:
                for pair in range(CH // 2):
                    alone(pool, dtx_ok, CH * b + 2 * pair + 2, pool_own)
                    with pool.Fori(0, NS // RING) as i:
                        for k in range(RING):
                            N = n_of(b, pair, RING * i + k)
                            alone(pool, bs_ok, N + 1, pool_own)
                            for c in range(2):
                                alone(pool, h_ok, 2 * N + c + 1, pool_own)
                                nc.gpsimd.tensor_tensor(db[2 * k + c][:], conv[:, 2 * pair + c, :], bs[k][:],
                                                        ALU.mult).then_inc(db_ok, 1)

        @block.scalar
        def _(act):
            act.wait_ge(w_in, 16 * 6)
            nc.scalar.activation(a_neg[:], cols[:, :, TAPS + 3:], ACT.Exp).then_inc(w_ok, 1)
            act.sem_inc(b_free, 1)
            act.sem_inc(pi_free, FB)

            def b_copy(b, pair, n, k):
                N = n_of(b, pair, n)
                act.wait_ge(b_ok, N + 1)
                act.wait_ge(db_ok, 2 * N + 2)
                nc.scalar.copy(bs[k][:], ps_b[:]).then_inc(bs_ok, 1)
                act.wait_ge(bs_ok, N + 1)
                act.sem_inc(b_free, 1)

            def state(b, pair, n, k, copy=True):
                N = n_of(b, pair, n)
                if copy:
                    b_copy(b, pair, n + 1, (k + 1) % RING)
                for c in range(2):
                    m = 2 * pair + c
                    act.wait_ge(dt_ok, CH * b + m + 1)
                    alone(act, acc_ok, 2 * N + c + 1, act_own)
                    nc.scalar.activation(da[2 * k + c][:], dt[:, m, :], ACT.Exp,
                                         scale=a_neg[:, m, bass.ds(n, 1)]).then_inc(da_ok, 1)

            def front(b):
                def project(m):
                    for n in range(NH):
                        i = NH * m + n
                        act.wait_ge(pi_ok, FRONT * b + i + 1)
                        src = front_ps(i)
                        if m < CH:
                            nc.scalar.copy(xpad[:, m, TAPS - 1 + n * HALF:TAPS - 1 + (n + 1) * HALF], src
                                           ).then_inc(pi_free, 1)
                        else:
                            nc.scalar.activation(sz[:, m - CH, n * HALF:(n + 1) * HALF], src, ACT.Silu
                                                 ).then_inc(pi_free, 1)

                act.preload_act_table_set("silu_and_others")
                for m in range(CH):
                    project(m)
                for m in range(CH):
                    project(CH + m)
                    act.wait_ge(conv_ok, TAPS * (CH * b + 2 * (m // 2)) + 2 * (TAPS - 1) + m % 2 + 1)
                    nc.scalar.activation(xc[:, m, :], conv[:, m, :], ACT.Silu, bias=conv_b[:, m, :]).then_inc(xc_ok, 1)
                base = 2 * 2 * CH
                for n in range(NH):
                    act.wait_ge(pi_ok, FRONT * b + base + n + 1)
                    nc.scalar.copy(bc[:, n * HALF:(n + 1) * HALF], front_ps(base + n)[0:BC3 + DTR, :]
                                   ).then_inc(bc_ok, 1)
                    act.wait_ge(bc_ok, NH * b + n + 1)
                    act.sem_inc(pi_free, 1)
                base += NH
                act.preload_act_table_set("natural_log_exp_and_others")
                for m in range(CH):
                    for n in range(NH):
                        i = NH * m + n
                        cut = slice(n * HALF, (n + 1) * HALF)
                        act.wait_ge(pi_ok, FRONT * b + base + i + 1)
                        nc.scalar.activation(dt[:, m, cut], front_ps(base + i), ACT.Abs,
                                             bias=dt_b[:, m, :]).then_inc(sp_a, 1)
                    act.wait_ge(sp_a, NH * (CH * b + m + 1))
                    nc.scalar.activation(dt[:, m, :], dt[:, m, :], ACT.Exp, scale=-1.0).then_inc(sp_v, 1)
                    act.wait_ge(sp_v, 2 * (CH * b + m) + 1)
                    nc.scalar.activation(dt[:, m, :], dt[:, m, :], ACT.Ln, bias=1.0).then_inc(sp_v, 1)
                    if m < AHEAD:
                        b_copy(b, 0, m, m)

            with act.Fori(0, B) as b:
                front(b)
                for pair in range(CH // 2):
                    end = pair == CH // 2 - 1
                    for k in range(0 if pair else RING):
                        state(b, pair, k, k, copy=k >= AHEAD - 1)
                    with act.Fori(0 if pair else 1, NS // RING - end) as i:
                        for k in range(RING):
                            state(b, pair, RING * i + k, k)
                    for n in range(NS - RING if end else NS, NS):
                        state(b, pair, n, n % RING, copy=n + 1 < NS)

        @block.vector
        def _(dve):
            nc.vector.memset(xpad[:, :, 0:TAPS - 1], 0.0)
            dve.wait_ge(w_ok, 1)
            nc.vector.tensor_scalar(a_neg[:], a_neg[:], -1.0, None, ALU.mult).then_inc(w_ok, 1)
            dve.wait_ge(w_ok, 2)
            dve.sem_inc(h_ok, NB)
            dve.sem_inc(hc_ok, 1)
            dve.sem_inc(acc_ok, NB)
            dve.sem_inc(db_ok, 2 * RING)
            dve.sem_inc(y_step, 2)

            def front(b):
                for m0 in range(0, CH, 2):
                    dve.wait_ge(stored, 16 * (CH * b + m0 + 2) + 16)
                    for k in range(TAPS):
                        for m in (m0, m0 + 1):
                            src = xpad[:, m, k:k + S]
                            if k == 0:
                                dve.wait_ge(pi_free, FRONT * b + NH * (m + 1) + FB)
                                nc.vector.tensor_scalar(conv[:, m, :], src, taps[:, m, 0:1], None, ALU.mult
                                                        ).then_inc(conv_ok, 1)
                            else:
                                dve.wait_ge(conv_ok, TAPS * (CH * b + m0) + 2 * (k - 1) + m - m0 + 1)
                                nc.vector.scalar_tensor_tensor(conv[:, m, :], src, taps[:, m, k:k + 1], conv[:, m, :],
                                                               ALU.mult, ALU.add).then_inc(conv_ok, 1)
                dve.wait_ge(bc_ok, NH * b + NH)
                step = 5 * b
                nc.vector.tensor_copy(stack[:], bc[0:BC3, :]).then_inc(bc_step, 1)
                dve.wait_ge(bc_step, step + 1)
                nc.vector.tensor_tensor(bc[0:BC3, :], bc[0:BC3, :], stack[:], ALU.subtract).then_inc(bc_step, 1)
                dve.wait_ge(bc_step, step + 2)
                nc.vector.tensor_copy(bc_mid[:], bc[0:BC3, :]).then_inc(bc_step, 1)
                dve.wait_ge(bc_step, step + 3)
                r = 2 * NS
                nc.vector.tensor_copy(stack[r:2 * r, :], bc_mid[r:2 * r, :]).then_inc(bc_step, 1)
                nc.vector.tensor_tensor(stack[2 * r:3 * r, :], bc[2 * r:3 * r, :], bc_mid[2 * r:3 * r, :], ALU.subtract
                                        ).then_inc(bc_step, 1)
                base = 2 * 2 * CH + NH
                for m in range(CH):
                    for n in range(NH):
                        i = NH * m + n
                        cut = slice(n * HALF, (n + 1) * HALF)
                        dve.wait_ge(sp_a, CH * NH * b + i + 1)
                        nc.vector.tensor_scalar(conv[:, m, cut], front_ps(base + i), dt_b[:, m, :], 0.0,
                                                ALU.add, ALU.max).then_inc(pi_free, 1)
                    dve.wait_ge(sp_v, 2 * (CH * b + m + 1))
                    dve.wait_ge(pi_free, FRONT * b + base + NH * (m + 1) + FB)
                    nc.vector.tensor_tensor(dt[:, m, :], dt[:, m, :], conv[:, m, :], ALU.add).then_inc(dt_ok, 1)
                    dve.wait_ge(dt_ok, CH * b + m + 1)
                    nc.vector.tensor_tensor(conv[:, m, :], dt[:, m, :], xc[:, m, :], ALU.mult).then_inc(dtx_ok, 1)

            def scan(b, pair, n, k):
                N = n_of(b, pair, n)
                for c in range(2):
                    dve.wait_ge(db_ok, 2 * RING + 2 * N + c + 1)
                    dve.wait_ge(da_ok, 2 * N + c + 1)
                    q = 2 * k + c
                    nc.vector.tensor_tensor_scan(da[q][:], da[q][:], db[q][:], 0.0, ALU.mult, ALU.add).then_inc(h_ok, 1)

            def times_c(b, pair, n, k):
                N = n_of(b, pair, n)
                dve.wait_ge(c_ok, N + 1)
                for c in range(2):
                    q = 2 * k + c
                    dve.wait_ge(h_ok, NB + 2 * N + c + 1)
                    nc.vector.tensor_tensor(da[q][:], da[q][:], ps_c[:], ALU.mult).then_inc(hc_ok, 1)

            def gated(b, pair):
                for c in range(2):
                    m = 2 * pair + c
                    dve.wait_ge(acc_ok, NB + 2 * NS * (2 * b + pair + 1) - 1 + c)
                    nc.vector.scalar_tensor_tensor(conv[:, m, :], xc[:, m, :], d_p[:, m, :], ps_y[:, c, :],
                                                   ALU.mult, ALU.add).then_inc(y_step, 1)
                for c in range(2):
                    m = 2 * pair + c
                    dve.wait_ge(y_step, 2 * (2 * b + pair) + c + 3)
                    nc.vector.tensor_tensor(conv[:, m, :], conv[:, m, :], sz[:, m, :], ALU.mult).then_inc(y_ok, 1)

            def state(b, pair, n, k):
                scan(b, pair, n, k)
                times_c(b, pair, n, k)

            with dve.Fori(0, B) as b:
                front(b)
                for pair in range(CH // 2):
                    for k in range(RING):
                        state(b, pair, k, k)
                        if pair and k == 1:
                            gated(b, pair - 1)
                    with dve.Fori(1, NS // RING) as i:
                        for k in range(RING):
                            state(b, pair, RING * i + k, k)
                gated(b, CH // 2 - 1)


DF = 1024
DG = 768
MF, MG = DF // P, DG // P
INT_SCALE = 1.0 / 127.0


def tail(nc, ym_in, xc_in, x2_in, w_out_d, w_fc_d, w_pr_d, w_gu_d, w_dn_d, ln2_d, ident_in, out):
    with ExitStack() as ctx:
        sb = lambda name, shape, dt=F32: ctx.enter_context(nc.sbuf_tensor(name, shape, dt))
        sem = lambda name: ctx.enter_context(nc.semaphore(name))
        ident = sb("d_ident", [P, P])
        w_out = sb("d_w_out", [P, CH, D])
        w_fc = sb("d_w_fc", [P, DC, DF])
        w_pr = sb("d_w_pr", [P, MF, D])
        w_gi = sb("d_w_gi", [P, DC, 2 * DG], I32)
        w_di = sb("d_w_di", [P, MG, D], I32)
        w_gu = sb("d_w_gu", [P, DC, 2 * DG])
        w_dn = sb("d_w_dn", [P, MG, D])
        ln_w = sb("d_ln_w", [P, DC])
        mhalf = sb("d_mhalf", [P, G])
        ym = [sb(f"d_ym{i}", [P, CH, GT]) for i in range(2)]
        xc = [sb(f"d_xc{i}", [P, G, D]) for i in range(2)]
        x2 = [sb(f"d_x2{i}", [P, G, D]) for i in range(2)]
        y1 = sb("d_y1", [P, G, D])
        x3 = sb("d_x3", [P, G, D])
        stats = sb("d_stats", [P, G, 6])
        mv = sb("d_mv", [P, G, 2])
        ve = sb("d_ve", [P, G])
        rstd = sb("d_rstd", [P, G])
        xn = [sb(f"d_xn{i}", [P, G, D]) for i in range(2)]
        nT = sb("d_nT", [P, DC, G, P])
        hT = sb("d_hT", [P, MF, GT])
        sg = [sb(f"d_sg{i}", [P, GT]) for i in range(2)]
        o = sb("d_o", [P, G, D])
        ps_t = [ctx.enter_context(nc.psum_tensor(f"d_ps_t{i}", [P, 2, DC, P], F32)) for i in range(2)]
        ps_y = [ctx.enter_context(nc.psum_tensor(f"d_ps_y{i}", [P, 2, D], F32)) for i in range(2)]
        ps_a = [ctx.enter_context(nc.psum_tensor(f"d_ps_a{i}", [P, GT], F32)) for i in range(2)]
        ps_u = [ctx.enter_context(nc.psum_tensor(f"d_ps_u{i}", [P, GT], F32)) for i in range(2)]
        w_in, w_rest, w_ok, in_s, in_free = sem("d_w_in"), sem("d_w_rest"), sem("d_w_ok"), sem("d_in"), sem("d_in_free")
        y_ok, y_free = sem("d_y_ok"), sem("d_y_free")
        t_ok, t_free = sem("d_t_ok"), sem("d_t_free")
        a_ok, a_free, u_ok, h_ok = sem("d_a_ok"), sem("d_a_free"), sem("d_u_ok"), sem("d_h_ok")
        step, r_ok, n_ok, s_ok, stored = sem("d_step"), sem("d_r_ok"), sem("d_n_ok"), sem("d_s_ok"), sem("d_stored")
        pool_own, dve_own, sp_own = (sem(f"d_{e}_own") for e in ("pool", "dve", "sp"))
        block = ctx.enter_context(nc.Block())
        NA = MF + MG

        def loop(eng, body):
            with eng.Fori(0, GROUPS // 2 - 1) as i:
                for k in range(2):
                    body(2 * i + k, k, 2)
            for k in range(2):
                body(GROUPS - 2 + k, k, 1 - k)

        FIRST = lambda g: 3 * g - 1 if not isinstance(g, int) or g else 0
        SECOND = lambda g: 3 * g + 1
        THIRD = lambda g, ahead: 3 * g + (3 if ahead else 2)

        def rows(x, g):
            return x[bass.ds(g * GT, GT), :].rearrange("(i p) d -> p i d", p=P)

        @block.sync
        def _(sp):
            for dst, src in ((w_out[:], w_out_d.rearrange("(c p) n -> p c n", p=P)), (ident[:], ident_in),
                             (ln_w[:], ln2_d)):
                sp.dma_start(dst, src).then_inc(w_in, 16)

            def load(g, k):
                sp.dma_start(ym[k][:], ym_in[:, bass.ds(g * GT, GT)].rearrange("(c p) t -> p c t", p=P)).then_inc(in_s, 16)
                sp.dma_start(xc[k][:], rows(xc_in, g)).then_inc(in_s, 16)
                sp.dma_start(x2[k][:], rows(x2_in, g)).then_inc(in_s, 16)

            def body(g, k, ahead):
                if ahead == 2:
                    alone(sp, in_s, 48 * g + 96, sp_own)
                    alone(sp, in_free, g + 1, sp_own)
                    load(g + 2, k)
                alone(sp, y_free, 2 * THIRD(g, ahead) + 2 + 2, sp_own)
                sp.dma_start(rows(out, g), o[:]).then_inc(stored, 16)

            load(0, 0)
            for dst, src in ((w_fc[:], w_fc_d.rearrange("(c p) n -> p c n", p=P)),
                             (w_gi[:], w_gu_d.rearrange("(c p) n -> p c n", p=P)),
                             (w_pr[:], w_pr_d.rearrange("(c p) n -> p c n", p=P)),
                             (w_di[:], w_dn_d.rearrange("(c p) n -> p c n", p=P))):
                sp.dma_start(dst, src).then_inc(w_rest, 16)
            alone(sp, in_s, 48, sp_own)
            load(1, 1)
            sp.sem_inc(stored, 16)
            loop(sp, body)
            sp.wait_ge(stored, 16 * GROUPS + 16)

        @block.gpsimd
        def _(pool):
            nc.gpsimd.memset(mhalf[:], -0.5).then_inc(pool_own, 1)
            pool.wait_ge(pool_own, 1)

            def first(g, k):
                alone(pool, step, 6 * g + 3, pool_own)
                nc.gpsimd.tensor_tensor(rstd[:], ve[:], mhalf[:], ALU.pow).then_inc(r_ok, 1)
                alone(pool, n_ok, 2 * g + 1, pool_own)
                nc.gpsimd.tensor_tensor(y1[:], y1[:], x2[k][:], ALU.add).then_inc(s_ok, 1)

            def body(g, k, ahead):
                alone(pool, step, 6 * g + 6, pool_own)
                nc.gpsimd.tensor_tensor(rstd[:], ve[:], mhalf[:], ALU.pow).then_inc(r_ok, 1)
                if ahead:
                    first(g + 1, 1 - k)

            first(0, 0)
            loop(pool, body)

        @block.vector
        def _(dve):
            dve.sem_inc(y_free, 2)
            dve.sem_inc(h_ok, 2)
            def first(g, k):
                dve.wait_ge(in_s, 48 * g + 48)
                for j in range(2):
                    dve.wait_ge(y_ok, 2 * FIRST(g) + j + 1)
                    nc.vector.tensor_tensor(y1[:, 2 * j:2 * j + 2, :], ps_y[j][:], xc[k][:, 2 * j:2 * j + 2, :],
                                            ALU.add).then_inc(y_free, 1)
                dve.wait_ge(y_free, 2 * FIRST(g) + 2 + 2)
                norm_stats(nc, dve, y1, stats, mv, ve, step, 6 * g, dve_own)
                dve.wait_ge(r_ok, 2 * g + 1)
                norm_apply(nc, dve, xn[0], y1, mv, rstd).then_inc(n_ok, 1)

            def body(g, k, ahead):
                dve.wait_ge(s_ok, g + 1)
                dve.sem_inc(in_free, 1)
                for j in range(2):
                    dve.wait_ge(y_ok, 2 * SECOND(g) + j + 1)
                    nc.vector.tensor_tensor(x3[:, 2 * j:2 * j + 2, :], ps_y[j][:], y1[:, 2 * j:2 * j + 2, :],
                                            ALU.add).then_inc(y_free, 1)
                dve.wait_ge(y_free, 2 * SECOND(g) + 2 + 2)
                norm_stats(nc, dve, x3, stats, mv, ve, step, 6 * g + 3, dve_own)
                dve.wait_ge(r_ok, 2 * g + 2)
                norm_apply(nc, dve, xn[1], x3, mv, rstd).then_inc(n_ok, 1)
                if ahead:
                    first(g + 1, 1 - k)
                for m in range(MG):
                    dve.wait_ge(a_free, NA * g + MF + m + 1 + 2)
                    dve.wait_ge(u_ok, MG * g + m + 1)
                    nc.vector.tensor_tensor(hT[:, m, :], ps_u[m % 2][:], sg[m % 2][:], ALU.mult).then_inc(h_ok, 1)
                dve.wait_ge(stored, 16 * g + 16)
                for j in range(2):
                    dve.wait_ge(y_ok, 2 * THIRD(g, ahead) + j + 1)
                    nc.vector.tensor_tensor(o[:, 2 * j:2 * j + 2, :], ps_y[j][:], x3[:, 2 * j:2 * j + 2, :],
                                            ALU.add).then_inc(y_free, 1)

            first(0, 0)
            dve.wait_ge(w_rest, 16 * 4)
            nc.vector.tensor_scalar(w_gu[:], w_gi[:], INT_SCALE, None, ALU.mult)
            nc.vector.tensor_scalar(w_dn[:], w_di[:], INT_SCALE, None, ALU.mult).then_inc(w_ok, 1)
            loop(dve, body)

        @block.scalar
        def _(act):
            act.wait_ge(w_in, 16 * 3)
            act.preload_act_table_set("silu_and_others")
            act.sem_inc(t_free, 2)
            act.sem_inc(a_free, 2)

            def turned(g, n):
                for j in range(2):
                    act.wait_ge(t_ok, 4 * g + 2 * n + j + 1)
                    for c in range(DC):
                        scale = ln_w[:, c:c + 1] if n == 0 else 1.0
                        last = nc.scalar.activation(nT[:, c, 2 * j:2 * j + 2, :], ps_t[j][:, :, c, :], ACT.Copy,
                                                    scale=scale)
                    last.then_inc(t_free, 1)

            def body(g, k, ahead):
                for m in range(MF):
                    act.wait_ge(a_ok, NA * g + m + 1)
                    nc.scalar.activation(hT[:, m, :], ps_a[m % 2][:], ACT.Silu).then_inc(a_free, 1)
                turned(g, 1)
                for m in range(MG):
                    act.wait_ge(a_ok, NA * g + MF + m + 1)
                    act.wait_ge(h_ok, MG * g + m + 1)
                    nc.scalar.activation(sg[m % 2][:], ps_a[m % 2][:], ACT.Silu).then_inc(a_free, 1)
                if ahead:
                    turned(g + 1, 0)

            turned(0, 0)
            loop(act, body)

        @block.tensor
        def _(pe):
            pe.wait_ge(w_in, 16 * 3)

            def turn(g, n):
                pe.wait_ge(n_ok, 2 * g + n + 1)
                for j in range(2):
                    pe.wait_ge(t_free, 4 * g + 2 * n + j + 1)
                    for i in range(2):
                        for c in range(DC):
                            last = nc.tensor.transpose(ps_t[j][:, i, c, :], xn[n][:, 2 * j + i, c * P:(c + 1) * P], ident[:])
                    last.then_inc(t_ok, 1)

            def rows_out(use, lhs, w, count):
                for j in range(2):
                    pe.wait_ge(y_free, 2 * use + j + 1)
                    for i in range(2):
                        for c in range(count):
                            at = (2 * j + i) * P
                            last = nc.tensor.matmul(ps_y[j][:, i, :], lhs[:, c, at:at + P], w[:, c, :],
                                                    start=(c == 0), stop=(c == count - 1))
                    last.then_inc(y_ok, 1)

            def hidden(dst, w, at):
                for c in range(DC):
                    last = nc.tensor.matmul(dst[:], w[:, c, at:at + P], nT[:, c].rearrange("p i t -> p (i t)"),
                                            start=(c == 0), stop=(c == DC - 1))
                return last

            def first(g, k):
                pe.wait_ge(in_s, 48 * g + 48)
                rows_out(FIRST(g), ym[k], w_out, CH)

            def body(g, k, ahead):
                pe.wait_ge(t_free, 4 * g + 2 + 2)
                for m in range(MF):
                    pe.wait_ge(a_free, NA * g + m + 1)
                    hidden(ps_a[m % 2], w_fc, m * P).then_inc(a_ok, 1)
                pe.wait_ge(a_free, NA * g + MF + 2)
                rows_out(SECOND(g), hT, w_pr, MF)
                if ahead:
                    first(g + 1, 1 - k)
                turn(g, 1)
                pe.wait_ge(t_free, 4 * g + 4 + 2)
                for m in range(MG):
                    pe.wait_ge(a_free, NA * g + MF + m + 1)
                    hidden(ps_a[m % 2], w_gu, m * P).then_inc(a_ok, 1)
                    pe.wait_ge(h_ok, MG * g + m + 1)
                    hidden(ps_u[m % 2], w_gu, DG + m * P).then_inc(u_ok, 1)
                if ahead:
                    turn(g + 1, 0)
                pe.wait_ge(h_ok, MG * g + MG + 2)
                rows_out(THIRD(g, ahead), hT, w_dn, MG)

            first(0, 0)
            turn(0, 0)
            pe.wait_ge(w_rest, 16 * 4)
            pe.wait_ge(w_ok, 1)
            loop(pe, body)


def kernel(**inputs):
    import ml_dtypes
    import numpy as np
    import concourse.bacc as bacc
    from concourse.bass_utils import run_bass_kernel_spmd as run

    f = {k: np.asarray(v) for k, v in inputs.items()}
    a = {k[8:]: v for k, v in f.items() if k.startswith("L0_attn_")}
    m = {k[8:]: v for k, v in f.items() if k.startswith("L1_attn_")}
    x_proj = m["x_proj_w"].T
    sel = np.zeros((BC3, 2 * NS, P), dtype=ml_dtypes.bfloat16)
    for n in range(2 * NS):
        sel[n::2 * NS, n] = 1
    arrays = {
        "x": a["hidden_states"].reshape(B * S, D),
        "w_qk": np.concatenate([a["Wq"].T, a["Wk"].T], axis=1),
        "w_vg": np.concatenate([a["Wv"].T, a["gate_W"].T, a["rel_W"][:, :D].T, a["rel_W"][:, D:].T, a["Wo"].T], axis=1),
        "b_qk": np.concatenate([a["bq"], a["bk"]]).reshape(4, P).T,
        "rows": np.concatenate([a["bv"], a["bo"], a["gate_b"], a["rel_b"], a["logical_bias"].T.reshape(-1)]),
        "w_fp8": f["L0_ffn_weight_fp8"].T,
        "scales": np.concatenate([f["L0_ffn_input_scale"], f["L0_ffn_weight_scale"]]),
        "b_fp8": f["L0_ffn_bias"],
        "ln1_w": m["ln1_w"].reshape(DC, P).T,
        "w_in": m["in_proj_w"].T,
        "w_x": np.concatenate([x_proj[:, DTR:]] * 3 + [x_proj[:, :DTR]], axis=1),
        "w_dt": m["dt_proj_w"].T,
        "cols": np.concatenate([m["conv_w"][:, 0], m["conv_b"][:, None], m["dt_proj_b"][:, None], m["Dp"][:, None],
                                m["A_log"]], axis=1),
        "sel": sel.reshape(BC3, -1),
        "w_out": m["out_proj_w"].T,
        "w_fc": m["fc_w"].T,
        "w_pr": m["proj_w"].T,
        "ln2_w": m["ln2_w"].reshape(DC, P).T,
        "w_gu": np.concatenate([f["L1_ffn_w_gate"].T, f["L1_ffn_w_up"].T], axis=1),
        "w_dn": f["L1_ffn_w_down"].T,
        "ident": np.eye(P, dtype=np.float32),
    }
    arrays = {"in_" + k: np.ascontiguousarray(v) for k, v in arrays.items()}
    nc = bacc.Bacc("TRN2", target_bir_lowering=False, num_devices=1)
    d = {k[3:]: nc.dram_tensor(k, v.shape, mybir.dt.from_np(v.dtype), kind="ExternalInput").ap()
         for k, v in arrays.items()}
    out = nc.dram_tensor("out", (B * S, D), F32, kind="ExternalOutput").ap()
    scratch = lambda name, shape, dt=F32: nc.dram_tensor(name + "_d", shape, dt, kind="Internal").ap()
    parts = scratch("parts", (3, 2 * D, B * S), BF16)
    x1, x2, xc = (scratch(n, (B * S, D)) for n in ("x1", "x2", "xc"))
    xl = scratch("xl", (D, B * S))
    ym = scratch("ym", (DI, B * S))
    attention(nc, d["x"], d["w_qk"], d["w_vg"], d["b_qk"], d["rows"], d["ident"], parts, x1)
    fp8_layer(nc, x1, d["w_fp8"], d["scales"], d["ln1_w"], d["b_fp8"], d["ident"], x2, xc, xl)
    mixer(nc, xl, d["w_in"], d["w_x"], d["w_dt"], d["cols"], d["sel"], d["ident"], ym)
    tail(nc, ym, xc, x2, d["w_out"], d["w_fc"], d["w_pr"], d["w_gu"], d["w_dn"], d["ln2_w"], d["ident"], out)
    r = run(nc, [arrays], core_ids=[0])
    return r.results[0]["out"].reshape(B, S, D)
```
